# Optimizing a Trainium2 kernel written in Bass

```python
import numpy as np
import jax
import jax.numpy as jnp

def _softmax(x, axis=-1):
    return jax.nn.softmax(x, axis=axis)
def _gelu(x):
    return jax.nn.gelu(x, approximate=True)
def _silu(x):
    return jax.nn.silu(x)
def _sigmoid(x):
    return jax.nn.sigmoid(x)
def _layernorm(x, axis=-1, eps=1e-5):
    m = jnp.mean(x, axis=axis, keepdims=True)
    v = jnp.var(x, axis=axis, keepdims=True)
    return (x - m) / jnp.sqrt(v + eps)
def _scatter_add(tgt, idx, src, axis=0):
    return tgt.at[idx].add(src)
def _segment_sum(src, seg, n):
    return jax.ops.segment_sum(src, seg, n)

kernel_name = 'mk_audio_tower_d1_tok_aud1d512_125261'

def setup_inputs(seed: int = 0):
    np.random.seed(seed)
    _w = jnp.asarray
    def _rec_inputs():
        import jax
        import jax.numpy as jnp
        _rk = jax.random.key(seed)
        x = (0.000214012 + 1.00007 * jax.random.normal(jax.random.fold_in(_rk, 1), (256, 16000), jnp.float32))
        return x
    x = _rec_inputs()
    def _L0_tok_setup():
        import jax, jax.numpy as jnp
        import numpy as np
        HOP = 512

        def _dct_ortho_basis(n):
            k = np.arange(n)[:, None].astype(np.float64)
            t = np.arange(n)[None, :].astype(np.float64)
            D = np.cos(np.pi * (2.0 * t + 1.0) * k / (2.0 * n))
            scale = np.full((n, 1), np.sqrt(2.0 / n))
            scale[0, 0] = np.sqrt(1.0 / n)
            return jnp.asarray((scale * D).astype(np.float32))
        key = jax.random.key(seed)
        x = jax.random.normal(key, (32, 1048000), dtype=jnp.float32)
        return {'x': x}
    _L0_tok_all = _L0_tok_setup()
    _L0_tok_in = {k: v for k, v in _L0_tok_all.items() if k in ()}
    del _L0_tok_all

    def _L0_attn_setup():
        import jax, jax.numpy as jnp
        import numpy as np
        B, L, C = (2, 1024, 512)
        H, P = (8, 4)
        D = C // H
        LN_EPS = 1e-05

        def _layernorm(x, g, b):
            mu = jnp.mean(x, axis=-1, keepdims=True)
            var = jnp.mean((x - mu) ** 2, axis=-1, keepdims=True)
            return (x - mu) * jax.lax.rsqrt(var + LN_EPS) * g + b
        key = jax.random.key(seed)
        ks = jax.random.split(key, 12)
        s = 0.02
        inp = {'features': jax.random.normal(ks[0], (B, L, C), jnp.float32), 'coords': jax.random.normal(ks[1], (B, L, 3), jnp.float32), 'ln_g': jnp.ones((C,), jnp.float32), 'ln_b': jnp.zeros((C,), jnp.float32), 'wq': jax.random.normal(ks[2], (C, C), jnp.float32) * s, 'bq': jnp.zeros((C,), jnp.float32), 'wk': jax.random.normal(ks[3], (C, C), jnp.float32) * s, 'bk': jnp.zeros((C,), jnp.float32), 'wv': jax.random.normal(ks[4], (C, C), jnp.float32) * s, 'bv': jnp.zeros((C,), jnp.float32), 'wqp': jax.random.normal(ks[5], (C, H * P * 3), jnp.float32) * s, 'bqp': jnp.zeros((H * P * 3,), jnp.float32), 'wkp': jax.random.normal(ks[6], (C, H * P * 3), jnp.float32) * s, 'bkp': jnp.zeros((H * P * 3,), jnp.float32), 'wvp': jax.random.normal(ks[7], (C, H * P * 3), jnp.float32) * s, 'bvp': jnp.zeros((H * P * 3,), jnp.float32), 'wo': jax.random.normal(ks[8], (C, C), jnp.float32) * s, 'bo': jnp.zeros((C,), jnp.float32), 'pscale': jnp.full((H,), 1.0 / np.sqrt(P), jnp.float32)}
        return inp
    _L0_attn_all = _L0_attn_setup()
    _L0_attn_in = {k: v for k, v in _L0_attn_all.items() if k in ('coords', 'ln_g', 'ln_b', 'wq', 'bq', 'wk', 'bk', 'wv', 'bv', 'wqp', 'bqp', 'wkp', 'bkp', 'wvp', 'bvp', 'wo', 'bo', 'pscale', )}
    del _L0_attn_all

    def _L0_ffn_setup():
        import jax, jax.numpy as jnp
        import numpy as np
        BINS = jnp.array([-1.5, -1.0, -0.5, 0.0, 0.5, 1.0, 1.5], dtype=jnp.float32)
        N_BINS = BINS.shape[0] + 1
        INDEX = 0
        key = jax.random.key(seed)
        k1, k2 = jax.random.split(key)
        x = jax.random.normal(k1, (8, 4096, 512), dtype=jnp.float32)
        W = jax.random.normal(k2, (N_BINS, 512, 512), dtype=jnp.float32) * 0.02
        return {'x': x, 'W': W}
    _L0_ffn_all = _L0_ffn_setup()
    _L0_ffn_in = {k: v for k, v in _L0_ffn_all.items() if k in ('W', )}
    del _L0_ffn_all

    return {
        "x": x,
        "L0_attn_coords": _L0_attn_in["coords"],
        "L0_attn_ln_g": _L0_attn_in["ln_g"],
        "L0_attn_ln_b": _L0_attn_in["ln_b"],
        "L0_attn_wq": _L0_attn_in["wq"],
        "L0_attn_bq": _L0_attn_in["bq"],
        "L0_attn_wk": _L0_attn_in["wk"],
        "L0_attn_bk": _L0_attn_in["bk"],
        "L0_attn_wv": _L0_attn_in["wv"],
        "L0_attn_bv": _L0_attn_in["bv"],
        "L0_attn_wqp": _L0_attn_in["wqp"],
        "L0_attn_bqp": _L0_attn_in["bqp"],
        "L0_attn_wkp": _L0_attn_in["wkp"],
        "L0_attn_bkp": _L0_attn_in["bkp"],
        "L0_attn_wvp": _L0_attn_in["wvp"],
        "L0_attn_bvp": _L0_attn_in["bvp"],
        "L0_attn_wo": _L0_attn_in["wo"],
        "L0_attn_bo": _L0_attn_in["bo"],
        "L0_attn_pscale": _L0_attn_in["pscale"],
        "L0_ffn_W": _L0_ffn_in["W"],
    }

def reference(x, L0_attn_coords, L0_attn_ln_g, L0_attn_ln_b, L0_attn_wq, L0_attn_bq, L0_attn_wk, L0_attn_bk, L0_attn_wv, L0_attn_bv, L0_attn_wqp, L0_attn_bqp, L0_attn_wkp, L0_attn_bkp, L0_attn_wvp, L0_attn_bvp, L0_attn_wo, L0_attn_bo, L0_attn_pscale, L0_ffn_W):
    import jax
    import jax.numpy as jnp
    def _L0_tok_ref(x):
        import jax, jax.numpy as jnp
        import numpy as np
        HOP = 512

        def _dct_ortho_basis(n):
            k = np.arange(n)[:, None].astype(np.float64)
            t = np.arange(n)[None, :].astype(np.float64)
            D = np.cos(np.pi * (2.0 * t + 1.0) * k / (2.0 * n))
            scale = np.full((n, 1), np.sqrt(2.0 / n))
            scale[0, 0] = np.sqrt(1.0 / n)
            return jnp.asarray((scale * D).astype(np.float32))
        x_len = x.shape[-1]
        pad_len = HOP - x_len % HOP
        x = jnp.pad(x, [(0, 0)] * (x.ndim - 1) + [(0, pad_len)])
        n_frames = x.shape[-1] // HOP
        frames = x.reshape(x.shape[:-1] + (n_frames, HOP))
        D = _dct_ortho_basis(HOP)
        return jnp.einsum('bfh,kh->bfk', frames, D)

    def _L0_attn_ref(features, coords, ln_g, ln_b, wq, bq, wk, bk, wv, bv, wqp, bqp, wkp, bkp, wvp, bvp, wo, bo, pscale):
        import jax, jax.numpy as jnp
        import numpy as np
        B, L, C = (2, 1024, 512)
        H, P = (8, 4)
        D = C // H
        LN_EPS = 1e-05

        def _layernorm(x, g, b):
            mu = jnp.mean(x, axis=-1, keepdims=True)
            var = jnp.mean((x - mu) ** 2, axis=-1, keepdims=True)
            return (x - mu) * jax.lax.rsqrt(var + LN_EPS) * g + b
        b, l, c = features.shape
        h = pscale.shape[0]
        d = c // h
        p = wqp.shape[1] // (h * 3)
        x = _layernorm(features, ln_g, ln_b)
        q_s = (x @ wq + bq).reshape(b, l, h, d).transpose(0, 2, 1, 3)
        k_s = (x @ wk + bk).reshape(b, l, h, d).transpose(0, 2, 1, 3)
        v_s = (x @ wv + bv).reshape(b, l, h, d).transpose(0, 2, 1, 3)
        q_p = (x @ wqp + bqp).reshape(b, l, h, p, 3).transpose(0, 2, 1, 3, 4)
        k_p = (x @ wkp + bkp).reshape(b, l, h, p, 3).transpose(0, 2, 1, 3, 4)
        logits_s = jnp.einsum('bhid,bhjd->bhij', q_s, k_s) * d ** (-0.5)
        dot = jnp.einsum('bhipk,bhjpk->bhij', q_p, k_p)
        qsq = jnp.sum(q_p * q_p, axis=(-1, -2))
        ksq = jnp.sum(k_p * k_p, axis=(-1, -2))
        pdist2 = qsq[..., :, None] + ksq[..., None, :] - 2.0 * dot
        logits = logits_s - pdist2 * pscale[None, :, None, None]
        attn = jax.nn.softmax(logits, axis=-1)
        out_s = jnp.einsum('bhij,bhjd->bhid', attn, v_s)
        out_s = out_s.transpose(0, 2, 1, 3).reshape(b, l, c)
        out = out_s @ wo + bo
        return out

    def _L0_ffn_ref(x, W):
        import jax, jax.numpy as jnp
        import numpy as np
        BINS = jnp.array([-1.5, -1.0, -0.5, 0.0, 0.5, 1.0, 1.5], dtype=jnp.float32)
        N_BINS = BINS.shape[0] + 1
        INDEX = 0
        y = x[..., INDEX]
        mem = jnp.sum(y[..., None] > BINS, axis=-1)
        B, T, D = x.shape
        xf = x.reshape(B * T, D)
        memf = mem.reshape(B * T)
        out = jnp.zeros((B * T, W.shape[-1]), dtype=x.dtype)
        for k in range(N_BINS):
            sel = (memf == k)[:, None].astype(x.dtype)
            out = out + sel * (xf @ W[k])
        return out.reshape(B, T, W.shape[-1])

    h = _L0_tok_ref(x)
    h = h + _L0_attn_ref(_layernorm(h, axis=-1), L0_attn_coords, L0_attn_ln_g, L0_attn_ln_b, L0_attn_wq, L0_attn_bq, L0_attn_wk, L0_attn_bk, L0_attn_wv, L0_attn_bv, L0_attn_wqp, L0_attn_bqp, L0_attn_wkp, L0_attn_bkp, L0_attn_wvp, L0_attn_bvp, L0_attn_wo, L0_attn_bo, L0_attn_pscale)
    h = h + _L0_ffn_ref(_layernorm(h, axis=-1), L0_ffn_W)
    return h


_drawn_inputs = setup_inputs


def setup_inputs(seed=0):
    import zlib

    import numpy as np

    out = dict(_drawn_inputs(seed))
    spreads = {'L0_attn_ln_g': (1.0, 0.2),
     'L0_attn_ln_b': (0.0, 0.1),
     'L0_attn_bq': (0.0, 0.1),
     'L0_attn_bk': (0.0, 0.1),
     'L0_attn_bv': (0.0, 0.1),
     'L0_attn_bqp': (0.0, 0.1),
     'L0_attn_bkp': (0.0, 0.1),
     'L0_attn_bvp': (0.0, 0.1),
     'L0_attn_bo': (0.0, 0.1),
     'L0_attn_pscale': (0.5, 0.2)}
    factors = {}
    for name, (base, spread) in spreads.items():
        noise = np.random.default_rng([zlib.crc32(name.encode()), seed]).standard_normal(out[name].shape)
        drawn = base * np.exp(spread * noise) if base else spread * noise
        out[name] = jnp.asarray(drawn.astype(out[name].dtype))
    for name, factor in factors.items():
        out[name] = (out[name] * factor).astype(out[name].dtype)
    return out
```

```python
import numpy as np
from contextlib import ExitStack

import concourse.bass as bass
from concourse import mybir


BATCH, SAMPLES, HOP = 256, 16000, 512
FRAMES = (SAMPLES + HOP - SAMPLES % HOP) // HOP
TAIL = SAMPLES - (FRAMES - 1) * HOP
ROWS = BATCH * FRAMES
C = HOP
HEADS, POINT = 8, 12
HD = C // HEADS
BINS = (-1.5, -1.0, -0.5, 0.0, 0.5, 1.0, 1.5)
EXPERTS = len(BINS) + 1
EPS = 1e-5
P = 128
CC = C // P
CLIPS = P // FRAMES
T = 4
BLOCK = T * P
NBLOCK = ROWS // BLOCK
NTILE = ROWS // P
HALF = HOP // 2
DOT, QSQ, KSQ = 64, 96, 108
FEAT = 120
BUCKET = ROWS
FTILE = NTILE + EXPERTS
TABLE = EXPERTS * BUCKET + P * P // 2
TABLE_ROWS = TABLE // P


def constants():
    k = np.arange(HOP)[:, None].astype(np.float64)
    n = np.arange(HOP)[None, :].astype(np.float64)
    basis = np.cos(np.pi * (2.0 * n + 1.0) * k / (2.0 * HOP))
    scale = np.full((HOP, 1), np.sqrt(2.0 / HOP))
    scale[0, 0] = np.sqrt(1.0 / HOP)
    basis = (scale * basis).astype(np.float32)
    dct = np.stack([basis[0::2, :HALF].T, basis[1::2, :HALF].T], axis=1)
    dct = dct.reshape(HALF // P, P, 2, HALF).transpose(1, 2, 0, 3)
    f = np.arange(P)
    cols = {}
    cols["ident"] = np.eye(P)
    cols["before"] = (f[:, None] < f[None, :]).astype(float)
    own_q = np.where(f < DOT, HD ** -0.5, np.where(f >= QSQ, 1.0, 0.0))
    per_q = np.where((f >= DOT) & (f < DOT + POINT), 2.0, 0.0)
    one_q = ((f >= KSQ) & (f < KSQ + POINT)).astype(float)
    one_k = ((f >= QSQ) & (f < QSQ + POINT)).astype(float)
    cols["own"] = np.stack([own_q] * HEADS + [np.ones(P)] * HEADS, axis=1)
    cols["per"] = np.stack([per_q] * HEADS + [np.zeros(P)] * HEADS, axis=1)
    cols["one"] = np.stack([one_q] * HEADS + [one_k] * HEADS, axis=1)
    cols["bins"] = np.tile(np.array(BINS), (P, 1))
    cols["bucket"] = np.tile(np.arange(EXPERTS) * BUCKET, (P, 1))
    cols["tile128"] = np.tile(np.arange(NTILE) * P, (P, 1))
    cols["partition"] = f[:, None]
    cols["lower"] = np.tile(np.tril(np.ones((EXPERTS, EXPERTS)), -1).reshape(-1), (P, 1))
    cols["rows"] = f[:, None] + P * np.arange(T)[None, :]
    at, place = 0, {}
    for name, a in cols.items():
        place[name] = (at, at + a.shape[1])
        at += a.shape[1]
    small = np.concatenate(list(cols.values()), axis=1).astype(np.float32)
    return np.ascontiguousarray(dct), np.ascontiguousarray(small), place


def audio_tower(nc, x, ln_g, ln_b, wq, bq, wk, bk, wv, bv, wqp, bqp, wkp, bkp, wo, bo, pscale, w_ffn,
                dct_in, small_in, place, out):
    f32, f32r, bf16, u32, i32 = (mybir.dt.float32, mybir.dt.float32r, mybir.dt.bfloat16,
                                 mybir.dt.uint32, mybir.dt.int32)
    ALU, ACT, AX = mybir.AluOpType, mybir.ActivationFunctionType, mybir.AxisListType
    XA = AX.X

    x_flat = x.rearrange("b n -> (b n)")
    out_rows = out.rearrange("b f c -> (b f) c")
    h1_dram = nc.dram_tensor("h1_rows", (ROWS + 1, C), f32, kind="Internal").ap()
    table = nc.dram_tensor("row_table", (TABLE, 1), f32, kind="Internal").ap()

    ctx = ExitStack()
    with ctx:
        def sb(name, shape, dt, where=ctx):
            return where.enter_context(nc.sbuf_tensor(name, shape, dt))

        def sem(name):
            return ctx.enter_context(nc.semaphore(name))

        tr = [ctx.enter_context(nc.psum_tensor(f"transposed{k}", [P, 512], f32)) for k in range(2)]
        ro = [ctx.enter_context(nc.psum_tensor(f"row_out{k}", [P, 512], f32)) for k in range(2)]
        qk = [ctx.enter_context(nc.psum_tensor(f"qk_out{k}", [P, 512], f32)) for k in range(2)]
        sc = [ctx.enter_context(nc.psum_tensor(f"scores{k}", [P, 2, HEADS, FRAMES], f32))
              for k in range(2)]

        small = sb("small", list(small_in.shape), f32)

        def const(name):
            a, b = place[name]
            return small[:, a:b]

        ident = const("ident")
        before_b = sb("before_bf16", [P, P], bf16)
        ones_b = sb("ones_bf16", [P, P], bf16)
        minus_half = sb("minus_half", [P, T], f32)
        onehot = sb("onehot", [P, T, EXPERTS], bf16)
        block_sum = sb("block_sum", [P, EXPERTS], f32)
        so_far = sb("so_far", [P, EXPERTS], bf16)
        above = sb("above", [P, T, EXPERTS + 1], f32)
        row_id = sb("row_id", [P, T], f32)
        ready_mark = sb("ready_mark", [P, 1], f32)

        part1 = ctx.enter_context(ExitStack())
        wqk_h = sb("wqk_high", [P, 2, CC, HEADS, FEAT], f32r, part1)
        wqk_l = sb("wqk_low", [P, 2, CC, HEADS, FEAT], f32r, part1)
        wv_h = sb("wv_high", [P, CC, C], f32r, part1)
        wv_l = sb("wv_low", [P, CC, C], f32r, part1)
        wo_h = sb("wo_high", [P, CC, C], f32r, part1)
        wo_l = sb("wo_low", [P, CC, C], f32r, part1)
        dct_h = sb("dct_high", [P, 2, 2, HALF], f32r, part1)
        dct_l = sb("dct_low", [P, 2, 2, HALF], f32r, part1)
        qk_bias = sb("qk_bias", [P, 2 * HEADS], f32, part1)
        neg_ps = sb("minus_pscale", [P, HEADS], f32, part1)
        out_bias = sb("out_bias", [P, C], f32, part1)

        setup = ExitStack()
        with setup:
            wst = sb("padded_weights", [P, 2, CC, HEADS, FEAT], f32, setup)
            raw_s = sb("raw_wq_wk", [P, 2, CC, C], f32, setup)
            raw_p = sb("raw_wqp_wkp", [P, 2, CC, HEADS * POINT], f32, setup)
            raw_v = sb("raw_wv", [P, CC, C], f32, setup)
            raw_o = sb("raw_wo", [P, CC, C], f32, setup)
            raw_d = sb("raw_dct", [P, 2, 2, HALF], f32, setup)
            ln_g_c = sb("ln_g_c", [P, CC], f32, setup)
            ln_b_c = sb("ln_b_c", [P, CC], f32, setup)
            bv_c = sb("bv_c", [P, CC], f32, setup)
            raw_b = sb("raw_qk_bias", [P, 2 * HEADS], f32, setup)
            feat_s = sb("feature_scale", [P, 2 * HEADS], f32, setup)
            ps_b = sb("pscale_b", [P, HEADS], f32, setup)
            ps2 = sb("two_pscale", [P, HEADS], f32, setup)
            bo_b = sb("bo_b", [P, C], f32, setup)
            v_bias = sb("v_bias", [P, CC], f32, setup)
            v_bias_b = sb("v_bias_b", [P, CC, P], f32, setup)
            sentinel = sb("sentinel", [P, TABLE // P], f32, setup)
            zero_row = sb("zero_row", [1, C], f32, setup)

        xs = sb("samples", [P, T, HOP], f32, part1)
        fold = sb("folded", [P, 2, 2, HALF], f32, part1)
        xt_h = sb("frames_t_high", [P, 2, 4, P], f32r, part1)
        xt_l = sb("frames_t_low", [P, 2, 4, P], f32r, part1)
        h = sb("h", [P, T, C], f32, part1)
        hb = sb("h_plus_bias", [P, T, C], f32, part1)
        z = sb("z", [P, T, C], f32, part1)
        zt_h = sb("z_t_high", [P, CC, BLOCK], f32r, part1)
        zt_l = sb("z_t_low", [P, CC, BLOCK], f32r, part1)
        qf = sb("q_features", [P, 2, BLOCK], f32, part1)
        kf = sb("k_features", [P, 2, BLOCK], f32, part1)
        v = sb("v", [P, T, C], f32, part1)
        prob = sb("prob", [P, 2, HEADS, FRAMES], f32, part1)
        prob_t = sb("prob_t", [P, 2, HEADS, P], f32, part1)
        ot_h = sb("attended_t_high", [P, 2, CC, P], f32r, part1)
        ot_l = sb("attended_t_low", [P, 2, CC, P], f32r, part1)
        h1 = sb("h1", [P, 2, C], f32, part1)
        stat = sb("stat", [P, T, 6], f32, part1)
        mv = sb("mean_var", [P, T, 2], f32, part1)
        var2 = sb("var_eps", [P, T], f32, part1)
        rs = sb("z_scale", [P, T], f32, part1)
        mx = sb("score_max", [P, 2, HEADS], f32, part1)
        sm = sb("prob_sum", [P, 2, HEADS], f32, part1)
        rc = sb("prob_scale", [P, 2, HEADS], f32, part1)
        stat1 = sb("stat1", [P, T, 6], f32, part1)
        mv1 = sb("mean_var1", [P, T, 2], f32, part1)
        var1 = sb("var_eps1", [P, T], f32, part1)
        rs1 = sb("scale1", [P, T], f32, part1)
        first_ch = sb("h1_channel0", [P, T], f32, part1)
        centred = sb("channel0_centred", [P, T], f32, part1)
        y0 = sb("channel0", [P, T], f32, part1)
        slot_b = sb("slot_by_expert", [P, T, EXPERTS], f32, part1)
        slot_m = sb("slot_masked", [P, T, EXPERTS], f32, part1)
        slot_f = sb("slot", [P, T], f32, part1)
        slot = sb("slot_index", [P, T], u32, part1)
        part1.close()

        we_h = sb("w_ffn_high", [P, EXPERTS * CC * C], f32r)
        we_l = sb("w_ffn_low", [P, EXPERTS * CC * C], f32r)
        we_raw = sb("w_ffn_raw", [P, 2, CC * C], f32)
        counts = sb("counts", [P, EXPERTS], f32)
        exceeds = sb("exceeds", [P, EXPERTS, NTILE], f32)
        tiles_of = sb("tiles_of", [P, EXPERTS], f32)
        lower_m = sb("lower_masked", [P, EXPERTS, EXPERTS], f32)
        first_of = sb("first_tile_of", [P, EXPERTS], f32)
        started = sb("started", [P, EXPERTS], f32)
        skipped = sb("skipped", [P, EXPERTS - 1], f32)
        expert_of = sb("expert_of", [P, 1], f32)
        start_of = sb("start_of", [P, 1], f32)
        in_bucket = sb("in_bucket", [P, 1], f32)
        table_f = sb("table_row_f", [P, 1], f32)
        table_r = sb("table_row", [P, 1], u32)
        picked = sb("picked", [P, P], f32)
        index = sb("index", [P, FTILE], u32)
        index_in = sb("index_in", [P, 4], u32)
        index_out = sb("index_out", [P, 4], u32)
        expert_row = sb("expert_row", [1, FTILE], i32)
        g = sb("gathered", [P, 4, C], f32)
        z2 = sb("z2", [P, 2, C], f32)
        z2t_h = sb("z2_t_high", [P, 2, CC, P], f32r)
        z2t_l = sb("z2_t_low", [P, 2, CC, P], f32r)
        res = sb("result", [P, 2, C], f32)
        stat2 = sb("stat2", [P, 2, 6], f32)
        mv2 = sb("mean_var2", [P, 2, 2], f32)
        var_2 = sb("var_eps2", [P, 2], f32)
        rs2 = sb("scale2", [P, 2], f32)

        small_in_s, big_in_s, bias_in_s = sem("small_in"), sem("big_in"), sem("bias_in")
        zeroed, consts_made, pool_consts = sem("zeroed"), sem("consts_made"), sem("pool_consts")
        pad_step = sem("pad_step")
        dve_setup, act_setup = sem("dve_setup"), sem("act_setup")
        padded, w_high, bias_step, bias_mm = sem("padded"), sem("w_high"), sem("bias_step"), sem("bias_mm")
        vb_ready, ob_mm = sem("vb_ready"), sem("ob_mm")
        total_d = sem("total_d")
        table_cleared, prob_t_zero, xs_zero = sem("table_cleared"), sem("prob_t_zero"), sem("xs_zero")
        x_loaded, folded, frames_t = sem("x_loaded"), sem("folded"), sem("frames_t")
        xt_high, xt_low, dct_mm, h_ready = sem("xt_high"), sem("xt_low"), sem("dct_mm"), sem("h_ready")
        stat_d, aggr_d, var_p, scale_p = sem("stat_d"), sem("aggr_d"), sem("var_p"), sem("scale_p")
        z_ready, z_t, zt_high, zt_low = sem("z_ready"), sem("z_t"), sem("zt_high"), sem("zt_low")
        q_mm, k_mm, q_ev, k_ev = sem("q_mm"), sem("k_mm"), sem("q_ev"), sem("k_ev")
        q_sq, scored = sem("q_sq"), sem("scored")
        v_mm, v_ev = sem("v_mm"), sem("v_ev")
        max_d, shifted, exped, summed = sem("max_d"), sem("shifted"), sem("exped"), sem("summed")
        inverted, normed, probs_t = sem("inverted"), sem("normed"), sem("probs_t")
        pv_mm, ot_high, ot_low, wo_mm = sem("pv_mm"), sem("ot_high"), sem("ot_low"), sem("wo_mm")
        h1_ready, hb_ready = sem("h1_ready"), sem("hb_ready")
        h1_stored = [sem("h1_stored0"), sem("h1_stored1")]
        stat1_d, aggr1_d, var1_p, scale1_p = (sem("stat1_d"), sem("aggr1_d"), sem("var1_p"),
                                              sem("scale1_p"))
        cent_d, y0_d, above_d, onehot_d, block_sum_d, so_far_d = (
            sem("cent_d"), sem("y0_d"), sem("above_d"), sem("onehot_d"), sem("block_sum_d"),
            sem("so_far_d"))
        rank_mm, slot_b_d, slot_m_d, slot_f_d, slot_d = (sem("rank_mm"), sem("slot_b_d"),
                                                         sem("slot_m_d"), sem("slot_f_d"),
                                                         sem("slot_d"))
        scattered, ids_next = sem("scattered"), sem("ids_next")
        count_mm, plan_d, plan_s, table_in, picked_t, plan_t, index_d = (
            sem("count_mm"), sem("plan_d"), sem("plan_s"), sem("table_in"), sem("picked_t"), sem("plan_t"),
            sem("index_d"))
        we_in = [sem("we_in0"), sem("we_in1")]
        we_high, we_low = sem("we_high"), sem("we_low")
        g_in = [sem(f"g_in{k}") for k in range(4)]
        stat2_d, aggr2_d, var2_p, scale2_p, z2_ready = (sem("stat2_d"), sem("aggr2_d"),
                                                        sem("var2_p"), sem("scale2_p"),
                                                        sem("z2_ready"))
        z2_t, z2t_high, z2t_low, ffn_mm, res_ready = (sem("z2_t"), sem("z2t_high"), sem("z2t_low"),
                                                      sem("ffn_mm"), sem("res_ready"))
        index_in_p, index_out_p = sem("index_in_p"), sem("index_out_p")
        res_out = [sem("res_out0"), sem("res_out1")]

        block = ctx.enter_context(nc.Block())
        XD = 5 * 16
        SMALL_DMAS, BIG_DMAS, BIAS_DMAS = 1, 7, 12

        @block.sync
        def _(sp):
            sp.dma_start(small[:, :], small_in).then_inc(small_in_s, 16)
            sp.dma_start(raw_d[:, :, :, :], dct_in).then_inc(big_in_s, 16)
            for n, w in enumerate((wq, wk)):
                sp.dma_start(raw_s[:, n, :, :], w.rearrange("(c p) n -> p c n", p=P)).then_inc(big_in_s, 16)
            for n, w in enumerate((wqp, wkp)):
                sp.dma_start(raw_p[:, n, :, :], w.rearrange("(c p) n -> p c n", p=P)).then_inc(big_in_s, 16)
            sp.dma_start(raw_v[:, :, :], wv.rearrange("(c p) n -> p c n", p=P)).then_inc(big_in_s, 16)
            sp.dma_start(raw_o[:, :, :], wo.rearrange("(c p) n -> p c n", p=P)).then_inc(big_in_s, 16)
            sp.wait_ge(pool_consts, 4)
            sp.dma_start(table.rearrange("(p n) a -> p (n a)", p=P), sentinel[:, :]).then_inc(table_cleared, 16)
            sp.dma_start(h1_dram[ROWS:ROWS + 1, :], zero_row[:, :]).then_inc(table_cleared, 16)

            def load_samples(a, first=False):
                base = a * (BLOCK // FRAMES * SAMPLES)
                src = x_flat[bass.ds(base, BLOCK // FRAMES * SAMPLES)].rearrange(
                    "(t c n) -> c t n", c=CLIPS, n=SAMPLES)
                if not first:
                    sp.wait_ge(folded, 8 * a)
                for c in range(CLIPS):
                    full = src[c, :, 0:(FRAMES - 1) * HOP].rearrange("t (f n) -> f t n", n=HOP)
                    sp.dma_start(xs[32 * c:32 * c + FRAMES - 1, :, :], full).then_inc(x_loaded, 16)
                tails = src[:, :, (FRAMES - 1) * HOP:SAMPLES]
                sp.dma_start(xs[FRAMES - 1:P:FRAMES, :, 0:TAIL], tails).then_inc(x_loaded, 16)

            sp.wait_ge(xs_zero, 1)
            load_samples(0, first=True)

            def stores(i, nxt):
                if nxt:
                    load_samples(i + 1)
                for t in range(T):
                    sp.wait_ge(h1_ready, i * T + t + 1)
                    sp.dma_start(h1_dram[bass.ds(i * BLOCK + t * P, P), :], h1[:, t % 2, :])\
                        .then_inc(h1_stored[t % 2], 16)

            with sp.Fori(0, NBLOCK - 1) as i:
                stores(i, True)
            stores(NBLOCK - 1, False)

            for e in range(EXPERTS):
                if e == 0:
                    sp.wait_ge(plan_d, 1)
                if e >= 2:
                    sp.wait_ge(we_low, e - 1)
                sp.dma_start(we_raw[:, e % 2, :].rearrange("p (c n) -> p c n", c=CC),
                             w_ffn[e, :, :].rearrange("(c p) n -> p c n", p=P)).then_inc(we_in[e % 2], 16)
            for k in range(2):
                sp.wait_ge(h1_stored[k], 16 * NTILE // 2)

        @block.gpsimd
        def _(pool):
            pool.memset(raw_b[:, :], 0.0).then_inc(pool_consts, 1)
            pool.memset(sentinel[:, :], float(ROWS)).then_inc(pool_consts, 1)
            pool.memset(zero_row[:, :], 0.0).then_inc(pool_consts, 1)
            pool.memset(minus_half[:, :], -0.5).then_inc(pool_consts, 1)
            pool.wait_ge(pool_consts, 1)
            for dst, src in ((ln_g_c, ln_g), (ln_b_c, ln_b), (bv_c, bv)):
                pool.dma_start(dst[:, :], src.rearrange("(c p) -> p c", p=P), allow_slow_non_contiguous=True).then_inc(bias_in_s, 16)
            for n, (s, pt, sq) in enumerate(((bq, bqp, QSQ), (bk, bkp, KSQ))):
                hs = slice(n * HEADS, (n + 1) * HEADS)
                pool.dma_start(raw_b[0:HD, hs], s.rearrange("(h d) -> d h", d=HD), allow_slow_non_contiguous=True).then_inc(bias_in_s, 16)
                for at in (DOT, sq):
                    pool.dma_start(raw_b[at:at + POINT, hs], pt.rearrange("(h d) -> d h", d=POINT), allow_slow_non_contiguous=True)\
                        .then_inc(bias_in_s, 16)
            pool.dma_start(ps_b[:, :], pscale.rearrange("(a h) -> a h", a=1).to_broadcast([P, HEADS]))\
                .then_inc(bias_in_s, 16)
            pool.dma_start(bo_b[:, :], bo.rearrange("(a h) -> a h", a=1).to_broadcast([P, C]))\
                .then_inc(bias_in_s, 16)
            pool.dma_start(row_id[:, :], small_in[:, place["rows"][0]:place["rows"][1]])\
                .then_inc(bias_in_s, 16)
            pool.wait_ge(dve_setup, 1)
            pool.wait_ge(act_setup, 1)
            pool.wait_ge(table_cleared, 32)
            pool.memset(prob_t[:, :, :, :], 0.0).then_inc(prob_t_zero, 1)
            pool.memset(xs[:, :, :], 0.0).then_inc(xs_zero, 1)

            def fold_tile(a, t, first):
                if t == 0:
                    pool.wait_ge(x_loaded, XD * (a + 1))
                if t >= 2 or not first:
                    pool.wait_ge(frames_t, a * T + t - 1)
                back = xs[:, t, HOP - 1:HALF - 1:-1]
                pool.tensor_tensor(fold[:, t % 2, 0, :], xs[:, t, 0:HALF], back, ALU.add).then_inc(folded, 1)
                pool.tensor_tensor(fold[:, t % 2, 1, :], xs[:, t, 0:HALF], back, ALU.subtract)\
                    .then_inc(folded, 1)

            def z_scale(a):
                pool.wait_ge(aggr_d, T * (a + 1))
                pool.nop(nofuse=True)
                pool.tensor_scalar(var2[:, :], mv[:, :, 1], 1.0 + EPS, EPS * EPS, ALU.mult, ALU.add)\
                    .then_inc(var_p, 1)
                pool.wait_ge(var_p, a + 1)
                pool.tensor_tensor(rs[:, :], var2[:, :], minus_half[:, :], ALU.pow).then_inc(scale_p, 1)

            def add_bias(a, first):
                for t in range(T):
                    pool.wait_ge(h_ready, a * T + t + 1)
                    if not first:
                        pool.wait_ge(h1_ready, (a - 1) * T + t + 1)
                    pool.tensor_tensor(hb[:, t, :], h[:, t, :], out_bias[:, :], ALU.add)\
                        .then_inc(hb_ready, 1)

            def scatter_ids(i, first=False):
                pool.wait_ge(slot_d, i + 1)
                pool.nop(nofuse=True)
                for t in range(T):
                    pool.indirect_dma_start(
                        out=table, out_offset=bass.IndirectOffsetOnAxis(ap=slot[:, t:t + 1], axis=0),
                        in_=row_id[:, t:t + 1], in_offset=None).then_inc(scattered, 16)
                pool.wait_ge(scattered, 16 * T * (i + 1))
                pool.nop(nofuse=True)
                pool.tensor_scalar(row_id[:, :], row_id[:, :], 1.0, float(BLOCK), ALU.mult, ALU.add)\
                    .then_inc(ids_next, 1)

            for t in range(T):
                fold_tile(0, t, True)
            z_scale(0)

            def body(i, nxt, first):
                add_bias(i, first)
                for hd in range(HEADS):
                    if hd == 1 and not first:
                        scatter_ids(i - 1)
                    if nxt and hd < T:
                        fold_tile(i + 1, hd, False)
                    if nxt and hd == 6:
                        z_scale(i + 1)
                for t in range(T):
                    pool.wait_ge(inverted, i * T + t + 1)
                    pr = prob[:, t % 2, :, :]
                    pool.tensor_tensor(pr, pr, rc[:, t % 2, :].unsqueeze(2).to_broadcast([P, HEADS, FRAMES]),
                                       ALU.mult).then_inc(normed, 1)
                pool.wait_ge(aggr1_d, T * (i + 1))
                pool.nop(nofuse=True)
                pool.tensor_scalar(var1[:, :], mv1[:, :, 1], 1.0, EPS, ALU.mult, ALU.add).then_inc(var1_p, 1)
                pool.wait_ge(var1_p, i + 1)
                pool.tensor_tensor(rs1[:, :], var1[:, :], minus_half[:, :], ALU.pow).then_inc(scale1_p, 1)

            body(0, True, True)
            with pool.Fori(1, NBLOCK - 1) as i:
                body(i, True, False)
            body(NBLOCK - 1, False, False)
            scatter_ids(NBLOCK - 1)

            pool.wait_ge(plan_d, 8)
            pool.wait_ge(scattered, 16 * T * NBLOCK)
            pool.indirect_dma_start(
                out=picked[0:FTILE, :], out_offset=None, in_=table.rearrange("(r n) a -> r (n a)", n=P),
                in_offset=bass.IndirectOffsetOnAxis(ap=table_r[0:FTILE, :], axis=0)).then_inc(table_in, 16)
            pool.wait_ge(index_d, 2)
            for k in range(2):
                pool.wait_ge(h1_stored[k], 16 * NTILE // 2)

            def gather(u, k):
                pool.tensor_copy(index_in[:, k:k + 1], index[:, bass.ds(u, 1)]).then_inc(index_in_p, 1)
                pool.wait_ge(index_in_p, u + 1)
                pool.nop(nofuse=True)
                pool.indirect_dma_start(
                    out=g[:, k, :], out_offset=None, in_=h1_dram,
                    in_offset=bass.IndirectOffsetOnAxis(ap=index_in[:, k:k + 1], axis=0))\
                    .then_inc(g_in[k], 16)

            gather(0, 0)
            gather(1, 1)

            def ffn_tile(u, w, k, load, first):
                pool.wait_ge(aggr2_d, u + 1)
                pool.nop(nofuse=True)
                pool.tensor_scalar(var_2[:, k % 2:k % 2 + 1], mv2[:, k % 2, 1:2], 1.0, EPS, ALU.mult, ALU.add)\
                    .then_inc(var2_p, 1)
                pool.wait_ge(var2_p, u + 1)
                pool.tensor_tensor(rs2[:, k % 2:k % 2 + 1], var_2[:, k % 2:k % 2 + 1],
                                   minus_half[:, 0:1], ALU.pow).then_inc(scale2_p, 1)
                if not first:
                    store(u - 1, w if k else w - 1, (k - 1) % 4)
                if load:
                    gather(u + 2, (k + 2) % 4)

            def store(u, w, k):
                if not (isinstance(w, int) and w == 0):
                    pool.wait_ge(res_out[k % 2], 16 * (2 * w + k // 2 - 1))
                pool.nop(nofuse=True)
                pool.tensor_copy(index_out[:, k:k + 1], index[:, bass.ds(u, 1)]).then_inc(index_out_p, 1)
                pool.wait_ge(index_out_p, u + 1)
                pool.nop(nofuse=True)
                pool.wait_ge(res_ready, u + 1)
                pool.nop(nofuse=True)
                pool.indirect_dma_start(
                    out=out_rows, out_offset=bass.IndirectOffsetOnAxis(ap=index_out[:, k:k + 1], axis=0),
                    in_=res[:, k % 2, :], in_offset=None, bounds_check=ROWS - 1, oob_is_err=False)\
                    .then_inc(res_out[k % 2], 16)

            for k in range(4):
                ffn_tile(k, 0, k, True, k == 0)
            for k in range(4):
                ffn_tile(4 + k, 1, k, True, False)
            with pool.Fori(2, FTILE // 4 - 1) as w:
                for k in range(4):
                    ffn_tile(4 * w + k, w, k, True, False)
            for k in range(4):
                ffn_tile(FTILE - 4 + k, FTILE // 4 - 1, k, k < 2, False)
            store(FTILE - 1, FTILE // 4 - 1, 3)
            for k in range(2):
                pool.wait_ge(res_out[k], 16 * FTILE // 2)

        @block.scalar
        def _(act):
            act.wait_ge(big_in_s, 16 * BIG_DMAS)
            act.wait_ge(bias_in_s, 16 * BIAS_DMAS)
            act.activation(dct_h[:, :, :, :], raw_d[:, :, :, :], ACT.Copy).then_inc(w_high, 1)
            act.activation(wo_h[:, :, :], raw_o[:, :, :], ACT.Copy).then_inc(w_high, 1)
            for cc in range(CC):
                act.activation(wv_h[:, cc, :], raw_v[:, cc, :], ACT.Identity,
                               scale=ln_g_c[:, cc:cc + 1]).then_inc(w_high, 1)
            act.wait_ge(padded, 1)
            for n in range(2):
                for cc in range(CC):
                    act.activation(wqk_h[:, n, cc, :, :], wst[:, n, cc, :, :], ACT.Identity,
                                   scale=ln_g_c[:, cc:cc + 1]).then_inc(w_high, 1)
            act.activation(neg_ps[:, :], ps_b[:, :], ACT.Copy, scale=-1.0).then_inc(act_setup, 1)

            def frames_high(a, t, first):
                act.wait_ge(frames_t, a * T + t + 1)
                if t >= 2 or not first:
                    act.wait_ge(dct_mm, a * T + t - 1)
                act.activation(xt_h[:, t % 2, :, :], tr[t % 2][:, :], ACT.Copy).then_inc(xt_high, 1)

            def h_out(a, t, first):
                act.wait_ge(dct_mm, a * T + t + 1)
                if t == 0 and not first:
                    act.wait_ge(hb_ready, T * a)
                    act.wait_ge(z_ready, T * a)
                act.activation(h[:, t, :].rearrange("p (m two) -> p two m", two=2),
                               ro[t % 2][:, :].rearrange("p (two m) -> p two m", two=2), ACT.Copy)\
                    .then_inc(h_ready, 1)

            def z_high(a, cc, first):
                act.wait_ge(z_t, a * CC + cc + 1)
                if cc == 0 and not first:
                    act.wait_ge(v_mm, a * T)
                act.activation(zt_h[:, cc, :], tr[cc % 2][:, :], ACT.Copy).then_inc(zt_high, 1)

            for t in range(T):
                frames_high(0, t, True)
                h_out(0, t, True)
            for cc in range(CC):
                z_high(0, cc, True)

            def features(i, hd, first):
                n = i * HEADS + hd
                act.wait_ge(q_mm, n + 1)
                if hd >= 2 or not first:
                    act.wait_ge(scored, n - 1)
                act.activation(qf[0:FEAT, hd % 2, :], qk[0][0:FEAT, :], ACT.Identity,
                               bias=qk_bias[0:FEAT, hd:hd + 1]).then_inc(q_ev, 1)
                act.wait_ge(k_mm, n + 1)
                bias = qk_bias[:, HEADS + hd:HEADS + hd + 1]
                act.activation(kf[0:QSQ, hd % 2, :], qk[1][0:QSQ, :], ACT.Identity, bias=bias[0:QSQ, :])\
                    .then_inc(k_ev, 1)
                act.activation(kf[QSQ:FEAT, hd % 2, :], qk[1][QSQ:FEAT, :], ACT.Square,
                               bias=bias[QSQ:FEAT, :]).then_inc(k_ev, 1)

            def body(i, nxt, first):
                for hd in range(HEADS):
                    features(i, hd, first)
                    if nxt and 1 <= hd <= T:
                        frames_high(i + 1, hd - 1, False)
                    if nxt and 2 <= hd <= T + 1:
                        h_out(i + 1, hd - 2, False)
                for t in range(T):
                    act.wait_ge(v_mm, i * T + t + 1)
                    act.activation(v[:, t, :], ro[t % 2][:, :], ACT.Copy).then_inc(v_ev, 1)
                    act.wait_ge(shifted, i * T + t + 1)
                    act.activation(prob[:, t % 2, :, :], prob[:, t % 2, :, :], ACT.Exp).then_inc(exped, 1)
                if nxt:
                    for cc in range(CC):
                        z_high(i + 1, cc, False)
                for t in range(T):
                    act.wait_ge(pv_mm, i * T + t + 1)
                    if t >= 2 or not first:
                        act.wait_ge(wo_mm, i * T + t - 1)
                    act.activation(ot_h[:, t % 2, :, :], tr[t % 2][:, :], ACT.Copy).then_inc(ot_high, 1)

            body(0, True, True)
            with act.Fori(1, NBLOCK - 1) as i:
                body(i, True, False)
            body(NBLOCK - 1, False, False)

            for e in range(EXPERTS):
                act.wait_ge(we_in[e % 2], 16 * (e // 2 + 1))
                act.activation(we_h[:, e * CC * C:(e + 1) * CC * C], we_raw[:, e % 2, :], ACT.Copy)\
                    .then_inc(we_high, 1)

            def ffn_high(u, k, first):
                act.wait_ge(z2_t, u + 1)
                if not first:
                    act.wait_ge(ffn_mm, u - 1)
                act.activation(z2t_h[:, k, :, :], tr[k][:, :], ACT.Copy).then_inc(z2t_high, 1)

            ffn_high(0, 0, True)
            ffn_high(1, 1, True)
            with act.Fori(1, FTILE // 2) as w:
                for k in range(2):
                    ffn_high(2 * w + k, k, False)

        @block.vector
        def _(dve):
            dve.memset(wst[:, :, :, :, :], 0.0).then_inc(zeroed, 1)
            dve.memset(ones_b[:, :], 1.0).then_inc(consts_made, 1)
            dve.memset(so_far[:, :], 0.0).then_inc(consts_made, 1)
            dve.memset(above[:, :, 0:1], 1.0).then_inc(consts_made, 1)
            dve.memset(above[:, :, EXPERTS:EXPERTS + 1], 0.0).then_inc(consts_made, 1)
            dve.wait_ge(small_in_s, 16 * SMALL_DMAS)
            dve.tensor_copy(before_b[:, :], const("before")).then_inc(consts_made, 1)
            dve.wait_ge(big_in_s, 16 * BIG_DMAS)
            dve.wait_ge(bias_in_s, 16 * BIAS_DMAS)
            dve.wait_ge(zeroed, 1)
            dve.tensor_scalar(ps2[:, :], ps_b[:, :], 2.0, None, ALU.mult).then_inc(pad_step, 1)
            dve.wait_ge(pad_step, 1)
            for cc in range(CC):
                for n, sq in ((0, QSQ), (1, KSQ)):
                    scalar = raw_s[:, n, cc, :].rearrange("p (h d) -> p h d", h=HEADS)
                    points = raw_p[:, n, cc, :].rearrange("p (h d) -> p h d", h=HEADS)
                    to = wst[:, n, cc, :, :]
                    if n == 0:
                        dve.tensor_scalar(to[:, :, 0:HD], scalar, HD ** -0.5, None, ALU.mult)\
                            .then_inc(pad_step, 1)
                        dve.tensor_tensor(to[:, :, DOT:DOT + POINT], points,
                                          ps2[:, :].unsqueeze(2).to_broadcast([P, HEADS, POINT]), ALU.mult)\
                            .then_inc(pad_step, 1)
                    else:
                        dve.tensor_copy(to[:, :, 0:HD], scalar).then_inc(pad_step, 1)
                        dve.tensor_copy(to[:, :, DOT:DOT + POINT], points).then_inc(pad_step, 1)
                    dve.tensor_copy(to[:, :, sq:sq + POINT], points).then_inc(pad_step, 1)
            dve.wait_ge(pad_step, 1 + 6 * CC)
            for n in range(2):
                hs = slice(n * HEADS, (n + 1) * HEADS)
                dve.tensor_tensor(feat_s[:, hs], const("per")[:, hs], ps_b[:, :], ALU.mult).then_inc(padded, 1)
            dve.wait_ge(padded, 2)
            dve.tensor_tensor(feat_s[:, :], feat_s[:, :], const("own"), ALU.add).then_inc(bias_step, 1)
            dve.wait_ge(bias_step, 1)
            dve.tensor_tensor(raw_b[:, :], raw_b[:, :], feat_s[:, :], ALU.mult).then_inc(bias_step, 1)
            dve.wait_ge(bias_step, 2)
            dve.tensor_tensor(raw_b[:, :], raw_b[:, :], const("one"), ALU.add).then_inc(bias_step, 1)
            dve.wait_ge(bias_step, 3)
            dve.wait_ge(bias_mm, 1)
            dve.tensor_tensor(qk_bias[0:FEAT, :], raw_b[0:FEAT, :], qk[0][0:FEAT, 0:2 * HEADS], ALU.add)\
                .then_inc(bias_step, 1)
            dve.tensor_tensor(v_bias[:, :], bv_c[:, :], qk[1][:, 0:CC], ALU.add).then_inc(bias_step, 1)
            dve.wait_ge(bias_step, 5)
            dve.tensor_copy(v_bias_b[:, :, :], v_bias[:, :].unsqueeze(2).to_broadcast([P, CC, P]))\
                .then_inc(vb_ready, 1)
            dve.wait_ge(w_high, 2 + 3 * CC)
            for cc in range(CC):
                dve.scalar_tensor_tensor(out=wv_l[:, cc, :], in0=raw_v[:, cc, :], scalar=ln_g_c[:, cc:cc + 1],
                                         in1=wv_h[:, cc, :], op0=ALU.mult, op1=ALU.subtract)\
                    .then_inc(bias_step, 1)
                for n in range(2):
                    dve.scalar_tensor_tensor(out=wqk_l[:, n, cc, :, :], in0=wst[:, n, cc, :, :],
                                             scalar=ln_g_c[:, cc:cc + 1], in1=wqk_h[:, n, cc, :, :],
                                             op0=ALU.mult, op1=ALU.subtract).then_inc(bias_step, 1)
            dve.tensor_tensor(wo_l[:, :, :], raw_o[:, :, :], wo_h[:, :, :], ALU.subtract).then_inc(bias_step, 1)
            dve.tensor_tensor(dct_l[:, :, :, :], raw_d[:, :, :, :], dct_h[:, :, :, :], ALU.subtract)\
                .then_inc(bias_step, 1)
            dve.wait_ge(ob_mm, 1)
            dve.tensor_tensor(out_bias[:, :], bo_b[:, :], ro[0][:, :], ALU.add).then_inc(bias_step, 1)
            dve.wait_ge(bias_step, 5 + 3 * CC + 3)
            dve.tensor_copy(ready_mark[:, :], ones_b[:, 0:1]).then_inc(dve_setup, 1)

            def frames_low(a, t):
                dve.wait_ge(xt_high, a * T + t + 1)
                dve.tensor_tensor(xt_l[:, t % 2, :, :], tr[t % 2][:, :].rearrange("p (c r) -> p c r", c=4),
                                  xt_h[:, t % 2, :, :], ALU.subtract).then_inc(xt_low, 1)

            def h_stats(a, t, first):
                dve.wait_ge(h_ready, a * T + t + 1)
                if t == 0 and not first:
                    dve.wait_ge(z_ready, T * a)
                dve.bn_stats(stat[:, t, :], h[:, t, :]).then_inc(stat_d, 1)
                dve.wait_ge(stat_d, a * T + t + 1)
                dve.nop(nofuse=True)
                dve.bn_aggr(mv[:, t, :], stat[:, t, :]).then_inc(aggr_d, 1)

            def z_tiles(a, first):
                dve.wait_ge(scale_p, a + 1)
                if not first:
                    dve.wait_ge(z_t, CC * a)
                for t in range(T):
                    dve.tensor_scalar(z[:, t, :], h[:, t, :], mv[:, t, 0:1], rs[:, t:t + 1],
                                      ALU.subtract, ALU.mult).then_inc(z_ready, 1)

            def z_low(a, cc):
                dve.wait_ge(zt_high, a * CC + cc + 1)
                dve.tensor_tensor(zt_l[:, cc, :], tr[cc % 2][:, :], zt_h[:, cc, :], ALU.subtract)\
                    .then_inc(zt_low, 1)

            for t in range(T):
                frames_low(0, t)
                h_stats(0, t, True)
            z_tiles(0, True)
            for cc in range(CC):
                z_low(0, cc)

            def query_square(i, hd):
                dve.wait_ge(q_ev, i * HEADS + hd + 1)
                sq = qf[QSQ:FEAT, hd % 2, :]
                dve.scalar_tensor_tensor(out=sq, in0=sq, scalar=neg_ps[QSQ:FEAT, hd:hd + 1], in1=sq,
                                         op0=ALU.mult, op1=ALU.mult).then_inc(q_sq, 1)

            def shift(i, t):
                s = sc[t // 2][:, t % 2, :, :]
                k = t % 2
                if t >= 2:
                    dve.wait_ge(probs_t, i * T + t - 1)
                dve.tensor_reduce(mx[:, k, :], s, XA, ALU.max).then_inc(max_d, 1)
                dve.wait_ge(max_d, i * T + t + 1)
                dve.tensor_tensor(prob[:, k, :, :], s, mx[:, k, :].unsqueeze(2).to_broadcast([P, HEADS, FRAMES]),
                                  ALU.subtract).then_inc(shifted, 1)

            def total(i, t):
                k = t % 2
                dve.wait_ge(exped, i * T + t + 1)
                dve.tensor_reduce(sm[:, k, :], prob[:, k, :, :], XA, ALU.add).then_inc(summed, 1)
                dve.wait_ge(summed, i * T + t + 1)
                if t >= 2:
                    dve.wait_ge(normed, i * T + t - 1)
                dve.reciprocal(rc[:, k, :], sm[:, k, :]).then_inc(inverted, 1)

            def spread(i, t, first):
                dve.wait_ge(normed, i * T + t + 1)
                if t >= 2 or not first:
                    dve.wait_ge(pv_mm, i * T + t - 1)
                for c in range(CLIPS):
                    q = slice(32 * c, 32 * c + 32)
                    last = dve.transpose(prob_t[q, t % 2, :, 32 * c:32 * c + 32], prob[q, t % 2, :, :])
                last.then_inc(probs_t, 1)

            def attended_low(i, t):
                dve.wait_ge(ot_high, i * T + t + 1)
                dve.tensor_tensor(ot_l[:, t % 2, :, :], tr[t % 2][:, :].rearrange("p (c r) -> p c r", c=CC),
                                  ot_h[:, t % 2, :, :], ALU.subtract).then_inc(ot_low, 1)

            def h1_tile(i, t, first):
                dve.wait_ge(wo_mm, i * T + t + 1)
                if t < 2:
                    if not first:
                        dve.wait_ge(h1_stored[t], 32 * i)
                else:
                    dve.wait_ge(h1_stored[t % 2], 32 * i + 16)
                dve.wait_ge(hb_ready, i * T + t + 1)
                dve.tensor_tensor(h1[:, t % 2, :], hb[:, t, :], ro[t % 2][:, :], ALU.add).then_inc(h1_ready, 1)
                dve.wait_ge(h1_ready, i * T + t + 1)
                dve.bn_stats(stat1[:, t, :], h1[:, t % 2, :]).then_inc(stat1_d, 1)
                dve.tensor_copy(first_ch[:, t:t + 1], h1[:, t % 2, 0:1]).then_inc(stat1_d, 1)
                dve.wait_ge(stat1_d, 2 * (i * T + t + 1))
                dve.nop(nofuse=True)
                dve.bn_aggr(mv1[:, t, :], stat1[:, t, :]).then_inc(aggr1_d, 1)

            def choose(i, first):
                dve.wait_ge(aggr1_d, T * (i + 1))
                dve.tensor_tensor(centred[:, :], first_ch[:, :], mv1[:, :, 0], ALU.subtract).then_inc(cent_d, 1)
                dve.wait_ge(cent_d, i + 1)
                dve.wait_ge(scale1_p, i + 1)
                dve.tensor_tensor(y0[:, :], centred[:, :], rs1[:, :], ALU.mult).then_inc(y0_d, 1)
                dve.wait_ge(y0_d, i + 1)
                dve.tensor_tensor(above[:, :, 1:EXPERTS], y0[:, :].unsqueeze(2).to_broadcast([P, T, EXPERTS - 1]),
                                  const("bins").unsqueeze(1).to_broadcast([P, T, EXPERTS - 1]), ALU.is_gt)\
                    .then_inc(above_d, 1)
                dve.wait_ge(above_d, i + 1)
                dve.tensor_tensor(onehot[:, :, :], above[:, :, 0:EXPERTS], above[:, :, 1:EXPERTS + 1],
                                  ALU.subtract).then_inc(onehot_d, 1)

            def slots(i):
                dve.wait_ge(rank_mm, i + 1)
                dve.tensor_tensor(slot_b[:, :, :], ro[0][:, 0:T * EXPERTS].rearrange("p (t e) -> p t e", t=T),
                                  const("bucket").unsqueeze(1).to_broadcast([P, T, EXPERTS]), ALU.add)\
                    .then_inc(slot_b_d, 1)
                dve.tensor_reduce(block_sum[:, :], onehot[:, :, :].rearrange("p t e -> p e t"), XA, ALU.add)\
                    .then_inc(block_sum_d, 1)
                dve.wait_ge(slot_b_d, i + 1)
                dve.tensor_tensor(slot_m[:, :, :], slot_b[:, :, :], onehot[:, :, :], ALU.mult)\
                    .then_inc(slot_m_d, 1)
                dve.wait_ge(block_sum_d, i + 1)
                dve.tensor_tensor(so_far[:, :], so_far[:, :], block_sum[:, :], ALU.add).then_inc(so_far_d, 1)
                dve.wait_ge(slot_m_d, i + 1)
                dve.tensor_reduce(slot_f[:, :], slot_m[:, :, :], XA, ALU.add).then_inc(slot_f_d, 1)
                dve.wait_ge(slot_f_d, i + 1)

            def slots_out(i, first):
                if not first:
                    dve.wait_ge(scattered, 16 * T * i)
                dve.tensor_copy(slot[:, :], slot_f[:, :]).then_inc(slot_d, 1)

            def body(i, nxt, first):
                for hd in range(HEADS):
                    query_square(i, hd)
                    if hd == 1 and not first:
                        slots(i - 1)
                        slots_out(i - 1, isinstance(i, int) and i == 1)
                    if nxt and 1 <= hd <= T:
                        frames_low(i + 1, hd - 1)
                    if nxt and 2 <= hd <= T + 1:
                        h_stats(i + 1, hd - 2, False)
                if nxt:
                    z_tiles(i + 1, False)
                dve.wait_ge(scored, HEADS * (i + 1))
                shift(i, 0)
                shift(i, 1)
                for t in range(2):
                    total(i, t)
                    spread(i, t, first)
                    shift(i, t + 2)
                if nxt:
                    for cc in range(CC):
                        z_low(i + 1, cc)
                for t in range(2):
                    total(i, t + 2)
                    attended_low(i, t)
                    spread(i, t + 2, first)
                h1_tile(i, 0, first)
                for t in range(2, T):
                    attended_low(i, t)
                    h1_tile(i, t - 1, first)
                h1_tile(i, T - 1, first)
                choose(i, first)

            body(0, True, True)
            body(1, True, False)
            with dve.Fori(2, NBLOCK - 1) as i:
                body(i, True, False)
            body(NBLOCK - 1, False, False)
            slots(NBLOCK - 1)
            slots_out(NBLOCK - 1, False)

            dve.wait_ge(count_mm, 1)
            dve.wait_ge(scattered, 16 * T * NBLOCK)
            for k in range(2):
                dve.wait_ge(h1_stored[k], 16 * NTILE // 2)
            dve.tensor_copy(counts[:, :], ro[1][:, 0:EXPERTS]).then_inc(plan_d, 1)
            dve.wait_ge(plan_d, 1)
            dve.tensor_tensor(exceeds[:, :, :], counts[:, :].unsqueeze(2).to_broadcast([P, EXPERTS, NTILE]),
                              const("tile128").unsqueeze(1).to_broadcast([P, EXPERTS, NTILE]), ALU.is_gt)\
                .then_inc(plan_d, 1)
            dve.wait_ge(plan_d, 2)
            dve.tensor_reduce(tiles_of[:, :], exceeds[:, :, :], XA, ALU.add).then_inc(plan_d, 1)
            dve.wait_ge(plan_d, 3)
            dve.tensor_tensor(lower_m[:, :, :], tiles_of[:, :].unsqueeze(1).to_broadcast([P, EXPERTS, EXPERTS]),
                              const("lower").rearrange("p (a b) -> p a b", a=EXPERTS), ALU.mult)\
                .then_inc(plan_d, 1)
            dve.wait_ge(plan_d, 4)
            dve.tensor_reduce(first_of[:, :], lower_m[:, :, :], XA, ALU.add).then_inc(plan_d, 1)
            dve.wait_ge(plan_d, 5)
            dve.tensor_scalar(started[:, :], first_of[:, :], const("partition"), None, ALU.is_le)\
                .then_inc(plan_d, 1)
            dve.wait_ge(plan_d, 6)
            dve.tensor_reduce(expert_of[:, :], started[:, 1:EXPERTS], XA, ALU.add).then_inc(plan_d, 1)
            dve.tensor_tensor(skipped[:, :], started[:, 1:EXPERTS], tiles_of[:, 0:EXPERTS - 1], ALU.mult)\
                .then_inc(plan_s, 1)
            dve.wait_ge(plan_s, 1)
            dve.tensor_reduce(start_of[:, :], skipped[:, :], XA, ALU.add).then_inc(plan_s, 1)
            dve.wait_ge(plan_s, 2)
            dve.tensor_tensor(in_bucket[:, :], const("partition"), start_of[:, :], ALU.subtract)\
                .then_inc(plan_s, 1)
            dve.wait_ge(plan_s, 3)
            dve.wait_ge(plan_d, 7)
            dve.scalar_tensor_tensor(out=table_f[:, :], in0=expert_of[:, :], scalar=float(BUCKET // P),
                                     in1=in_bucket[:, :], op0=ALU.mult, op1=ALU.add).then_inc(plan_s, 1)
            dve.wait_ge(plan_s, 4)
            dve.tensor_copy(table_r[:, :], table_f[:, :]).then_inc(plan_d, 1)
            dve.wait_ge(plan_t, 1)
            dve.tensor_copy(expert_row[0:1, :], ro[0][0:1, 0:FTILE]).then_inc(index_d, 1)
            dve.wait_ge(picked_t, 1)
            dve.tensor_copy(index[:, :], tr[0][:, 0:FTILE]).then_inc(index_d, 1)

            for e in range(EXPERTS):
                dve.wait_ge(we_high, e + 1)
                dve.tensor_tensor(we_l[:, e * CC * C:(e + 1) * CC * C], we_raw[:, e % 2, :],
                                  we_h[:, e * CC * C:(e + 1) * CC * C], ALU.subtract).then_inc(we_low, 1)

            def ffn_stats(u, w, k, first):
                dve.wait_ge(g_in[k], 16 * (w + 1))
                if not first:
                    dve.wait_ge(z2_ready, u - 1)
                dve.bn_stats(stat2[:, k % 2, :], g[:, k, :]).then_inc(stat2_d, 1)
                dve.wait_ge(stat2_d, u + 1)
                dve.nop(nofuse=True)
                dve.bn_aggr(mv2[:, k % 2, :], stat2[:, k % 2, :]).then_inc(aggr2_d, 1)

            def ffn_norm(u, k, first):
                dve.wait_ge(scale2_p, u + 1)
                if not first:
                    dve.wait_ge(z2_t, u - 1)
                dve.tensor_scalar(z2[:, k % 2, :], g[:, k, :], mv2[:, k % 2, 0:1], rs2[:, k % 2:k % 2 + 1],
                                  ALU.subtract, ALU.mult).then_inc(z2_ready, 1)

            def ffn_low(u, k):
                dve.wait_ge(z2t_high, u + 1)
                dve.tensor_tensor(z2t_l[:, k % 2, :, :], tr[k % 2][:, :].rearrange("p (c r) -> p c r", c=CC),
                                  z2t_h[:, k % 2, :, :], ALU.subtract).then_inc(z2t_low, 1)

            def ffn_out(u, w, k, first):
                dve.wait_ge(ffn_mm, u + 1)
                if not first:
                    dve.wait_ge(res_out[k % 2], 16 * (2 * w + k // 2))
                dve.tensor_tensor(res[:, k % 2, :], g[:, k, :], ro[k % 2][:, :], ALU.add).then_inc(res_ready, 1)

            def ffn_group(w, first, last):
                for k in range(4):
                    u = 4 * w + k
                    ffn_stats(u, w, k, first and k < 2)
                    ffn_norm(u, k, first and k < 2)
                    ffn_low(u, k)
                    if not (first and k == 0):
                        pk = (k - 1) % 4
                        ffn_out(u - 1, w if k else w - 1, pk, first and k - 1 < 2)

            ffn_group(0, True, False)
            with dve.Fori(1, FTILE // 4) as w:
                ffn_group(w, False, False)
            ffn_out(FTILE - 1, FTILE // 4 - 1, 3, False)

        @block.tensor
        def _(pe):
            pe.wait_ge(padded, 2)
            for n in range(2):
                for hd in range(HEADS):
                    for cc in range(CC):
                        pe.matmul(qk[0][0:FEAT, n * HEADS + hd:n * HEADS + hd + 1], wst[:, n, cc, hd, :],
                                  ln_b_c[:, cc:cc + 1], start=cc == 0, stop=cc == CC - 1)
            for co in range(CC):
                for cc in range(CC):
                    last = pe.matmul(qk[1][:, co:co + 1], raw_v[:, cc, co * P:(co + 1) * P],
                                     ln_b_c[:, cc:cc + 1], start=cc == 0, stop=cc == CC - 1)
            last.then_inc(bias_mm, 1)
            pe.wait_ge(vb_ready, 1)
            for cc in range(CC):
                last = pe.matmul(ro[0][:, :], v_bias_b[:, cc, :], raw_o[:, cc, :], start=cc == 0, stop=cc == CC - 1)
            last.then_inc(ob_mm, 1)
            pe.wait_ge(dve_setup, 1)

            def product(out_ap, pairs):
                n = 0
                for (wh, wl), (mh, ml) in pairs:
                    for w, m in ((wh, mh), (wh, ml), (wl, mh)):
                        n += 1
                        last = pe.matmul(out_ap, w, m, start=n == 1, stop=n == 3 * len(pairs))
                return last

            def transpose_frames(a, t):
                pe.wait_ge(folded, 2 * (a * T + t + 1))
                for c in range(4):
                    last = pe.transpose(tr[t % 2][:, c * P:(c + 1) * P],
                                        fold[:, t % 2, c // 2, (c % 2) * P:(c % 2 + 1) * P], ident)
                last.then_inc(frames_t, 1)

            def dct(a, t):
                pe.wait_ge(xt_low, a * T + t + 1)
                for eo in range(2):
                    last = product(ro[t % 2][:, eo * HALF:(eo + 1) * HALF],
                                   [((xt_h[:, t % 2, 2 * eo + c, :], xt_l[:, t % 2, 2 * eo + c, :]),
                                     (dct_h[:, eo, c, :], dct_l[:, eo, c, :])) for c in range(2)])
                last.then_inc(dct_mm, 1)

            def transpose_z(a, cc):
                pe.wait_ge(z_ready, T * (a + 1))
                if cc >= 2:
                    pe.wait_ge(zt_low, a * CC + cc - 1)
                for t in range(T):
                    last = pe.transpose(tr[cc % 2][:, t * P:(t + 1) * P], z[:, t, cc * P:(cc + 1) * P], ident)
                last.then_inc(z_t, 1)

            transpose_frames(0, 0)
            transpose_frames(0, 1)
            for t in range(T):
                if t >= 2:
                    pe.wait_ge(h_ready, t - 1)
                dct(0, t)
                if t + 2 < T:
                    transpose_frames(0, t + 2)
            for cc in range(CC):
                if cc < 2:
                    pe.wait_ge(xt_low, T)
                transpose_z(0, cc)

            def features(i, hd, side, first):
                if hd == 0 and side == 0:
                    pe.wait_ge(zt_low, CC * (i + 1))
                if hd or not first:
                    if side == 0:
                        pe.wait_ge(q_ev, i * HEADS + hd)
                    else:
                        pe.wait_ge(k_ev, 2 * (i * HEADS + hd))
                product(qk[side][0:FEAT, :],
                        [((wqk_h[:, side, cc, hd, :], wqk_l[:, side, cc, hd, :]),
                          (zt_h[:, cc, :], zt_l[:, cc, :])) for cc in range(CC)])\
                    .then_inc((q_mm, k_mm)[side], 1)

            def scores(i, hd, first):
                n = i * HEADS + hd
                pe.wait_ge(q_sq, n + 1)
                pe.wait_ge(k_ev, 2 * (n + 1))
                if hd == 0 and not first:
                    pe.wait_ge(shifted, T * i)
                for t in range(T):
                    for c in range(CLIPS):
                        cols = slice(t * P + 32 * c, t * P + 32 * c + 32)
                        last = pe.matmul(sc[t // 2][32 * c:32 * c + 32, t % 2, hd, :], qf[0:FEAT, hd % 2, cols],
                                         kf[0:FEAT, hd % 2, cols], start=True, stop=True)
                last.then_inc(scored, 1)

            def values(i, t):
                if t >= 2:
                    pe.wait_ge(v_ev, i * T + t - 1)
                product(ro[t % 2][:, :],
                        [((zt_h[:, cc, t * P:(t + 1) * P], zt_l[:, cc, t * P:(t + 1) * P]),
                          (wv_h[:, cc, :], wv_l[:, cc, :])) for cc in range(CC)]).then_inc(v_mm, 1)

            def attend(i, t):
                pe.wait_ge(probs_t, i * T + t + 1)
                pe.wait_ge(v_ev, i * T + t + 1)
                if t >= 2:
                    pe.wait_ge(ot_low, i * T + t - 1)
                for hd in range(HEADS):
                    half = 64 * (hd % 2)
                    last = pe.matmul(tr[t % 2][half:half + HD, (hd // 2) * P:(hd // 2 + 1) * P],
                                     v[:, t, hd * HD:(hd + 1) * HD], prob_t[:, t % 2, hd, :],
                                     start=True, stop=True)
                last.then_inc(pv_mm, 1)

            def project(i, t):
                pe.wait_ge(ot_low, i * T + t + 1)
                if t >= 2:
                    pe.wait_ge(h1_ready, i * T + t - 1)
                product(ro[t % 2][:, :],
                        [((ot_h[:, t % 2, cc, :], ot_l[:, t % 2, cc, :]), (wo_h[:, cc, :], wo_l[:, cc, :]))
                         for cc in range(CC)]).then_inc(wo_mm, 1)

            def rank(i):
                pe.wait_ge(onehot_d, i + 1)
                pe.wait_ge(h1_ready, T * (i + 1))
                r = ro[0][:, 0:T * EXPERTS].rearrange("p (t e) -> p t e", t=T)
                pe.matmul(r, before_b[:, :], onehot[:, :, :], start=True, stop=False)
                for t in range(1, T):
                    pe.matmul(r[:, t:T, :], ones_b[:, :], onehot[:, 0:T - t, :], start=False, stop=False)
                pe.matmul(r, ones_b[:, :], so_far[:, :].unsqueeze(1).to_broadcast([P, T, EXPERTS]),
                          start=False, stop=True).then_inc(rank_mm, 1)

            def body(i, nxt, first):
                for hd in range(HEADS):
                    for side in range(2):
                        features(i, hd, side, first)
                    if hd:
                        scores(i, hd - 1, first)
                    if hd == 0 and not first:
                        pe.wait_ge(so_far_d, i - 1) if not (isinstance(i, int) and i == 1) else None
                        rank(i - 1)
                    if nxt and hd < T:
                        if hd < 2:
                            pe.wait_ge(ot_low, T * i) if not first else pe.wait_ge(zt_low, CC)
                        transpose_frames(i + 1, hd)
                    if nxt and 1 <= hd <= T:
                        if hd == 1 and not first:
                            pe.wait_ge(slot_b_d, i)
                        if hd >= 3:
                            pe.wait_ge(h_ready, (i + 1) * T + hd - 2)
                        if hd == 2:
                            pe.wait_ge(h1_ready, i * T) if not first else None
                        dct(i + 1, hd - 1)
                scores(i, HEADS - 1, first)
                for t in range(T):
                    if nxt and t < 2:
                        pe.wait_ge(h_ready, (i + 1) * T + t + 3)
                    if not nxt and t == 0:
                        pe.wait_ge(slot_b_d, i)
                    values(i, t)
                if nxt:
                    for cc in range(CC):
                        if cc == 0:
                            pe.wait_ge(xt_low, (i + 2) * T)
                        transpose_z(i + 1, cc)
                for t in range(T):
                    if t < 2:
                        if nxt:
                            pe.wait_ge(zt_low, CC * (i + 2))
                        else:
                            pe.wait_ge(zt_low, CC * NBLOCK)
                    attend(i, t)
                    if t:
                        if t < 3:
                            pe.wait_ge(v_ev, i * T + t + 2)
                        project(i, t - 1)
                project(i, T - 1)

            body(0, True, True)
            body(1, True, False)
            with pe.Fori(2, NBLOCK - 1) as i:
                body(i, True, False)
            body(NBLOCK - 1, False, False)
            pe.wait_ge(so_far_d, NBLOCK - 1)
            rank(NBLOCK - 1)
            pe.wait_ge(so_far_d, NBLOCK)
            pe.matmul(ro[1][:, 0:EXPERTS], ones_b[:, :], so_far[:, :], start=True, stop=True).then_inc(count_mm, 1)

            pe.wait_ge(plan_d, 8)
            pe.matmul(ro[0][0:1, 0:FTILE], expert_of[0:FTILE, :], ident[0:FTILE, 0:FTILE],
                      start=True, stop=True).then_inc(plan_t, 1)
            pe.wait_ge(table_in, 16)
            pe.transpose(tr[0][:, 0:FTILE], picked[0:FTILE, :], ident[0:FTILE, 0:FTILE]).then_inc(picked_t, 1)
            pe.wait_ge(index_d, 2)

            def transpose_rows(u, k, first):
                pe.wait_ge(z2_ready, u + 1)
                if not first:
                    pe.wait_ge(z2t_low, u - 1)
                for cc in range(CC):
                    last = pe.transpose(tr[k][:, cc * P:(cc + 1) * P], z2[:, k, cc * P:(cc + 1) * P], ident)
                last.then_inc(z2_t, 1)

            def expert_product(u, k, first):
                e = pe.value_load(expert_row[0:1, bass.ds(u, 1)], min_val=0, max_val=EXPERTS - 1)
                pe.wait_ge(we_low, e + 1)
                pe.wait_ge(z2t_low, u + 1)
                if not first:
                    pe.wait_ge(res_ready, u - 1)
                at = e * (CC * C)
                product(ro[k][:, :],
                        [((z2t_h[:, k, cc, :], z2t_l[:, k, cc, :]),
                          (we_h[:, bass.ds(at + cc * C, C)], we_l[:, bass.ds(at + cc * C, C)]))
                         for cc in range(CC)]).then_inc(ffn_mm, 1)

            transpose_rows(0, 0, True)
            transpose_rows(1, 1, True)
            expert_product(0, 0, True)
            transpose_rows(2, 0, False)
            expert_product(1, 1, True)
            with pe.Fori(1, FTILE // 2 - 1) as w:
                for k in range(2):
                    transpose_rows(2 * w + k + 1, 1 - k, False)
                    expert_product(2 * w + k, k, False)
            transpose_rows(FTILE - 1, 1, False)
            expert_product(FTILE - 2, 0, False)
            expert_product(FTILE - 1, 1, False)


_INS = ["x", "L0_attn_ln_g", "L0_attn_ln_b", "L0_attn_wq", "L0_attn_bq", "L0_attn_wk", "L0_attn_bk",
        "L0_attn_wv", "L0_attn_bv", "L0_attn_wqp", "L0_attn_bqp", "L0_attn_wkp", "L0_attn_bkp",
        "L0_attn_wo", "L0_attn_bo", "L0_attn_pscale", "L0_ffn_W"]


def kernel(**inputs):
    import concourse.bacc as bacc
    from concourse.bass_utils import run_bass_kernel_spmd

    nc = bacc.Bacc("TRN2", target_bir_lowering=False, num_devices=1)
    dct, small, place = constants()
    arrays = {f"in_{n}": np.ascontiguousarray(inputs[n]) for n in _INS}
    arrays["const_dct"], arrays["const_small"] = dct, small
    aps = [nc.dram_tensor(n, a.shape, mybir.dt.from_np(a.dtype), kind="ExternalInput").ap()
           for n, a in arrays.items()]
    out = nc.dram_tensor("out", (BATCH, FRAMES, C), mybir.dt.float32, kind="ExternalOutput").ap()
    audio_tower(nc, *aps, place, out)
    r = run_bass_kernel_spmd(nc, [arrays], core_ids=[0])
    return r.results[0]["out"]
```

```python
import numpy as np
from contextlib import ExitStack

import concourse.bass as bass
from concourse import mybir


BATCH, SAMPLES, HOP = 256, 16000, 512
FRAMES = (SAMPLES + HOP - SAMPLES % HOP) // HOP
TAIL = SAMPLES - (FRAMES - 1) * HOP
ROWS = BATCH * FRAMES
C = HOP
HEADS, POINT = 8, 12
POINTS = HEADS * POINT
HD = C // HEADS
BINS = (-1.5, -1.0, -0.5, 0.0, 0.5, 1.0, 1.5)
EXPERTS = len(BINS) + 1
EPS = 1e-5
P = 128
CC = C // P
PAIRS = HEADS // 2
CLIPS = P // FRAMES
T = 4
BLOCK = T * P
NBLOCK = ROWS // BLOCK
NTILE = ROWS // P
HALF = HOP // 2
QK = C + POINTS
BUCKET = ROWS
FTILE = NTILE + EXPERTS
TABLE = EXPERTS * BUCKET + P * P // 2
CW = C + 2
EW = CC * C


def point_rows(head):
    return HD * (1 - head % 2)


def constants():
    k = np.arange(HOP)[:, None].astype(np.float64)
    n = np.arange(HOP)[None, :].astype(np.float64)
    basis = np.cos(np.pi * (2.0 * n + 1.0) * k / (2.0 * HOP))
    scale = np.full((HOP, 1), np.sqrt(2.0 / HOP))
    scale[0, 0] = np.sqrt(1.0 / HOP)
    basis = (scale * basis).astype(np.float32)
    dct = np.stack([basis[0::2, :HALF].T, basis[1::2, :HALF].T], axis=1)
    dct = dct.reshape(HALF // P, P, 2, HALF).transpose(1, 2, 0, 3)
    f = np.arange(P)
    cols = {}
    cols["ident"] = np.eye(P)
    cols["before"] = f[:, None] < f[None, :]
    cols["head_of"] = (f[:, None] == np.arange(POINTS)[None, :] // POINT)
    cols["bins"] = np.tile(np.array(BINS), (P, 1))
    cols["bucket"] = np.tile(np.arange(EXPERTS) * BUCKET, (P, 1))
    cols["tile128"] = np.tile(np.arange(NTILE) * P, (P, 1))
    cols["partition"] = f[:, None]
    cols["lower"] = np.tile(np.tril(np.ones((EXPERTS, EXPERTS)), -1).reshape(-1), (P, 1))
    cols["rows"] = f[:, None] + P * np.arange(T)[None, :]
    at, place = 0, {}
    for name, a in cols.items():
        place[name] = (at, at + a.shape[1])
        at += a.shape[1]
    small = np.concatenate([a.astype(np.float32) for a in cols.values()], axis=1)
    return np.ascontiguousarray(dct), np.ascontiguousarray(small), place


def audio_tower(nc, x, ln_g, ln_b, wq, bq, wk, bk, wv, bv, wqp, bqp, wkp, bkp, wo, bo, pscale, w_ffn,
                dct_in, small_in, place, out):
    f32, f32r, bf16, u32, i32 = (mybir.dt.float32, mybir.dt.float32r, mybir.dt.bfloat16,
                                 mybir.dt.uint32, mybir.dt.int32)
    ALU, ACT, XA = mybir.AluOpType, mybir.ActivationFunctionType, mybir.AxisListType.X

    x_flat = x.rearrange("b n -> (b n)")
    out_rows = out.rearrange("b f c -> (b f) c")
    h1_dram = nc.dram_tensor("h1_rows", (ROWS + 1, CW), f32, kind="Internal").ap()
    table = nc.dram_tensor("row_table", (TABLE, 1), f32, kind="Internal").ap()

    ctx = ExitStack()
    with ctx:
        def sb(name, shape, dt, where=ctx):
            return where.enter_context(nc.sbuf_tensor(name, shape, dt))

        def sem(name):
            return ctx.enter_context(nc.semaphore(name))

        tr = [ctx.enter_context(nc.psum_tensor(f"transposed{k}", [P, 512], f32)) for k in range(2)]
        ro = [ctx.enter_context(nc.psum_tensor(f"row_out{k}", [P, 512], f32)) for k in range(2)]
        qk = [ctx.enter_context(nc.psum_tensor(f"qk_out{k}", [P, 512], f32)) for k in range(2)]
        sc = [ctx.enter_context(nc.psum_tensor(f"scores{k}", [P, 2, HEADS, FRAMES], f32))
              for k in range(2)]

        small = sb("small", list(small_in.shape), f32)

        def const(name):
            a, b = place[name]
            return small[:, a:b]

        ident = const("ident")
        before_b = sb("before_bf16", [P, P], bf16)
        ones_b = sb("ones_bf16", [P, P], bf16)
        minus_half = sb("minus_half", [P, T], f32)
        onehot = sb("onehot", [P, T, EXPERTS], bf16)
        so_far = sb("so_far", [P, EXPERTS], bf16)
        block_sum = sb("block_sum", [P, EXPERTS], f32)
        above = sb("above", [P, T, EXPERTS + 1], f32)
        row_id = sb("row_id", [P, T], f32)

        part1 = ctx.enter_context(ExitStack())
        wqk_h = sb("wqk_high", [P, 2, CC, QK], f32r, part1)
        wqk_l = sb("wqk_low", [P, 2, CC, QK], f32r, part1)
        wv_h = sb("wv_high", [P, CC, C], f32r, part1)
        wv_l = sb("wv_low", [P, CC, C], f32r, part1)
        wo_h = sb("wo_high", [P, CC, C], f32r, part1)
        wo_l = sb("wo_low", [P, CC, C], f32r, part1)
        dct_h = sb("dct_high", [P, 2, 2, HALF], f32r, part1)
        dct_l = sb("dct_low", [P, 2, 2, HALF], f32r, part1)
        out_bias = sb("out_bias", [P, C], f32, part1)
        bias_s = sb("bias_scalar", [P, 2 * PAIRS], f32, part1)
        bias_p = sb("bias_points", [P, 2], f32, part1)
        bias_dot = sb("bias_query_points", [P, 1], f32, part1)
        ps2 = sb("two_pscale", [P, 1], f32, part1)
        xs = sb("samples", [P, T, HOP], f32, part1)
        fold = sb("folded_tiles", [P, 2, 2, HALF], f32, part1)
        xt_h = sb("frames_t_high", [P, 2, 4, P], f32r, part1)
        xt_l = sb("frames_t_low", [P, 2, 4, P], f32r, part1)
        h = sb("h", [P, T, C], f32, part1)
        z = sb("z", [P, T, C], f32, part1)
        zt_h = sb("z_t_high", [P, CC, BLOCK], f32r, part1)
        zt_l = sb("z_t_low", [P, CC, BLOCK], f32r, part1)
        hb = sb("h_plus_bias", [P, T, C], f32, part1)
        v = sb("v", [P, T, C], f32, part1)
        stat = sb("stat", [P, T, 6], f32, part1)
        mv = sb("mean_var", [P, T, 2], f32, part1)
        var_e = sb("var_eps", [P, T], f32, part1)
        rs = sb("z_scale", [P, T], f32, part1)
        mx = sb("score_max", [P, 2, HEADS], f32, part1)
        sm = sb("prob_sum", [P, 2, HEADS], f32, part1)
        rc = sb("prob_scale", [P, 2, HEADS], f32, part1)
        stat1 = sb("stat1", [P, T, 6], f32, part1)
        var1 = sb("var_eps1", [P, T], f32, part1)
        y0 = sb("channel0", [P, T], f32, part1)
        slot_b = sb("slot_by_expert", [P, T, EXPERTS], f32, part1)
        slot_m = sb("slot_masked", [P, T, EXPERTS], f32, part1)
        slot_f = sb("slot", [P, T], f32, part1)
        slot = sb("slot_index", [P, T], u32, part1)

        setup = ExitStack()
        with setup:
            raw_s = sb("raw_wq_wk", [P, 2, CC, C], f32, setup)
            raw_p = sb("raw_wqp_wkp", [P, 2, CC, POINTS], f32, setup)
            raw_v = sb("raw_wv", [P, CC, C], f32, setup)
            raw_o = sb("raw_wo", [P, CC, C], f32, setup)
            raw_d = sb("raw_dct", [P, 2, 2, HALF], f32, setup)
            gain = sb("ln_gain", [P, CC], f32, setup)
            gain_q = sb("ln_gain_q", [P, CC], f32, setup)
            shift_c = sb("ln_shift", [P, CC], f32, setup)
            raw_bs = sb("raw_bias_scalar", [P, 2 * PAIRS], f32, setup)
            raw_bp = sb("raw_bias_points", [P, 2], f32, setup)
            raw_bv = sb("raw_bias_v", [P, CC], f32, setup)
            ps_c = sb("pscale_column", [HEADS, 1], f32, setup)
            ps_b = sb("pscale_b", [P, HEADS], f32, setup)
            neg_ps = sb("minus_pscale", [P, HEADS], f32, setup)
            bo_b = sb("bo_b", [P, C], f32, setup)
            v_bias = sb("v_bias", [P, CC], f32, setup)
            v_bias_b = sb("v_bias_b", [P, CC, P], f32, setup)
            sentinel = sb("sentinel", [P, TABLE // P], f32, setup)
            zero_row = sb("zero_row", [1, CW], f32, setup)

        qf = sb("q_features", [P, HEADS, BLOCK], f32, part1)
        kf = sb("k_features", [P, HEADS, BLOCK], f32, part1)
        prob = sb("prob", [P, 2, HEADS, FRAMES], f32, part1)
        prob_t = sb("prob_t", [P, 2, HEADS, P], f32, part1)
        ot_h = sb("attended_t_high", [P, 2, CC, P], f32r, part1)
        ot_l = sb("attended_t_low", [P, 2, CC, P], f32r, part1)
        h1 = sb("h1", [P, 2, CW], f32, part1)
        part1.close()

        we_raw = sb("w_ffn_raw", [P, 2, EW], f32)
        we = sb("w_ffn_halves", [P, EXPERTS * 2 * EW], f32r)
        counts = sb("counts", [P, EXPERTS], f32)
        exceeds = sb("exceeds", [P, EXPERTS, NTILE], f32)
        tiles_of = sb("tiles_of", [P, EXPERTS], f32)
        lower_m = sb("lower_masked", [P, EXPERTS, EXPERTS], f32)
        first_of = sb("first_tile_of", [P, EXPERTS], f32)
        started = sb("started", [P, EXPERTS], f32)
        skipped = sb("skipped", [P, EXPERTS - 1], f32)
        expert_of = sb("expert_of", [P, 1], f32)
        start_of = sb("start_of", [P, 1], f32)
        in_bucket = sb("in_bucket", [P, 1], f32)
        table_f = sb("table_row_f", [P, 1], f32)
        table_r = sb("table_row", [P, 1], u32)
        picked = sb("picked", [P, P], f32)
        index = sb("index", [P, FTILE], u32)
        index_in = sb("index_in", [P, 8], u32)
        index_out = sb("index_out", [P, 4], u32)
        expert_row = sb("expert_row", [1, FTILE], i32)
        g = sb("gathered", [P, 8, CW], f32)
        z2 = sb("z2", [P, 2, C], f32)
        z2t_h = sb("z2_t_high", [P, 2, CC, P], f32r)
        z2t_l = sb("z2_t_low", [P, 2, CC, P], f32r)
        res = sb("result", [P, 4, C], f32)

        small_in_s, dct_in_s, w_in_s, bias_in_s = (sem("small_in"), sem("dct_in"), sem("w_in"),
                                                   sem("bias_in"))
        pool_consts, consts_made, split_high, split_low = (sem("pool_consts"), sem("consts_made"),
                                                           sem("split_high"), sem("split_low"))
        gain_made, bias_step, bias_mm, vb_ready, ob_mm, bias_done = (
            sem("gain_made"), sem("bias_step"), sem("bias_mm"), sem("vb_ready"), sem("ob_mm"),
            sem("bias_done"))
        table_cleared, prob_t_zero, xs_zero = sem("table_cleared"), sem("prob_t_zero"), sem("xs_zero")
        rows_zero, fixed_src, fixed_rows = sem("rows_zero"), sem("fixed_src"), sem("fixed_rows")
        x_loaded, folded, frames_t = sem("x_loaded"), sem("folded"), sem("frames_t")
        xt_high, xt_low, dct_mm, h_ready = sem("xt_high"), sem("xt_low"), sem("dct_mm"), sem("h_ready")
        stat_d, aggr_d, var_p, scale_p = sem("stat_d"), sem("aggr_d"), sem("var_p"), sem("scale_p")
        z_ready, z_t, zt_high, zt_low = sem("z_ready"), sem("z_t"), sem("zt_high"), sem("zt_low")
        q_mm, k_mm, q_ev, k_ev = sem("q_mm"), sem("k_mm"), sem("q_ev"), sem("k_ev")
        points_in = [sem(f"points_in{m}") for m in range(PAIRS)]
        scored = sem("scored")
        v_mm, v_ev = sem("v_mm"), sem("v_ev")
        max_d, shifted, exped, summed = sem("max_d"), sem("shifted"), sem("exped"), sem("summed")
        inverted, normed, probs_t = sem("inverted"), sem("normed"), sem("probs_t")
        pv_mm, ot_high, ot_low, wo_mm = sem("pv_mm"), sem("ot_high"), sem("ot_low"), sem("wo_mm")
        h1_ready, hb_ready = sem("h1_ready"), sem("hb_ready")
        h1_stored = [sem("h1_stored0"), sem("h1_stored1")]
        stat1_d, aggr1_d, var1_p, scale1_p = (sem("stat1_d"), sem("aggr1_d"), sem("var1_p"),
                                              sem("scale1_p"))
        y0_d, above_d, onehot_d, block_sum_d, so_far_d = (
            sem("y0_d"), sem("above_d"), sem("onehot_d"), sem("block_sum_d"), sem("so_far_d"))
        rank_mm, slot_b_d, slot_m_d, slot_f_d, slot_d = (sem("rank_mm"), sem("slot_b_d"),
                                                         sem("slot_m_d"), sem("slot_f_d"),
                                                         sem("slot_d"))
        scattered, ids_next = sem("scattered"), sem("ids_next")
        count_mm, plan_d, plan_s, table_in, picked_t, plan_t, index_d = (
            sem("count_mm"), sem("plan_d"), sem("plan_s"), sem("table_in"), sem("picked_t"),
            sem("plan_t"), sem("index_d"))
        we_in = [sem("we_in0"), sem("we_in1")]
        we_high, we_low = sem("we_high"), sem("we_low")
        index_in_p, index_out_p = sem("index_in_p"), sem("index_out_p")
        g_in = [sem(f"g_in{k}") for k in range(8)]
        z2_ready, z2_t, z2t_high, z2t_low, ffn_mm, res_ready = (
            sem("z2_ready"), sem("z2_t"), sem("z2t_high"), sem("z2t_low"), sem("ffn_mm"),
            sem("res_ready"))
        res_out = [sem(f"res_out{k}") for k in range(4)]

        block = ctx.enter_context(nc.Block())
        XD = 5 * 16
        PD = 2 * 4 * 16
        FEATURES = 1 + PAIRS
        GROUPS = FTILE // 8

        @block.sync
        def _(sp):
            sp.dma_start(small[:, :], small_in).then_inc(small_in_s, 16)
            sp.dma_start(raw_d[:, :, :, :], dct_in).then_inc(dct_in_s, 16)

            def load_samples(a, first):
                src = x_flat[bass.ds(a * (BLOCK // FRAMES * SAMPLES), BLOCK // FRAMES * SAMPLES)]\
                    .rearrange("(t c n) -> c t n", c=CLIPS, n=SAMPLES)
                if not first:
                    sp.wait_ge(folded, 2 * T * a)
                for c in range(CLIPS):
                    full = src[c, :, 0:(FRAMES - 1) * HOP].rearrange("t (f n) -> f t n", n=HOP)
                    sp.dma_start(xs[32 * c:32 * c + FRAMES - 1, :, :], full).then_inc(x_loaded, 16)
                tails = src[:, :, (FRAMES - 1) * HOP:SAMPLES]
                sp.dma_start(xs[FRAMES - 1:P:FRAMES, :, 0:TAIL], tails).then_inc(x_loaded, 16)

            sp.wait_ge(xs_zero, 1)
            load_samples(0, True)
            for n, w in enumerate((wq, wk)):
                sp.dma_start(raw_s[:, n, :, :], w.rearrange("(c p) n -> p c n", p=P)).then_inc(w_in_s, 16)
            for n, w in enumerate((wqp, wkp)):
                sp.dma_start(raw_p[:, n, :, :], w.rearrange("(c p) n -> p c n", p=P)).then_inc(w_in_s, 16)
            sp.dma_start(raw_v[:, :, :], wv.rearrange("(c p) n -> p c n", p=P)).then_inc(w_in_s, 16)
            sp.dma_start(raw_o[:, :, :], wo.rearrange("(c p) n -> p c n", p=P)).then_inc(w_in_s, 16)
            sp.wait_ge(pool_consts, 2)
            sp.dma_start(table.rearrange("(p n) a -> p (n a)", p=P), sentinel[:, :]).then_inc(table_cleared, 16)
            sp.dma_start(h1_dram[ROWS:ROWS + 1, :], zero_row[:, :]).then_inc(table_cleared, 16)
            sp.wait_ge(rows_zero, 4)
            sp.wait_ge(fixed_src, 2)
            for hd in range(HEADS):
                src = (hb, v)[hd % 2][0:POINT, hd // 2, :]
                at = point_rows(hd)
                sp.dma_start(qf[at + 2 * POINT:at + 3 * POINT, hd, :], src).then_inc(fixed_rows, 16)
                sp.dma_start(kf[at + POINT:at + 2 * POINT, hd, :], src).then_inc(fixed_rows, 16)
            load_samples(1, False)

            def points(i):
                sp.wait_ge(q_ev, (2 * FEATURES) * i + 2)
                sp.wait_ge(k_ev, (2 * FEATURES) * i + 2)
                for hd in range(HEADS):
                    at = point_rows(hd)
                    for f, square, j in ((qf, POINT, 0), (kf, 2 * POINT, 2)):
                        rows = slice(POINT * hd, POINT * (hd + 1))
                        sp.dma_start(f[at:at + POINT, hd, :], v[rows, j, :]).then_inc(points_in[hd // 2], 16)
                        sp.dma_start(f[at + square:at + square + POINT, hd, :], v[rows, j + 1, :])\
                            .then_inc(points_in[hd // 2], 16)

            def body(i, load):
                points(i)
                if load:
                    load_samples(i + 2, False)
                for t in range(T):
                    sp.wait_ge(scale1_p, i * T + t + 1)
                    sp.dma_start(h1_dram[bass.ds(i * BLOCK + t * P, P), :], h1[:, t % 2, :])\
                        .then_inc(h1_stored[t % 2], 16)

            with sp.Fori(0, NBLOCK - 2) as i:
                body(i, True)
            body(NBLOCK - 2, False)
            points(NBLOCK - 1)
            sp.wait_ge(v_mm, T * NBLOCK)

            def load_expert(e):
                sp.dma_start(we_raw[:, e % 2, :].rearrange("p (c n) -> p c n", c=CC),
                             w_ffn[e, :, :].rearrange("(c p) n -> p c n", p=P)).then_inc(we_in[e % 2], 16)

            load_expert(0)
            load_expert(1)
            for t in range(T):
                sp.wait_ge(scale1_p, (NBLOCK - 1) * T + t + 1)
                sp.dma_start(h1_dram[bass.ds((NBLOCK - 1) * BLOCK + t * P, P), :], h1[:, t % 2, :])\
                    .then_inc(h1_stored[t % 2], 16)
            for e in range(2, EXPERTS):
                sp.wait_ge(we_low, e - 1)
                load_expert(e)
            for k in range(2):
                sp.wait_ge(h1_stored[k], 16 * NTILE // 2)

        @block.gpsimd
        def _(pool):
            pool.memset(xs[:, :, :], 0.0).then_inc(xs_zero, 1)
            pool.memset(sentinel[:, :], float(ROWS)).then_inc(pool_consts, 1)
            pool.memset(zero_row[:, :], 0.0).then_inc(pool_consts, 1)
            pool.memset(minus_half[:, :], -0.5).then_inc(pool_consts, 1)
            for dst, src in ((gain, ln_g), (shift_c, ln_b), (raw_bv, bv),
                             (raw_bs[:, 0:PAIRS], bq), (raw_bs[:, PAIRS:2 * PAIRS], bk)):
                pool.dma_start(dst[:, :], src.rearrange("(c p) -> p c", p=P),
                               allow_slow_non_contiguous=True).then_inc(bias_in_s, 16)
            for n, src in enumerate((bqp, bkp)):
                pool.dma_start(raw_bp[0:POINTS, n:n + 1], src.rearrange("(p a) -> p a", a=1),
                               allow_slow_non_contiguous=True).then_inc(bias_in_s, 16)
            pool.dma_start(ps_c[:, :], pscale.rearrange("(p a) -> p a", a=1),
                           allow_slow_non_contiguous=True).then_inc(bias_in_s, 16)
            pool.dma_start(ps_b[:, :], pscale.rearrange("(a h) -> a h", a=1).to_broadcast([P, HEADS]))\
                .then_inc(bias_in_s, 16)
            pool.dma_start(bo_b[:, :], bo.rearrange("(a h) -> a h", a=1).to_broadcast([P, C]))\
                .then_inc(bias_in_s, 16)
            pool.dma_start(row_id[:, :], small_in[:, place["rows"][0]:place["rows"][1]])\
                .then_inc(bias_in_s, 16)

            def fold_tile(a, t, first):
                if t == 0:
                    pool.wait_ge(x_loaded, XD * (a + 1))
                if t >= 2 or not first:
                    pool.wait_ge(frames_t, a * T + t - 1)
                back = xs[:, t, HOP - 1:HALF - 1:-1]
                pool.tensor_tensor(fold[:, t % 2, 0, :], xs[:, t, 0:HALF], back, ALU.add).then_inc(folded, 1)
                pool.tensor_tensor(fold[:, t % 2, 1, :], xs[:, t, 0:HALF], back, ALU.subtract)\
                    .then_inc(folded, 1)

            def z_scale(a):
                pool.wait_ge(aggr_d, T * (a + 1))
                pool.nop(nofuse=True)
                pool.tensor_scalar(var_e[:, :], mv[:, :, 1], 1.0 + EPS, EPS * EPS, ALU.mult, ALU.add)\
                    .then_inc(var_p, 1)
                pool.wait_ge(var_p, a + 1)
                pool.tensor_tensor(rs[:, :], var_e[:, :], minus_half[:, :], ALU.pow).then_inc(scale_p, 1)

            for t in range(T):
                fold_tile(0, t, True)
            z_scale(0)
            pool.wait_ge(split_high, 2 + 5 * CC)
            pool.wait_ge(split_low, 2 + 5 * CC)
            pool.wait_ge(bias_done, 2)
            pool.wait_ge(table_cleared, 32)
            for f in (qf, kf):
                for parity in range(2):
                    pad = point_rows(parity) + 32
                    pool.memset(f[pad:pad + 32, parity::2, :], 0.0).then_inc(rows_zero, 1)
            pool.wait_ge(rows_zero, 4)
            pool.memset(prob_t[:, :, :, :], 0.0).then_inc(prob_t_zero, 1)

            def add_bias(a, first):
                for t in range(T):
                    pool.wait_ge(h_ready, a * T + t + 1)
                    if not first:
                        pool.wait_ge(h1_ready, (a - 1) * T + t + 1)
                    elif t == 0:
                        pool.wait_ge(fixed_rows, 2 * HEADS * 16)
                    pool.tensor_tensor(hb[:, t, :], h[:, t, :], out_bias[:, :], ALU.add)\
                        .then_inc(hb_ready, 1)

            def scatter_ids(i, first):
                if not first:
                    pool.wait_ge(scattered, 16 * T * i)
                    pool.nop(nofuse=True)
                    pool.tensor_scalar(row_id[:, :], row_id[:, :], 1.0, float(BLOCK), ALU.mult, ALU.add)\
                        .then_inc(ids_next, 1)
                    pool.wait_ge(ids_next, i)
                pool.wait_ge(slot_d, i + 1)
                pool.nop(nofuse=True)
                for t in range(T):
                    pool.indirect_dma_start(
                        out=table, out_offset=bass.IndirectOffsetOnAxis(ap=slot[:, t:t + 1], axis=0),
                        in_=row_id[:, t:t + 1], in_offset=None).then_inc(scattered, 16)

            def body(i, nxt, first, second):
                if nxt:
                    fold_tile(i + 1, 0, False)
                    fold_tile(i + 1, 1, False)
                add_bias(i, first)
                if nxt:
                    fold_tile(i + 1, 2, False)
                    fold_tile(i + 1, 3, False)
                if not first:
                    scatter_ids(i - 1, second)
                if nxt:
                    z_scale(i + 1)
                for t in range(T):
                    pool.wait_ge(inverted, i * T + t + 1)
                    pr = prob[:, t % 2, :, :]
                    pool.tensor_tensor(pr, pr, rc[:, t % 2, :].unsqueeze(2).to_broadcast([P, HEADS, FRAMES]),
                                       ALU.mult).then_inc(normed, 1)
                for t in range(T):
                    pool.wait_ge(aggr1_d, i * T + t + 1)
                    pool.nop(nofuse=True)
                    pool.tensor_scalar(var1[:, t:t + 1], h1[:, t % 2, C + 1:C + 2], 1.0, EPS,
                                       ALU.mult, ALU.add).then_inc(var1_p, 1)
                    pool.wait_ge(var1_p, i * T + t + 1)
                    pool.tensor_tensor(h1[:, t % 2, C + 1:C + 2], var1[:, t:t + 1], minus_half[:, 0:1],
                                       ALU.pow).then_inc(scale1_p, 1)

            body(0, True, True, False)
            body(1, True, False, True)
            with pool.Fori(2, NBLOCK - 1) as i:
                body(i, True, False, False)
            body(NBLOCK - 1, False, False, False)
            scatter_ids(NBLOCK - 1, False)

            pool.wait_ge(plan_d, 8)
            pool.wait_ge(scattered, 16 * T * NBLOCK)
            pool.indirect_dma_start(
                out=picked[0:FTILE, :], out_offset=None, in_=table.rearrange("(r n) a -> r (n a)", n=P),
                in_offset=bass.IndirectOffsetOnAxis(ap=table_r[0:FTILE, :], axis=0)).then_inc(table_in, 16)
            pool.wait_ge(index_d, 2)
            for k in range(2):
                pool.wait_ge(h1_stored[k], 16 * NTILE // 2)

            def gather(u, k):
                pool.tensor_copy(index_in[:, k:k + 1], index[:, bass.ds(u, 1)]).then_inc(index_in_p, 1)
                pool.wait_ge(index_in_p, u + 1)
                pool.nop(nofuse=True)
                pool.indirect_dma_start(
                    out=g[:, k, :], out_offset=None, in_=h1_dram,
                    in_offset=bass.IndirectOffsetOnAxis(ap=index_in[:, k:k + 1], axis=0))\
                    .then_inc(g_in[k], 16)

            def store(u, w, k):
                n = 2 * w + k // 4
                if not (isinstance(n, int) and n == 0):
                    pool.wait_ge(res_out[k % 4], 16 * n)
                    pool.nop(nofuse=True)
                pool.tensor_copy(index_out[:, k % 4:k % 4 + 1], index[:, bass.ds(u, 1)])\
                    .then_inc(index_out_p, 1)
                pool.wait_ge(index_out_p, u + 1)
                pool.nop(nofuse=True)
                pool.wait_ge(res_ready, u + 1)
                pool.nop(nofuse=True)
                pool.indirect_dma_start(
                    out=out_rows, out_offset=bass.IndirectOffsetOnAxis(ap=index_out[:, k % 4:k % 4 + 1], axis=0),
                    in_=res[:, k % 4, :], in_offset=None, bounds_check=ROWS - 1, oob_is_err=False)\
                    .then_inc(res_out[k % 4], 16)

            for k in range(4):
                gather(k, k)

            def group(w, last):
                for k in range(8):
                    if k < 4 or not last:
                        gather(8 * w + k + 4, (k + 4) % 8)
                    store(8 * w + k, w, k)

            group(0, False)
            with pool.Fori(1, GROUPS - 1) as w:
                group(w, False)
            group(GROUPS - 1, True)
            for k in range(4):
                pool.wait_ge(res_out[k], 16 * FTILE // 4)

        @block.scalar
        def _(act):
            act.wait_ge(dct_in_s, 16)
            act.activation(dct_h[:, :, :, :], raw_d[:, :, :, :], ACT.Copy).then_inc(split_high, 1)

            def frames_high(a, t, first):
                act.wait_ge(frames_t, a * T + t + 1)
                if t >= 2 or not first:
                    act.wait_ge(dct_mm, a * T + t - 1)
                act.activation(xt_h[:, t % 2, :, :], tr[t % 2][:, :], ACT.Copy).then_inc(xt_high, 1)

            def h_out(a, t, first):
                act.wait_ge(dct_mm, a * T + t + 1)
                if t == 0 and not first:
                    act.wait_ge(hb_ready, T * a)
                    act.wait_ge(z_ready, T * a)
                act.activation(h[:, t, :].rearrange("p (m two) -> p two m", two=2),
                               ro[t % 2][:, :].rearrange("p (two m) -> p two m", two=2), ACT.Copy)\
                    .then_inc(h_ready, 1)

            def z_high(a, cc, first):
                act.wait_ge(z_t, a * CC + cc + 1)
                if cc == 0 and not first:
                    act.wait_ge(v_mm, a * T)
                act.activation(zt_h[:, cc, :], qk[cc % 2][:, :], ACT.Copy).then_inc(zt_high, 1)

            for t in range(T):
                frames_high(0, t, True)
                h_out(0, t, True)
            act.wait_ge(w_in_s, 6 * 16)
            act.wait_ge(gain_made, 1)
            for cc in range(CC):
                for n, by in ((0, gain_q), (1, gain)):
                    act.activation(wqk_h[:, n, cc, 0:C], raw_s[:, n, cc, :], ACT.Identity,
                                   scale=by[:, cc:cc + 1]).then_inc(split_high, 1)
                    act.activation(wqk_h[:, n, cc, C:QK], raw_p[:, n, cc, :], ACT.Identity,
                                   scale=gain[:, cc:cc + 1]).then_inc(split_high, 1)
                act.activation(wv_h[:, cc, :], raw_v[:, cc, :], ACT.Identity,
                               scale=gain[:, cc:cc + 1]).then_inc(split_high, 1)
            act.activation(wo_h[:, :, :], raw_o[:, :, :], ACT.Copy).then_inc(split_high, 1)
            for cc in range(CC):
                z_high(0, cc, True)

            def point_features(i, side, first):
                act.wait_ge((q_mm, k_mm)[side], FEATURES * i + 1)
                if side == 0 and first:
                    act.wait_ge(fixed_rows, 2 * HEADS * 16)
                    act.wait_ge(bias_done, 2)
                src, dst, ev = qk[side], v[:, 2 * side:2 * side + 2, :], (q_ev, k_ev)[side]
                if side == 0:
                    act.activation(dst[0:POINTS, 0, :], src[0:POINTS, :], ACT.Identity,
                                   scale=ps2[0:POINTS, :], bias=bias_dot[0:POINTS, :]).then_inc(ev, 1)
                else:
                    act.activation(dst[0:POINTS, 0, :], src[0:POINTS, :], ACT.Identity,
                                   bias=bias_p[0:POINTS, 1:2]).then_inc(ev, 1)
                act.activation(dst[0:POINTS, 1, :], src[0:POINTS, :], ACT.Square,
                               bias=bias_p[0:POINTS, side:side + 1]).then_inc(ev, 1)

            def pair_features(i, m, side):
                act.wait_ge((q_mm, k_mm)[side], FEATURES * i + m + 2)
                if m == 0 and not (isinstance(i, int) and i == 0):
                    act.wait_ge(scored, PAIRS * i)
                f, ev = (qf, kf)[side], (q_ev, k_ev)[side]
                for j in range(2):
                    rows = slice(HD * j, HD * (j + 1))
                    act.activation(f[rows, 2 * m + j, :], qk[side][rows, :], ACT.Identity,
                                   bias=bias_s[rows, side * PAIRS + m:side * PAIRS + m + 1]).then_inc(ev, 1)

            def body(i, nxt, first):
                point_features(i, 0, first)
                point_features(i, 1, first)
                if nxt:
                    frames_high(i + 1, 0, False)
                pair_features(i, 0, 0)
                if nxt:
                    frames_high(i + 1, 1, False)
                pair_features(i, 0, 1)
                if nxt:
                    h_out(i + 1, 0, False)
                for m in range(1, PAIRS):
                    pair_features(i, m, 0)
                    if nxt and m + 1 < T:
                        frames_high(i + 1, m + 1, False)
                    if nxt and m == PAIRS - 1:
                        h_out(i + 1, T - 1, False)
                    pair_features(i, m, 1)
                    if nxt and m < PAIRS - 1:
                        h_out(i + 1, m, False)
                for t in range(T):
                    act.wait_ge(v_mm, i * T + t + 1)
                    if t == 0:
                        for m in range(PAIRS):
                            act.wait_ge(points_in[m], PD * (i + 1))
                    act.activation(v[:, t, :], ro[t % 2][:, :], ACT.Copy).then_inc(v_ev, 1)
                    act.wait_ge(shifted, i * T + t + 1)
                    act.activation(prob[:, t % 2, :, :], prob[:, t % 2, :, :], ACT.Exp).then_inc(exped, 1)
                for t in range(T):
                    if nxt and t % 2 == 0:
                        z_high(i + 1, t, False)
                        z_high(i + 1, t + 1, False)
                    act.wait_ge(pv_mm, i * T + t + 1)
                    if t >= 2 or not first:
                        act.wait_ge(wo_mm, i * T + t - 1)
                    act.activation(ot_h[:, t % 2, :, :], tr[t % 2][:, :], ACT.Copy).then_inc(ot_high, 1)

            body(0, True, True)
            with act.Fori(1, NBLOCK - 1) as i:
                body(i, True, False)
            body(NBLOCK - 1, False, False)

            for e in range(EXPERTS):
                act.wait_ge(we_in[e % 2], 16 * (e // 2 + 1))
                if e == 2:
                    act.wait_ge(plan_d, 1)
                at = e * 2 * EW
                act.activation(we[:, at:at + EW], we_raw[:, e % 2, :], ACT.Copy).then_inc(we_high, 1)

            def ffn_high(u, k, first):
                act.wait_ge(z2_t, u + 1)
                if not first:
                    act.wait_ge(ffn_mm, u - 1)
                act.activation(z2t_h[:, k, :, :], tr[k][:, :], ACT.Copy).then_inc(z2t_high, 1)

            ffn_high(0, 0, True)
            ffn_high(1, 1, True)
            with act.Fori(1, FTILE // 2) as w:
                for k in range(2):
                    ffn_high(2 * w + k, k, False)

        @block.vector
        def _(dve):
            dve.memset(ones_b[:, :], 1.0).then_inc(consts_made, 1)
            dve.memset(so_far[:, :], 0.0).then_inc(consts_made, 1)
            dve.memset(above[:, :, 0:1], 1.0).then_inc(consts_made, 1)
            dve.memset(above[:, :, EXPERTS:EXPERTS + 1], 0.0).then_inc(consts_made, 1)
            dve.wait_ge(small_in_s, 16)
            dve.tensor_copy(before_b[:, :], const("before")).then_inc(consts_made, 1)
            dve.wait_ge(split_high, 1)
            dve.tensor_tensor(dct_l[:, :, :, :], raw_d[:, :, :, :], dct_h[:, :, :, :], ALU.subtract)\
                .then_inc(split_low, 1)

            def frames_low(a, t):
                dve.wait_ge(xt_high, a * T + t + 1)
                dve.tensor_tensor(xt_l[:, t % 2, :, :], tr[t % 2][:, :].rearrange("p (c r) -> p c r", c=4),
                                  xt_h[:, t % 2, :, :], ALU.subtract).then_inc(xt_low, 1)

            def h_stats(a, t, first):
                dve.wait_ge(h_ready, a * T + t + 1)
                if t == 0 and not first:
                    dve.wait_ge(z_ready, T * a)
                dve.bn_stats(stat[:, t, :], h[:, t, :]).then_inc(stat_d, 1)
                dve.wait_ge(stat_d, a * T + t + 1)
                dve.nop(nofuse=True)
                dve.bn_aggr(mv[:, t, :], stat[:, t, :]).then_inc(aggr_d, 1)

            def z_tiles(a, first):
                dve.wait_ge(scale_p, a + 1)
                if not first:
                    dve.wait_ge(z_t, CC * a)
                for t in range(T):
                    dve.tensor_scalar(z[:, t, :], h[:, t, :], mv[:, t, 0:1], rs[:, t:t + 1],
                                      ALU.subtract, ALU.mult).then_inc(z_ready, 1)

            def z_low(a, cc):
                dve.wait_ge(zt_high, a * CC + cc + 1)
                dve.tensor_tensor(zt_l[:, cc, :], qk[cc % 2][:, :], zt_h[:, cc, :], ALU.subtract)\
                    .then_inc(zt_low, 1)

            dve.wait_ge(bias_in_s, 11 * 16)
            dve.tensor_scalar(gain_q[:, :], gain[:, :], HD ** -0.5, None, ALU.mult).then_inc(gain_made, 1)
            for t in range(T):
                frames_low(0, t)
                h_stats(0, t, True)
            z_tiles(0, True)

            dve.wait_ge(bias_mm, 1)
            dve.tensor_scalar(ps2[0:POINTS, :], qk[0][0:POINTS, 16:17], 2.0, None, ALU.mult).then_inc(bias_step, 1)
            dve.tensor_tensor(bias_s[:, :], raw_bs[:, :], qk[0][:, 0:2 * PAIRS], ALU.add).then_inc(bias_step, 1)
            dve.tensor_tensor(bias_p[0:POINTS, :], raw_bp[0:POINTS, :], qk[0][0:POINTS, 8:10], ALU.add)\
                .then_inc(bias_step, 1)
            dve.tensor_tensor(v_bias[:, :], raw_bv[:, :], qk[0][:, 12:12 + CC], ALU.add).then_inc(bias_step, 1)
            dve.tensor_scalar(neg_ps[:, :], ps_b[:, :], -1.0, None, ALU.mult).then_inc(bias_step, 1)
            dve.wait_ge(bias_step, 5)
            dve.tensor_copy(v_bias_b[:, :, :], v_bias[:, :].unsqueeze(2).to_broadcast([P, CC, P]))\
                .then_inc(vb_ready, 1)
            dve.tensor_scalar(bias_s[:, 0:PAIRS], bias_s[:, 0:PAIRS], HD ** -0.5, None, ALU.mult)\
                .then_inc(bias_step, 1)
            dve.tensor_tensor(bias_dot[0:POINTS, :], bias_p[0:POINTS, 0:1], ps2[0:POINTS, :], ALU.mult)\
                .then_inc(bias_step, 1)
            for parity, dst in enumerate((hb, v)):
                dve.tensor_copy(dst[0:POINT, :, :],
                                neg_ps[0:POINT, parity::2].unsqueeze(2).to_broadcast([POINT, T, C]))\
                    .then_inc(fixed_src, 1)
            for cc in range(CC):
                for n, by in ((0, gain_q), (1, gain)):
                    dve.wait_ge(split_high, 1 + 5 * cc + 2 * n + 2)
                    dve.scalar_tensor_tensor(out=wqk_l[:, n, cc, 0:C], in0=raw_s[:, n, cc, :],
                                             scalar=by[:, cc:cc + 1], in1=wqk_h[:, n, cc, 0:C],
                                             op0=ALU.mult, op1=ALU.subtract).then_inc(split_low, 1)
                    dve.scalar_tensor_tensor(out=wqk_l[:, n, cc, C:QK], in0=raw_p[:, n, cc, :],
                                             scalar=gain[:, cc:cc + 1], in1=wqk_h[:, n, cc, C:QK],
                                             op0=ALU.mult, op1=ALU.subtract).then_inc(split_low, 1)
                dve.wait_ge(split_high, 1 + 5 * (cc + 1))
                dve.scalar_tensor_tensor(out=wv_l[:, cc, :], in0=raw_v[:, cc, :], scalar=gain[:, cc:cc + 1],
                                         in1=wv_h[:, cc, :], op0=ALU.mult, op1=ALU.subtract)\
                    .then_inc(split_low, 1)
            dve.wait_ge(split_high, 2 + 5 * CC)
            dve.tensor_tensor(wo_l[:, :, :], raw_o[:, :, :], wo_h[:, :, :], ALU.subtract).then_inc(split_low, 1)
            dve.wait_ge(ob_mm, 1)
            dve.wait_ge(bias_step, 7)
            dve.tensor_tensor(out_bias[:, :], bo_b[:, :], qk[1][:, :], ALU.add).then_inc(bias_done, 2)
            for cc in range(CC):
                z_low(0, cc)

            def shift(i, t):
                s = sc[t // 2][:, t % 2, :, :]
                k = t % 2
                if t >= 2:
                    dve.wait_ge(probs_t, i * T + t - 1)
                dve.tensor_reduce(mx[:, k, :], s, XA, ALU.max).then_inc(max_d, 1)
                dve.wait_ge(max_d, i * T + t + 1)
                dve.tensor_tensor(prob[:, k, :, :], s, mx[:, k, :].unsqueeze(2).to_broadcast([P, HEADS, FRAMES]),
                                  ALU.subtract).then_inc(shifted, 1)

            def total(i, t):
                k = t % 2
                dve.wait_ge(exped, i * T + t + 1)
                dve.tensor_reduce(sm[:, k, :], prob[:, k, :, :], XA, ALU.add).then_inc(summed, 1)
                dve.wait_ge(summed, i * T + t + 1)
                if t >= 2:
                    dve.wait_ge(normed, i * T + t - 1)
                dve.reciprocal(rc[:, k, :], sm[:, k, :]).then_inc(inverted, 1)

            def spread(i, t, first):
                dve.wait_ge(normed, i * T + t + 1)
                if t >= 2 or not first:
                    dve.wait_ge(pv_mm, i * T + t - 1)
                elif t == 0:
                    dve.wait_ge(prob_t_zero, 1)
                for c in range(CLIPS):
                    q = slice(32 * c, 32 * c + 32)
                    last = dve.transpose(prob_t[q, t % 2, :, 32 * c:32 * c + 32], prob[q, t % 2, :, :])
                last.then_inc(probs_t, 1)

            def attended_low(i, t):
                dve.wait_ge(ot_high, i * T + t + 1)
                dve.tensor_tensor(ot_l[:, t % 2, :, :], tr[t % 2][:, :].rearrange("p (c r) -> p c r", c=CC),
                                  ot_h[:, t % 2, :, :], ALU.subtract).then_inc(ot_low, 1)

            def h1_tile(i, t, first):
                dve.wait_ge(wo_mm, i * T + t + 1)
                if t >= 2:
                    dve.wait_ge(h1_stored[t % 2], 32 * i + 16)
                    dve.wait_ge(y0_d, i * T + t - 1)
                elif not first:
                    dve.wait_ge(h1_stored[t], 32 * i)
                dve.wait_ge(hb_ready, i * T + t + 1)
                dve.tensor_tensor(h1[:, t % 2, 0:C], hb[:, t, :], ro[t % 2][:, :], ALU.add).then_inc(h1_ready, 1)
                dve.wait_ge(h1_ready, i * T + t + 1)
                dve.bn_stats(stat1[:, t, :], h1[:, t % 2, 0:C]).then_inc(stat1_d, 1)
                dve.wait_ge(stat1_d, i * T + t + 1)
                dve.nop(nofuse=True)
                dve.bn_aggr(h1[:, t % 2, C:CW], stat1[:, t, :]).then_inc(aggr1_d, 1)

            def channel0(i, t):
                dve.wait_ge(scale1_p, i * T + t + 1)
                dve.tensor_scalar(y0[:, t:t + 1], h1[:, t % 2, 0:1], h1[:, t % 2, C:C + 1],
                                  h1[:, t % 2, C + 1:CW], ALU.subtract, ALU.mult).then_inc(y0_d, 1)

            def choose(i):
                dve.wait_ge(y0_d, T * (i + 1))
                dve.tensor_tensor(above[:, :, 1:EXPERTS], y0[:, :].unsqueeze(2).to_broadcast([P, T, EXPERTS - 1]),
                                  const("bins").unsqueeze(1).to_broadcast([P, T, EXPERTS - 1]), ALU.is_gt)\
                    .then_inc(above_d, 1)
                dve.wait_ge(above_d, i + 1)
                dve.tensor_tensor(onehot[:, :, :], above[:, :, 0:EXPERTS], above[:, :, 1:EXPERTS + 1],
                                  ALU.subtract).then_inc(onehot_d, 1)

            def slots(i, first):
                dve.wait_ge(rank_mm, i + 1)
                dve.tensor_tensor(slot_b[:, :, :], ro[0][:, 0:T * EXPERTS].rearrange("p (t e) -> p t e", t=T),
                                  const("bucket").unsqueeze(1).to_broadcast([P, T, EXPERTS]), ALU.add)\
                    .then_inc(slot_b_d, 1)
                dve.tensor_reduce(block_sum[:, :], onehot[:, :, :].rearrange("p t e -> p e t"), XA, ALU.add)\
                    .then_inc(block_sum_d, 1)
                dve.wait_ge(slot_b_d, i + 1)
                dve.tensor_tensor(slot_m[:, :, :], slot_b[:, :, :], onehot[:, :, :], ALU.mult)\
                    .then_inc(slot_m_d, 1)
                dve.wait_ge(block_sum_d, i + 1)
                dve.tensor_tensor(so_far[:, :], so_far[:, :], block_sum[:, :], ALU.add).then_inc(so_far_d, 1)
                dve.wait_ge(slot_m_d, i + 1)
                dve.tensor_reduce(slot_f[:, :], slot_m[:, :, :], XA, ALU.add).then_inc(slot_f_d, 1)
                dve.wait_ge(slot_f_d, i + 1)
                if not first:
                    dve.wait_ge(scattered, 16 * T * i)
                dve.tensor_copy(slot[:, :], slot_f[:, :]).then_inc(slot_d, 1)

            def body(i, nxt, first, second):
                if not first:
                    slots(i - 1, second)
                if nxt:
                    frames_low(i + 1, 0)
                    frames_low(i + 1, 1)
                    for t in range(2, T):
                        h_stats(i + 1, t - 2, False)
                        frames_low(i + 1, t)
                    h_stats(i + 1, T - 2, False)
                    h_stats(i + 1, T - 1, False)
                    z_tiles(i + 1, False)
                dve.wait_ge(scored, PAIRS * (i + 1))
                shift(i, 0)
                shift(i, 1)
                for t in range(2):
                    total(i, t)
                    spread(i, t, first)
                    shift(i, t + 2)
                for t in range(2):
                    total(i, t + 2)
                    if nxt:
                        z_low(i + 1, t)
                for t in range(2):
                    attended_low(i, t)
                    spread(i, t + 2, first)
                if nxt:
                    z_low(i + 1, 2)
                    z_low(i + 1, 3)
                h1_tile(i, 0, first)
                attended_low(i, 2)
                h1_tile(i, 1, first)
                channel0(i, 0)
                attended_low(i, 3)
                h1_tile(i, 2, first)
                channel0(i, 1)
                h1_tile(i, 3, first)
                channel0(i, 2)
                channel0(i, 3)
                choose(i)

            body(0, True, True, False)
            body(1, True, False, True)
            with dve.Fori(2, NBLOCK - 1) as i:
                body(i, True, False, False)
            body(NBLOCK - 1, False, False, False)
            slots(NBLOCK - 1, False)

            def expert_low(e):
                at = e * 2 * EW
                dve.wait_ge(we_high, e + 1)
                dve.tensor_tensor(we[:, at + EW:at + 2 * EW], we_raw[:, e % 2, :], we[:, at:at + EW],
                                  ALU.subtract).then_inc(we_low, 1)

            dve.wait_ge(count_mm, 1)
            expert_low(0)
            dve.wait_ge(scattered, 16 * T * NBLOCK)
            for k in range(2):
                dve.wait_ge(h1_stored[k], 16 * NTILE // 2)
            dve.tensor_copy(counts[:, :], ro[1][:, 0:EXPERTS]).then_inc(plan_d, 1)
            dve.wait_ge(plan_d, 1)
            dve.tensor_tensor(exceeds[:, :, :], counts[:, :].unsqueeze(2).to_broadcast([P, EXPERTS, NTILE]),
                              const("tile128").unsqueeze(1).to_broadcast([P, EXPERTS, NTILE]), ALU.is_gt)\
                .then_inc(plan_d, 1)
            dve.wait_ge(plan_d, 2)
            dve.tensor_reduce(tiles_of[:, :], exceeds[:, :, :], XA, ALU.add).then_inc(plan_d, 1)
            dve.wait_ge(plan_d, 3)
            dve.tensor_tensor(lower_m[:, :, :], tiles_of[:, :].unsqueeze(1).to_broadcast([P, EXPERTS, EXPERTS]),
                              const("lower").rearrange("p (a b) -> p a b", a=EXPERTS), ALU.mult)\
                .then_inc(plan_d, 1)
            dve.wait_ge(plan_d, 4)
            dve.tensor_reduce(first_of[:, :], lower_m[:, :, :], XA, ALU.add).then_inc(plan_d, 1)
            dve.wait_ge(plan_d, 5)
            dve.tensor_scalar(started[:, :], first_of[:, :], const("partition"), None, ALU.is_le)\
                .then_inc(plan_d, 1)
            dve.wait_ge(plan_d, 6)
            dve.tensor_reduce(expert_of[:, :], started[:, 1:EXPERTS], XA, ALU.add).then_inc(plan_d, 1)
            dve.tensor_tensor(skipped[:, :], started[:, 1:EXPERTS], tiles_of[:, 0:EXPERTS - 1], ALU.mult)\
                .then_inc(plan_s, 1)
            dve.wait_ge(plan_s, 1)
            dve.tensor_reduce(start_of[:, :], skipped[:, :], XA, ALU.add).then_inc(plan_s, 1)
            dve.wait_ge(plan_s, 2)
            dve.tensor_tensor(in_bucket[:, :], const("partition"), start_of[:, :], ALU.subtract)\
                .then_inc(plan_s, 1)
            dve.wait_ge(plan_s, 3)
            dve.wait_ge(plan_d, 7)
            dve.scalar_tensor_tensor(out=table_f[:, :], in0=expert_of[:, :], scalar=float(BUCKET // P),
                                     in1=in_bucket[:, :], op0=ALU.mult, op1=ALU.add).then_inc(plan_s, 1)
            dve.wait_ge(plan_s, 4)
            dve.tensor_copy(table_r[:, :], table_f[:, :]).then_inc(plan_d, 1)
            expert_low(1)
            dve.wait_ge(plan_t, 1)
            dve.tensor_copy(expert_row[0:1, :], ro[0][0:1, 0:FTILE]).then_inc(index_d, 1)
            dve.wait_ge(picked_t, 1)
            dve.tensor_copy(index[:, :], tr[0][:, 0:FTILE]).then_inc(index_d, 1)
            for e in range(2, EXPERTS):
                expert_low(e)

            def ffn_norm(u, w, k, first):
                dve.wait_ge(g_in[k], 16 * (w + 1))
                if not first:
                    dve.wait_ge(z2_t, u - 1)
                dve.tensor_scalar(z2[:, k % 2, :], g[:, k, 0:C], g[:, k, C:C + 1], g[:, k, C + 1:CW],
                                  ALU.subtract, ALU.mult).then_inc(z2_ready, 1)

            def ffn_low(u, k):
                dve.wait_ge(z2t_high, u + 1)
                dve.tensor_tensor(z2t_l[:, k % 2, :, :], tr[k % 2][:, :].rearrange("p (c r) -> p c r", c=CC),
                                  z2t_h[:, k % 2, :, :], ALU.subtract).then_inc(z2t_low, 1)

            def ffn_out(u, w, k):
                dve.wait_ge(ffn_mm, u + 1)
                n = 2 * w + k // 4
                if not (isinstance(n, int) and n == 0):
                    dve.wait_ge(res_out[k % 4], 16 * n)
                dve.tensor_tensor(res[:, k % 4, :], g[:, k, 0:C], ro[k % 2][:, :], ALU.add).then_inc(res_ready, 1)

            ffn_norm(0, 0, 0, True)
            ffn_norm(1, 0, 1, True)
            ffn_low(0, 0)
            ffn_low(1, 1)
            ffn_norm(2, 0, 2, False)

            def group(w, last):
                for k in range(8):
                    u = 8 * w + k
                    ffn_out(u, w, k)
                    if k < 6 or not last:
                        ffn_low(u + 2, k)
                    if k < 5 or not last:
                        ffn_norm(u + 3, w if k < 5 else w + 1, (k + 3) % 8, False)

            group(0, False)
            with dve.Fori(1, GROUPS - 1) as w:
                group(w, False)
            group(GROUPS - 1, True)

        @block.tensor
        def _(pe):
            def product(out_ap, pairs):
                n = 0
                for (wh, wl), (mh, ml) in pairs:
                    for w, m in ((wh, mh), (wh, ml), (wl, mh)):
                        n += 1
                        last = pe.matmul(out_ap, w, m, start=n == 1, stop=n == 3 * len(pairs))
                return last

            def transpose_frames(a, t):
                pe.wait_ge(folded, 2 * (a * T + t + 1))
                for c in range(4):
                    last = pe.transpose(tr[t % 2][:, c * P:(c + 1) * P],
                                        fold[:, t % 2, c // 2, (c % 2) * P:(c % 2 + 1) * P], ident)
                last.then_inc(frames_t, 1)

            def dct(a, t):
                pe.wait_ge(xt_low, a * T + t + 1)
                for eo in range(2):
                    last = product(ro[t % 2][:, eo * HALF:(eo + 1) * HALF],
                                   [((xt_h[:, t % 2, 2 * eo + c, :], xt_l[:, t % 2, 2 * eo + c, :]),
                                     (dct_h[:, eo, c, :], dct_l[:, eo, c, :])) for c in range(2)])
                last.then_inc(dct_mm, 1)

            def transpose_z(a, cc):
                pe.wait_ge(z_ready, T * (a + 1))
                if cc >= 2:
                    pe.wait_ge(zt_low, a * CC + cc - 1)
                for t in range(T):
                    last = pe.transpose(qk[cc % 2][:, t * P:(t + 1) * P], z[:, t, cc * P:(cc + 1) * P], ident)
                last.then_inc(z_t, 1)

            pe.wait_ge(small_in_s, 16)
            transpose_frames(0, 0)
            transpose_frames(0, 1)
            pe.wait_ge(split_low, 1)
            for t in range(T):
                if t >= 2:
                    pe.wait_ge(h_ready, t - 1)
                dct(0, t)
                if t + 2 < T:
                    transpose_frames(0, t + 2)

            pe.wait_ge(w_in_s, 6 * 16)
            pe.wait_ge(bias_in_s, 11 * 16)
            for n in range(2):
                for m in range(PAIRS):
                    at = n * PAIRS + m
                    for cc in range(CC):
                        pe.matmul(qk[0][:, at:at + 1], raw_s[:, n, cc, m * P:(m + 1) * P],
                                  shift_c[:, cc:cc + 1], start=cc == 0, stop=cc == CC - 1)
                for cc in range(CC):
                    pe.matmul(qk[0][0:POINTS, 8 + n:9 + n], raw_p[:, n, cc, :],
                              shift_c[:, cc:cc + 1], start=cc == 0, stop=cc == CC - 1)
            for co in range(CC):
                for cc in range(CC):
                    pe.matmul(qk[0][:, 12 + co:13 + co], raw_v[:, cc, co * P:(co + 1) * P],
                              shift_c[:, cc:cc + 1], start=cc == 0, stop=cc == CC - 1)
            pe.matmul(qk[0][0:POINTS, 16:17], const("head_of")[0:HEADS, :], ps_c[:, :], start=True, stop=True)\
                .then_inc(bias_mm, 1)
            pe.wait_ge(vb_ready, 1)
            for cc in range(CC):
                last = pe.matmul(qk[1][:, :], v_bias_b[:, cc, :], raw_o[:, cc, :], start=cc == 0, stop=cc == CC - 1)
            last.then_inc(ob_mm, 1)
            pe.wait_ge(bias_done, 2)
            for cc in range(CC):
                transpose_z(0, cc)

            def features(i, s, side, first):
                if s == 0 and side == 0:
                    pe.wait_ge(zt_low, CC * (i + 1))
                elif s:
                    pe.wait_ge((q_ev, k_ev)[side], 2 * (FEATURES * i + s))
                cols = slice(C, QK) if s == 0 else slice((s - 1) * P, s * P)
                rows = POINTS if s == 0 else P
                product(qk[side][0:rows, :],
                        [((wqk_h[:, side, cc, cols], wqk_l[:, side, cc, cols]),
                          (zt_h[:, cc, :], zt_l[:, cc, :])) for cc in range(CC)])\
                    .then_inc((q_mm, k_mm)[side], 1)

            def scores(i, m, first):
                pe.wait_ge(q_ev, 2 * (FEATURES * i + m + 2))
                pe.wait_ge(k_ev, 2 * (FEATURES * i + m + 2))
                pe.wait_ge(points_in[m], PD * (i + 1))
                if m == 0:
                    if first:
                        pe.wait_ge(fixed_rows, 2 * HEADS * 16)
                    else:
                        pe.wait_ge(shifted, T * i)
                for hd in (2 * m, 2 * m + 1):
                    for t in range(T):
                        for c in range(CLIPS):
                            cols = slice(t * P + 32 * c, t * P + 32 * c + 32)
                            last = pe.matmul(sc[t // 2][32 * c:32 * c + 32, t % 2, hd, :], qf[:, hd, cols],
                                             kf[:, hd, cols], start=True, stop=True)
                last.then_inc(scored, 1)

            def values(i, t):
                if t >= 2:
                    pe.wait_ge(v_ev, i * T + t - 1)
                product(ro[t % 2][:, :],
                        [((zt_h[:, cc, t * P:(t + 1) * P], zt_l[:, cc, t * P:(t + 1) * P]),
                          (wv_h[:, cc, :], wv_l[:, cc, :])) for cc in range(CC)]).then_inc(v_mm, 1)

            def attend(i, t):
                pe.wait_ge(probs_t, i * T + t + 1)
                pe.wait_ge(v_ev, i * T + t + 1)
                if t >= 2:
                    pe.wait_ge(ot_low, i * T + t - 1)
                for hd in range(HEADS):
                    half = 64 * (hd % 2)
                    last = pe.matmul(tr[t % 2][half:half + HD, (hd // 2) * P:(hd // 2 + 1) * P],
                                     v[:, t, hd * HD:(hd + 1) * HD], prob_t[:, t % 2, hd, :],
                                     start=True, stop=True)
                last.then_inc(pv_mm, 1)

            def project(i, t):
                pe.wait_ge(ot_low, i * T + t + 1)
                if t >= 2:
                    pe.wait_ge(h1_ready, i * T + t - 1)
                else:
                    pe.wait_ge(v_ev, i * T + t + 3)
                product(ro[t % 2][:, :],
                        [((ot_h[:, t % 2, cc, :], ot_l[:, t % 2, cc, :]), (wo_h[:, cc, :], wo_l[:, cc, :]))
                         for cc in range(CC)]).then_inc(wo_mm, 1)

            def rank(i, first):
                pe.wait_ge(onehot_d, i + 1)
                pe.wait_ge(h1_ready, T * (i + 1))
                if not first:
                    pe.wait_ge(so_far_d, i)
                r = ro[0][:, 0:T * EXPERTS].rearrange("p (t e) -> p t e", t=T)
                pe.matmul(r, before_b[:, :], onehot[:, :, :], start=True, stop=False)
                for t in range(1, T):
                    pe.matmul(r[:, t:T, :], ones_b[:, :], onehot[:, 0:T - t, :], start=False, stop=False)
                pe.matmul(r, ones_b[:, :], so_far[:, :].unsqueeze(1).to_broadcast([P, T, EXPERTS]),
                          start=False, stop=True).then_inc(rank_mm, 1)

            def body(i, nxt, first, second):
                n = 0
                for s in range(FEATURES):
                    for side in range(2):
                        features(i, s, side, first)
                        if n == 1:
                            if not first:
                                rank(i - 1, second)
                            if nxt:
                                if first:
                                    pe.wait_ge(xt_low, T)
                                else:
                                    pe.wait_ge(ot_low, T * i)
                                transpose_frames(i + 1, 0)
                        if nxt and n == 2:
                            transpose_frames(i + 1, 1)
                        if n == 3:
                            if nxt and not first:
                                pe.wait_ge(slot_b_d, i)
                            if nxt and first:
                                pe.wait_ge(h_ready, T)
                            if nxt:
                                dct(i + 1, 0)
                        if nxt and n == 4:
                            transpose_frames(i + 1, 2)
                        if nxt and n == 5:
                            if not first:
                                pe.wait_ge(h1_ready, T * i)
                            dct(i + 1, 1)
                        if nxt and n == 6:
                            transpose_frames(i + 1, 3)
                        if nxt and n in (7, 8):
                            pe.wait_ge(h_ready, (i + 1) * T + n - 6)
                            dct(i + 1, n - 5)
                        if n in (5, 7, 9):
                            scores(i, (n - 5) // 2, first)
                        n += 1
                if nxt:
                    pe.wait_ge(h_ready, (i + 2) * T)
                else:
                    pe.wait_ge(slot_b_d, i)
                values(i, 0)
                scores(i, PAIRS - 1, first)
                values(i, 1)
                values(i, 2)
                if nxt:
                    transpose_z(i + 1, 0)
                    transpose_z(i + 1, 1)
                values(i, 3)
                attend(i, 0)
                attend(i, 1)
                if nxt:
                    transpose_z(i + 1, 2)
                project(i, 0)
                if nxt:
                    transpose_z(i + 1, 3)
                attend(i, 2)
                project(i, 1)
                attend(i, 3)
                project(i, 2)
                project(i, 3)

            body(0, True, True, False)
            body(1, True, False, True)
            with pe.Fori(2, NBLOCK - 1) as i:
                body(i, True, False, False)
            body(NBLOCK - 1, False, False, False)
            rank(NBLOCK - 1, False)
            pe.wait_ge(so_far_d, NBLOCK)
            pe.matmul(ro[1][:, 0:EXPERTS], ones_b[:, :], so_far[:, :], start=True, stop=True).then_inc(count_mm, 1)

            pe.wait_ge(plan_d, 8)
            pe.matmul(ro[0][0:1, 0:FTILE], expert_of[0:FTILE, :], ident[0:FTILE, 0:FTILE],
                      start=True, stop=True).then_inc(plan_t, 1)
            pe.wait_ge(table_in, 16)
            pe.transpose(tr[0][:, 0:FTILE], picked[0:FTILE, :], ident[0:FTILE, 0:FTILE]).then_inc(picked_t, 1)
            pe.wait_ge(index_d, 2)

            def transpose_rows(u, k, first):
                pe.wait_ge(z2_ready, u + 1)
                if not first:
                    pe.wait_ge(z2t_low, u - 1)
                for cc in range(CC):
                    last = pe.transpose(tr[k][:, cc * P:(cc + 1) * P], z2[:, k, cc * P:(cc + 1) * P], ident)
                last.then_inc(z2_t, 1)

            def expert_product(u, k, first):
                e = pe.value_load(expert_row[0:1, bass.ds(u, 1)], min_val=0, max_val=EXPERTS - 1)
                pe.wait_ge(we_low, e + 1)
                pe.wait_ge(z2t_low, u + 1)
                if not first:
                    pe.wait_ge(res_ready, u - 1)
                at = e * (2 * EW)
                product(ro[k][:, :],
                        [((z2t_h[:, k, cc, :], z2t_l[:, k, cc, :]),
                          (we[:, bass.ds(at + cc * C, C)], we[:, bass.ds(at + EW + cc * C, C)]))
                         for cc in range(CC)]).then_inc(ffn_mm, 1)

            transpose_rows(0, 0, True)
            transpose_rows(1, 1, True)
            for k in range(2):
                expert_product(k, k, True)
                transpose_rows(k + 2, k, False)
            with pe.Fori(1, FTILE // 2 - 1) as w:
                for k in range(2):
                    expert_product(2 * w + k, k, False)
                    transpose_rows(2 * w + k + 2, k, False)
            for k in range(2):
                expert_product(FTILE - 2 + k, k, False)


_INS = ["x", "L0_attn_ln_g", "L0_attn_ln_b", "L0_attn_wq", "L0_attn_bq", "L0_attn_wk", "L0_attn_bk",
        "L0_attn_wv", "L0_attn_bv", "L0_attn_wqp", "L0_attn_bqp", "L0_attn_wkp", "L0_attn_bkp",
        "L0_attn_wo", "L0_attn_bo", "L0_attn_pscale", "L0_ffn_W"]


def kernel(**inputs):
    import concourse.bacc as bacc
    from concourse.bass_utils import run_bass_kernel_spmd

    nc = bacc.Bacc("TRN2", target_bir_lowering=False, num_devices=1)
    dct, small, place = constants()
    arrays = {f"in_{n}": np.ascontiguousarray(inputs[n]) for n in _INS}
    arrays["const_dct"], arrays["const_small"] = dct, small
    aps = [nc.dram_tensor(n, a.shape, mybir.dt.from_np(a.dtype), kind="ExternalInput").ap()
           for n, a in arrays.items()]
    out = nc.dram_tensor("out", (BATCH, FRAMES, C), mybir.dt.float32, kind="ExternalOutput").ap()
    audio_tower(nc, *aps, place, out)
    r = run_bass_kernel_spmd(nc, [arrays], core_ids=[0])
    return r.results[0]["out"]
```

```python
import numpy as np
from contextlib import ExitStack

import concourse.bass as bass
from concourse import mybir


BATCH, SAMPLES, HOP = 256, 16000, 512
FRAMES = (SAMPLES + HOP - SAMPLES % HOP) // HOP
TAIL = SAMPLES - (FRAMES - 1) * HOP
ROWS = BATCH * FRAMES
C = HOP
HEADS, POINT = 8, 12
POINTS = HEADS * POINT
HD = C // HEADS
BINS = (-1.5, -1.0, -0.5, 0.0, 0.5, 1.0, 1.5)
EXPERTS = len(BINS) + 1
EPS = 1e-5
P = 128
CC = C // P
PAIRS = HEADS // 2
CLIPS = P // FRAMES
T = 4
BLOCK = T * P
NBLOCK = ROWS // BLOCK
NTILE = ROWS // P
HALF = HOP // 2
QK = C + POINTS
BUCKET = ROWS
FTILE = NTILE + EXPERTS - 1
GROUP = 8
GROUPS = -(-FTILE // GROUP)
LAST = FTILE - GROUP * (GROUPS - 1)
TABLE = EXPERTS * BUCKET + P * P // 2
CW = C + 2
EW = CC * C


def point_rows(head):
    return HD * (1 - head % 2)


def points_by_parity(ap):
    return ap.rearrange("a (h two p) -> a two p h", two=2, p=POINT)


def constants():
    k = np.arange(HOP)[:, None].astype(np.float64)
    n = np.arange(HOP)[None, :].astype(np.float64)
    basis = np.cos(np.pi * (2.0 * n + 1.0) * k / (2.0 * HOP))
    scale = np.full((HOP, 1), np.sqrt(2.0 / HOP))
    scale[0, 0] = np.sqrt(1.0 / HOP)
    basis = (scale * basis).astype(np.float32)
    dct = np.stack([basis[0::2, :HALF].T, basis[1::2, :HALF].T], axis=1)
    dct = dct.reshape(HALF // P, P, 2, HALF).transpose(1, 2, 0, 3)
    f = np.arange(P)
    cols = {}
    cols["ident"] = np.eye(P)
    cols["before"] = f[:, None] < f[None, :]
    at = np.arange(POINTS)
    cols["head_of"] = (f[:, None] == 2 * (at % PAIRS) + at // (POINTS // 2))
    cols["bins"] = np.tile(np.array(BINS), (P, 1))
    cols["bucket"] = np.tile(np.arange(EXPERTS) * BUCKET, (P, 1))
    cols["tile128"] = np.tile(np.arange(NTILE) * P, (P, 1))
    cols["partition"] = f[:, None]
    cols["lower"] = np.tile(np.tril(np.ones((EXPERTS, EXPERTS)), -1).reshape(-1), (P, 1))
    cols["rows"] = f[:, None] + P * np.arange(T)[None, :]
    at, place = 0, {}
    for name, a in cols.items():
        place[name] = (at, at + a.shape[1])
        at += a.shape[1]
    small = np.concatenate([a.astype(np.float32) for a in cols.values()], axis=1)
    return np.ascontiguousarray(dct), np.ascontiguousarray(small), place


def audio_tower(nc, x, ln_g, ln_b, wq, bq, wk, bk, wv, bv, wqp, bqp, wkp, bkp, wo, bo, pscale, w_ffn,
                dct_in, small_in, place, out):
    f32, f32r, bf16, u32, i32 = (mybir.dt.float32, mybir.dt.float32r, mybir.dt.bfloat16,
                                 mybir.dt.uint32, mybir.dt.int32)
    ALU, ACT, XA = mybir.AluOpType, mybir.ActivationFunctionType, mybir.AxisListType.X

    x_flat = x.rearrange("b n -> (b n)")
    out_rows = out.rearrange("b f c -> (b f) c")
    h1_dram = nc.dram_tensor("h1_rows", (ROWS + 1, CW), f32, kind="Internal").ap()
    table = nc.dram_tensor("row_table", (TABLE, 1), f32, kind="Internal").ap()

    ctx = ExitStack()
    with ctx:
        def sb(name, shape, dt, where=ctx):
            return where.enter_context(nc.sbuf_tensor(name, shape, dt))

        def sem(name):
            return ctx.enter_context(nc.semaphore(name))

        tr = [ctx.enter_context(nc.psum_tensor(f"transposed{k}", [P, 512], f32)) for k in range(2)]
        ro = [ctx.enter_context(nc.psum_tensor(f"row_out{k}", [P, 512], f32)) for k in range(2)]
        qk = [ctx.enter_context(nc.psum_tensor(f"qk_out{k}", [P, 512], f32)) for k in range(2)]
        sc = [ctx.enter_context(nc.psum_tensor(f"scores{k}", [P, 2, HEADS, FRAMES], f32))
              for k in range(2)]

        small = sb("small", list(small_in.shape), f32)

        def const(name):
            a, b = place[name]
            return small[:, a:b]

        ident = const("ident")
        before_b = sb("before_bf16", [P, P], bf16)
        ones_b = sb("ones_bf16", [P, P], bf16)
        minus_half = sb("minus_half", [P, T], f32)
        onehot = sb("onehot", [P, T, EXPERTS], bf16)
        so_far = sb("so_far", [P, EXPERTS], bf16)
        block_sum = sb("block_sum", [P, EXPERTS], f32)
        above = sb("above", [P, T, EXPERTS + 1], f32)
        row_id = sb("row_id", [P, T], f32)
        counts = sb("counts", [P, EXPERTS], f32)
        tiles_of = sb("tiles_of", [P, EXPERTS], f32)
        lower_m = sb("lower_masked", [P, EXPERTS, EXPERTS], f32)
        first_of = sb("first_tile_of", [P, EXPERTS], f32)
        started = sb("started", [P, EXPERTS], f32)
        skipped = sb("skipped", [P, EXPERTS - 1], f32)
        expert_of = sb("expert_of", [P, 1], f32)
        start_of = sb("start_of", [P, 1], f32)
        in_bucket = sb("in_bucket", [P, 1], f32)
        table_f = sb("table_row_f", [P, 1], f32)
        table_r = sb("table_row", [P, 1], u32)

        part1 = ctx.enter_context(ExitStack())
        wo_h = sb("wo_high", [P, CC, C], f32r, part1)
        wo_l = sb("wo_low", [P, CC, C], f32r, part1)
        out_bias = sb("out_bias", [P, C], f32, part1)
        exceeds = out_bias[:, 0:EXPERTS * NTILE].rearrange("p (e t) -> p e t", e=EXPERTS)
        bias_s = sb("bias_scalar", [P, 2 * PAIRS], f32, part1)
        bias_p = sb("bias_points", [P, 2], f32, part1)
        bias_dot = sb("bias_query_points", [P, 1], f32, part1)
        ps2 = sb("two_pscale", [P, 1], f32, part1)
        hb = sb("h_plus_bias", [P, T, C], f32, part1)
        v = sb("v", [P, T, C], f32, part1)
        stat = sb("stat", [P, T, 6], f32, part1)
        mv = sb("mean_var", [P, T, 2], f32, part1)
        var_e = sb("var_eps", [P, T], f32, part1)
        rs = sb("z_scale", [P, T], f32, part1)
        mx = sb("score_max", [P, 2, HEADS], f32, part1)
        sm = sb("prob_sum", [P, 2, HEADS], f32, part1)
        rc = sb("prob_scale", [P, 2, HEADS], f32, part1)
        stat1 = sb("stat1", [P, T, 6], f32, part1)
        var1 = sb("var_eps1", [P, T], f32, part1)
        y0 = sb("channel0", [P, T], f32, part1)
        slot_b = sb("slot_by_expert", [P, T, EXPERTS], f32, part1)
        slot_m = sb("slot_masked", [P, T, EXPERTS], f32, part1)
        slot_f = sb("slot", [P, T], f32, part1)
        slot = sb("slot_index", [P, T], u32, part1)
        dct_h = sb("dct_high", [P, 2, 2, HALF], f32r, part1)
        dct_l = sb("dct_low", [P, 2, 2, HALF], f32r, part1)
        xs = sb("samples", [P, T, HOP], f32, part1)
        fold = sb("folded_tiles", [P, 2, 2, HALF], f32, part1)
        xt_h = sb("frames_t_high", [P, 2, 4, P], f32r, part1)
        xt_l = sb("frames_t_low", [P, 2, 4, P], f32r, part1)
        h = sb("h", [P, T, C], f32, part1)
        z = sb("z", [P, T, C], f32, part1)
        wqk_h = sb("wqk_high", [P, 2, CC, QK], f32r, part1)
        wqk_l = sb("wqk_low", [P, 2, CC, QK], f32r, part1)
        wv_h = sb("wv_high", [P, CC, C], f32r, part1)
        wv_l = sb("wv_low", [P, CC, C], f32r, part1)
        zt_h = sb("z_t_high", [P, CC, BLOCK], f32r, part1)
        zt_l = sb("z_t_low", [P, CC, BLOCK], f32r, part1)

        setup = ExitStack()
        with setup:
            raw_s = sb("raw_wq_wk", [P, 2, CC, C], f32, setup)
            raw_v = sb("raw_wv", [P, CC, C], f32, setup)
            raw_d = sb("raw_dct", [P, 2, 2, HALF], f32, setup)
            raw_p = sb("raw_wqp_wkp", [P, 2, CC, POINTS], f32, setup)
            sentinel = sb("sentinel", [P, TABLE // P], f32, setup)
            raw_o = sb("raw_wo", [P, CC, C], f32, setup)
            gain = sb("ln_gain", [P, CC], f32, setup)
            gain_q = sb("ln_gain_q", [P, CC], f32, setup)
            shift_c = sb("ln_shift", [P, CC], f32, setup)
            raw_bs = sb("raw_bias_scalar", [P, 2 * PAIRS], f32, setup)
            raw_bp = sb("raw_bias_points", [P, 2], f32, setup)
            raw_bv = sb("raw_bias_v", [P, CC], f32, setup)
            ps_c = sb("pscale_column", [HEADS, 1], f32, setup)
            ps_b = sb("pscale_b", [P, HEADS], f32, setup)
            neg_ps = sb("minus_pscale", [P, HEADS], f32, setup)
            bo_b = sb("bo_b", [P, C], f32, setup)
            v_bias = sb("v_bias", [P, CC], f32, setup)
            v_bias_b = sb("v_bias_b", [P, CC, P], f32, setup)
            zero_row = sb("zero_row", [1, CW], f32, setup)

        qf = sb("q_features", [P, HEADS, BLOCK], f32, part1)
        kf = sb("k_features", [P, HEADS, BLOCK], f32, part1)
        prob = sb("prob", [P, 2, HEADS, FRAMES], f32, part1)
        prob_t = sb("prob_t", [P, 2, HEADS, P], f32, part1)
        ot_h = sb("attended_t_high", [P, 2, CC, P], f32r, part1)
        ot_l = sb("attended_t_low", [P, 2, CC, P], f32r, part1)
        h1 = sb("h1", [P, 2, CW], f32, part1)
        part1.close()

        picked = sb("picked", [P, P], f32)
        index = sb("index", [P, FTILE], u32)
        index_now = sb("index_now", [P, GROUP], u32)
        expert_row = sb("expert_row", [1, FTILE], i32)
        g = sb("gathered", [P, GROUP, CW], f32)
        z2 = sb("z2", [P, 2, C], f32)
        z2t_h = sb("z2_t_high", [P, 2, CC, P], f32r)
        z2t_l = sb("z2_t_low", [P, 2, CC, P], f32r)
        res = sb("result", [P, 4, C], f32)
        we = sb("w_ffn_halves", [P, EXPERTS * 2 * EW], f32r)
        we_raw = we.bitcast(f32)[:, :].rearrange("p (e h n) -> p e h n", e=EXPERTS, h=2)

        small_in_s, dct_in_s, w_in_s, wvo_in_s, gain_in_s, bias_in_s = (
            sem("small_in"), sem("dct_in"), sem("w_in"), sem("wvo_in"), sem("gain_in"), sem("bias_in"))
        pool_consts, consts_made, split_high, split_low = (sem("pool_consts"), sem("consts_made"),
                                                           sem("split_high"), sem("split_low"))
        gain_made, bias_step, bias_mm, vb_ready, ob_mm, bias_done = (
            sem("gain_made"), sem("bias_step"), sem("bias_mm"), sem("vb_ready"), sem("ob_mm"),
            sem("bias_done"))
        table_cleared, prob_t_zero, xs_zero = sem("table_cleared"), sem("prob_t_zero"), sem("xs_zero")
        rows_zero, fixed_src, fixed_rows = sem("rows_zero"), sem("fixed_src"), sem("fixed_rows")
        rows_mm, rows_ev = sem("rows_mm"), sem("rows_ev")
        x_loaded, folded, frames_t = sem("x_loaded"), sem("folded"), sem("frames_t")
        xt_high, xt_low, dct_mm, h_ready = sem("xt_high"), sem("xt_low"), sem("dct_mm"), sem("h_ready")
        stat_d, aggr_d, var_p, scale_p = sem("stat_d"), sem("aggr_d"), sem("var_p"), sem("scale_p")
        z_ready, z_t, zt_high, zt_low = sem("z_ready"), sem("z_t"), sem("zt_high"), sem("zt_low")
        q_mm, k_mm, q_ev, k_ev = sem("q_mm"), sem("k_mm"), sem("q_ev"), sem("k_ev")
        points_in, scored = sem("points_in"), sem("scored")
        v_mm, v_ev = sem("v_mm"), sem("v_ev")
        max_d, shifted, exped, summed = sem("max_d"), sem("shifted"), sem("exped"), sem("summed")
        inverted, normed, probs_t = sem("inverted"), sem("normed"), sem("probs_t")
        pv_mm, ot_high, ot_low, wo_mm = sem("pv_mm"), sem("ot_high"), sem("ot_low"), sem("wo_mm")
        h1_ready, hb_ready = sem("h1_ready"), sem("hb_ready")
        h1_stored = [sem("h1_stored0"), sem("h1_stored1")]
        stat1_d, aggr1_d, var1_p, scale1_p = (sem("stat1_d"), sem("aggr1_d"), sem("var1_p"),
                                              sem("scale1_p"))
        y0_d, above_d, onehot_d, block_sum_d, so_far_d = (
            sem("y0_d"), sem("above_d"), sem("onehot_d"), sem("block_sum_d"), sem("so_far_d"))
        rank_mm, slot_b_d, slot_m_d, slot_f_d, slot_d = (sem("rank_mm"), sem("slot_b_d"),
                                                         sem("slot_m_d"), sem("slot_f_d"),
                                                         sem("slot_d"))
        scattered, ids_next = sem("scattered"), sem("ids_next")
        count_mm, plan_d, plan_s, table_in, picked_t, plan_t, index_d = (
            sem("count_mm"), sem("plan_d"), sem("plan_s"), sem("table_in"), sem("picked_t"),
            sem("plan_t"), sem("index_d"))
        we_in = [sem(f"we_in{e}") for e in range(EXPERTS)]
        we_high, we_low = sem("we_high"), sem("we_low")
        index_now_d = sem("index_now_d")
        g_in = [sem(f"g_in{k}") for k in range(8)]
        z2_ready, z2_t, z2t_high, z2t_low, ffn_mm, res_ready = (
            sem("z2_ready"), sem("z2_t"), sem("z2t_high"), sem("z2t_low"), sem("ffn_mm"),
            sem("res_ready"))
        res_out = [sem(f"res_out{k}") for k in range(4)]

        block = ctx.enter_context(nc.Block())
        FIXED = 96
        EARLY = 2
        SPLITS = 2 + 5 * CC
        XD = 5 * 16
        PD = 2 * 4 * 16
        FEATURES = 1 + PAIRS

        bias_rows = [sc[0][0:1, :, :, :].rearrange("p t h k -> p (t h k)"),
                     sc[1][0:1, :, :, :].rearrange("p t h k -> p (t h k)"),
                     tr[1][0:1, :], tr[0][0:1, 0:2 * POINTS]]
        bias_out, value_out = ro

        @block.sync
        def _(sp):
            sp.dma_start(small[:, :], small_in).then_inc(small_in_s, 16)

            def load_samples(a, first):
                src = x_flat[bass.ds(a * (BLOCK // FRAMES * SAMPLES), BLOCK // FRAMES * SAMPLES)]\
                    .rearrange("(t c n) -> c t n", c=CLIPS, n=SAMPLES)
                if not first:
                    sp.wait_ge(folded, 2 * T * a)
                for c in range(CLIPS):
                    full = src[c, :, 0:(FRAMES - 1) * HOP].rearrange("t (f n) -> f t n", n=HOP)
                    sp.dma_start(xs[32 * c:32 * c + FRAMES - 1, :, :], full).then_inc(x_loaded, 16)
                tails = src[:, :, (FRAMES - 1) * HOP:SAMPLES]
                sp.dma_start(xs[FRAMES - 1:P:FRAMES, :, 0:TAIL], tails).then_inc(x_loaded, 16)

            sp.wait_ge(xs_zero, 1)
            load_samples(0, True)
            sp.dma_start(raw_d[:, :, :, :], dct_in).then_inc(dct_in_s, 16)
            for n, w in enumerate((wq, wk)):
                sp.dma_start(raw_s[:, n, :, :], w.rearrange("(c p) n -> p c n", p=P)).then_inc(w_in_s, 16)
            for n, w in enumerate((wqp, wkp)):
                sp.dma_start(raw_p[:, n, :, :], w.rearrange("(c p) n -> p c n", p=P)).then_inc(w_in_s, 16)
            sp.dma_start(raw_v[:, :, :], wv.rearrange("(c p) n -> p c n", p=P)).then_inc(wvo_in_s, 16)
            sp.dma_start(raw_o[:, :, :], wo.rearrange("(c p) n -> p c n", p=P)).then_inc(wvo_in_s, 16)
            sp.wait_ge(pool_consts, 2)
            sp.dma_start(table.rearrange("(p n) a -> p (n a)", p=P), sentinel[:, :]).then_inc(table_cleared, 16)
            sp.dma_start(h1_dram[ROWS:ROWS + 1, :], zero_row[:, :]).then_inc(table_cleared, 16)
            load_samples(1, False)
            sp.wait_ge(rows_zero, 4)
            sp.wait_ge(fixed_src, 2)
            for parity, src in enumerate((v, hb)):
                at = point_rows(parity)
                for f, row in ((qf, at + 2 * POINT), (kf, at + POINT)):
                    sp.dma_start(f[row:row + POINT, parity::2, :], src[FIXED:FIXED + POINT, :, :])\
                        .then_inc(fixed_rows, 16)

            def points(i):
                sp.wait_ge(q_ev, (2 * FEATURES) * i + 2)
                sp.wait_ge(k_ev, (2 * FEATURES) * i + 2)
                for parity in range(2):
                    at = point_rows(parity)
                    rows = slice(parity * POINTS // 2, (parity + 1) * POINTS // 2)
                    for f, square, j in ((qf, POINT, 0), (kf, 2 * POINT, 2)):
                        sp.dma_start(f[at:at + POINT, parity::2, :], v[rows, j, :]).then_inc(points_in, 16)
                        sp.dma_start(f[at + square:at + square + POINT, parity::2, :], v[rows, j + 1, :])\
                            .then_inc(points_in, 16)

            def store_h1(i, t):
                sp.wait_ge(scale1_p, i * T + t + 1)
                sp.dma_start(h1_dram[bass.ds(i * BLOCK + t * P, P), :], h1[:, t % 2, :])\
                    .then_inc(h1_stored[t % 2], 16)

            def body(i, load):
                points(i)
                if load:
                    load_samples(i + 2, False)
                for t in range(T):
                    store_h1(i, t)

            with sp.Fori(0, NBLOCK - 2) as i:
                body(i, True)
            body(NBLOCK - 2, False)
            points(NBLOCK - 1)

            def load_expert(e):
                sp.dma_start(we_raw[:, e, 1, :].rearrange("p (c n) -> p c n", c=CC),
                             w_ffn[e, :, :].rearrange("(c p) n -> p c n", p=P)).then_inc(we_in[e], 16)

            sp.wait_ge(folded, 2 * T * NBLOCK)
            sp.wait_ge(hb_ready, T * NBLOCK)
            sp.wait_ge(z_t, CC * NBLOCK)
            for e in range(EARLY):
                load_expert(e)
            sp.wait_ge(v_mm, T * NBLOCK)
            load_expert(EARLY)
            for t in range(T):
                load_expert(EARLY + 1 + t)
                store_h1(NBLOCK - 1, t)
            load_expert(EXPERTS - 1)
            for k in range(2):
                sp.wait_ge(h1_stored[k], 16 * NTILE // 2)

        @block.gpsimd
        def _(pool):
            pool.memset(sentinel[:, :], float(ROWS)).then_inc(pool_consts, 1)
            pool.memset(zero_row[:, :], 0.0).then_inc(pool_consts, 1)
            pool.memset(minus_half[:, :], -0.5).then_inc(pool_consts, 1)

            def fold_tile(a, t, first):
                if t == 0:
                    pool.wait_ge(x_loaded, XD * (a + 1))
                if t >= 2 or not first:
                    pool.wait_ge(frames_t, a * T + t - 1)
                back = xs[:, t, HOP - 1:HALF - 1:-1]
                pool.tensor_tensor(fold[:, t % 2, 0, :], xs[:, t, 0:HALF], back, ALU.add).then_inc(folded, 1)
                pool.tensor_tensor(fold[:, t % 2, 1, :], xs[:, t, 0:HALF], back, ALU.subtract)\
                    .then_inc(folded, 1)

            def z_scale(a):
                pool.wait_ge(aggr_d, T * (a + 1))
                pool.nop(nofuse=True)
                pool.tensor_scalar(var_e[:, :], mv[:, :, 1], 1.0 + EPS, EPS * EPS, ALU.mult, ALU.add)\
                    .then_inc(var_p, 1)
                pool.wait_ge(var_p, a + 1)
                pool.tensor_tensor(rs[:, :], var_e[:, :], minus_half[:, :], ALU.pow).then_inc(scale_p, 1)

            for dst, src in ((raw_bv, bv), (raw_bs[:, 0:PAIRS], bq)):
                pool.dma_start(dst[:, :], src.rearrange("(c p) -> p c", p=P),
                               allow_slow_non_contiguous=True).then_inc(bias_in_s, 16)
            for t in range(T):
                fold_tile(0, t, True)
            pool.dma_start(raw_bs[:, PAIRS:2 * PAIRS], bk.rearrange("(c p) -> p c", p=P),
                           allow_slow_non_contiguous=True).then_inc(bias_in_s, 16)
            for n, src in enumerate((bqp, bkp)):
                pool.dma_start(raw_bp[0:POINTS, n:n + 1], points_by_parity(src.rearrange("(a p) -> a p", a=1)),
                               allow_slow_non_contiguous=True).then_inc(bias_in_s, 16)
            pool.dma_start(ps_b[:, :], pscale.rearrange("(a h) -> a h", a=1).to_broadcast([P, HEADS]))\
                .then_inc(bias_in_s, 16)
            pool.dma_start(bo_b[:, :], bo.rearrange("(a h) -> a h", a=1).to_broadcast([P, C]))\
                .then_inc(bias_in_s, 16)
            pool.dma_start(row_id[:, :], small_in[:, place["rows"][0]:place["rows"][1]])\
                .then_inc(bias_in_s, 16)
            z_scale(0)
            fold_tile(1, 0, False)
            fold_tile(1, 1, False)
            pool.wait_ge(folded, 2 * (T + 2))
            pool.wait_ge(split_low, SPLITS)
            pool.wait_ge(rows_mm, 4)
            pool.wait_ge(table_cleared, 32)
            for f in (qf, kf):
                for parity in range(2):
                    pad = point_rows(parity) + 32
                    pool.memset(f[pad:pad + 32, parity::2, :], 0.0).then_inc(rows_zero, 1)
            pool.wait_ge(rows_zero, 4)
            pool.wait_ge(fixed_src, 2)
            pool.wait_ge(bias_done, 2)
            pool.memset(prob_t[:, :, :, :], 0.0).then_inc(prob_t_zero, 1)

            def add_bias(a, first):
                for t in range(T):
                    pool.wait_ge(h_ready, a * T + t + 1)
                    if not first:
                        pool.wait_ge(h1_ready, (a - 1) * T + t + 1)
                    elif t == 0:
                        pool.wait_ge(fixed_rows, 4 * 16)
                    pool.tensor_tensor(hb[:, t, :], h[:, t, :], out_bias[:, :], ALU.add)\
                        .then_inc(hb_ready, 1)

            def scatter_ids(i, first):
                if not first:
                    pool.wait_ge(scattered, 16 * T * i)
                    pool.nop(nofuse=True)
                    pool.tensor_scalar(row_id[:, :], row_id[:, :], 1.0, float(BLOCK), ALU.mult, ALU.add)\
                        .then_inc(ids_next, 1)
                    pool.wait_ge(ids_next, i)
                pool.wait_ge(slot_d, i + 1)
                pool.nop(nofuse=True)
                for t in range(T):
                    pool.indirect_dma_start(
                        out=table, out_offset=bass.IndirectOffsetOnAxis(ap=slot[:, t:t + 1], axis=0),
                        in_=row_id[:, t:t + 1], in_offset=None).then_inc(scattered, 16)

            def body(i, nxt, first, second):
                if nxt and not first:
                    fold_tile(i + 1, 0, False)
                    fold_tile(i + 1, 1, False)
                add_bias(i, first)
                if nxt:
                    fold_tile(i + 1, 2, False)
                    fold_tile(i + 1, 3, False)
                if not first:
                    scatter_ids(i - 1, second)
                if nxt:
                    z_scale(i + 1)
                for t in range(T):
                    pool.wait_ge(inverted, i * T + t + 1)
                    pr = prob[:, t % 2, :, :]
                    pool.tensor_tensor(pr, pr, rc[:, t % 2, :].unsqueeze(2).to_broadcast([P, HEADS, FRAMES]),
                                       ALU.mult).then_inc(normed, 1)
                for t in range(T):
                    pool.wait_ge(aggr1_d, i * T + t + 1)
                    pool.nop(nofuse=True)
                    pool.tensor_scalar(var1[:, t:t + 1], h1[:, t % 2, C + 1:C + 2], 1.0, EPS,
                                       ALU.mult, ALU.add).then_inc(var1_p, 1)
                    pool.wait_ge(var1_p, i * T + t + 1)
                    pool.tensor_tensor(h1[:, t % 2, C + 1:C + 2], var1[:, t:t + 1], minus_half[:, 0:1],
                                       ALU.pow).then_inc(scale1_p, 1)

            body(0, True, True, False)
            body(1, True, False, True)
            with pool.Fori(2, NBLOCK - 1) as i:
                body(i, True, False, False)
            body(NBLOCK - 1, False, False, False)
            scatter_ids(NBLOCK - 1, False)

            pool.wait_ge(plan_d, 8)
            pool.wait_ge(scattered, 16 * T * NBLOCK)
            for k in range(2):
                pool.wait_ge(h1_stored[k], 16 * NTILE // 2)
            pool.indirect_dma_start(
                out=picked[0:FTILE, :], out_offset=None, in_=table.rearrange("(r n) a -> r (n a)", n=P),
                in_offset=bass.IndirectOffsetOnAxis(ap=table_r[0:FTILE, :], axis=0)).then_inc(table_in, 16)
            pool.wait_ge(index_d, 2)

            def gather(u, k):
                if not (isinstance(u, int) and u < GROUP):
                    pool.wait_ge(index_now_d, u - GROUP + 2)
                    pool.nop(nofuse=True)
                pool.indirect_dma_start(
                    out=g[:, k, :], out_offset=None, in_=h1_dram,
                    in_offset=bass.IndirectOffsetOnAxis(ap=index_now[:, k:k + 1], axis=0))\
                    .then_inc(g_in[k], 16)

            def store(u, k):
                pool.wait_ge(res_ready, u + 1)
                pool.nop(nofuse=True)
                pool.indirect_dma_start(
                    out=out_rows, out_offset=bass.IndirectOffsetOnAxis(ap=index_now[:, k:k + 1], axis=0),
                    in_=res[:, k % 4, :], in_offset=None, bounds_check=ROWS - 1, oob_is_err=False)\
                    .then_inc(res_out[k % 4], 16)

            pool.wait_ge(index_now_d, 1)
            for k in range(4):
                gather(k, k)

            def group(w, last):
                for k in range(LAST if last else GROUP):
                    if k + 4 < LAST or not last:
                        gather(GROUP * w + k + 4, (k + 4) % GROUP)
                    store(GROUP * w + k, k)

            group(0, False)
            with pool.Fori(1, GROUPS - 1) as w:
                group(w, False)
            group(GROUPS - 1, True)
            for k in range(4):
                pool.wait_ge(res_out[k], 16 * (FTILE // 4 + (k < FTILE % 4)))

        @block.scalar
        def _(act):
            for dst, src in ((gain, ln_g), (shift_c, ln_b)):
                act.dma_start(dst[:, :], src.rearrange("(c p) -> p c", p=P),
                              allow_slow_non_contiguous=True).then_inc(gain_in_s, 16)
            act.dma_start(ps_c[:, :], pscale.rearrange("(p a) -> p a", a=1),
                          allow_slow_non_contiguous=True).then_inc(gain_in_s, 16)
            act.wait_ge(dct_in_s, 16)
            act.activation(dct_h[:, :, :, :], raw_d[:, :, :, :], ACT.Copy).then_inc(split_high, 1)

            def frames_high(a, t, first):
                act.wait_ge(frames_t, a * T + t + 1)
                if t >= 2 or not first:
                    act.wait_ge(dct_mm, a * T + t - 1)
                act.activation(xt_h[:, t % 2, :, :], tr[t % 2][:, :], ACT.Copy).then_inc(xt_high, 1)

            def h_out(a, t, first):
                act.wait_ge(dct_mm, a * T + t + 1)
                if t == 0 and not first:
                    act.wait_ge(hb_ready, T * a)
                    act.wait_ge(z_ready, T * a)
                act.activation(h[:, t, :].rearrange("p (m two) -> p two m", two=2),
                               ro[t % 2][:, :].rearrange("p (two m) -> p two m", two=2), ACT.Copy)\
                    .then_inc(h_ready, 1)

            def z_high(a, cc, first):
                act.wait_ge(z_t, a * CC + cc + 1)
                if cc == 0 and not first:
                    act.wait_ge(v_mm, a * T)
                act.activation(zt_h[:, cc, :], qk[cc % 2][:, :], ACT.Copy).then_inc(zt_high, 1)

            frames_high(0, 0, True)
            for t in range(T):
                if t + 1 < T:
                    frames_high(0, t + 1, True)
                h_out(0, t, True)
                if t == 0:
                    act.wait_ge(w_in_s, 4 * 16)
                    act.wait_ge(gain_made, 1)
                for n, by in ((0, gain_q), (1, gain)):
                    act.activation(wqk_h[:, n, t, 0:C], raw_s[:, n, t, :], ACT.Identity,
                                   scale=by[:, t:t + 1]).then_inc(split_high, 1)
                    act.activation(wqk_h[:, n, t, C:QK].rearrange("a (two p h) -> a two p h", two=2, p=POINT),
                                   points_by_parity(raw_p[:, n, t, :]), ACT.Identity,
                                   scale=gain[:, t:t + 1]).then_inc(split_high, 1)
            act.wait_ge(wvo_in_s, 2 * 16)
            for cc in range(CC):
                act.activation(wv_h[:, cc, :], raw_v[:, cc, :], ACT.Identity,
                               scale=gain[:, cc:cc + 1]).then_inc(split_high, 1)
            act.activation(wo_h[:, :, :], raw_o[:, :, :], ACT.Copy).then_inc(split_high, 1)
            for n, row in enumerate(bias_rows):
                act.wait_ge(rows_mm, n + 1)
                act.activation(v[0:1, n, 0:row.shape[-1]], row, ACT.Copy).then_inc(rows_ev, 1)
            for cc in range(CC):
                z_high(0, cc, True)

            def point_features(i, side, first):
                act.wait_ge((q_mm, k_mm)[side], FEATURES * i + 1)
                if side == 0 and first:
                    act.wait_ge(bias_step, 7)
                src, dst, ev = qk[side], v[:, 2 * side:2 * side + 2, :], (q_ev, k_ev)[side]
                if side == 0:
                    act.activation(dst[0:POINTS, 0, :], src[0:POINTS, :], ACT.Identity,
                                   scale=ps2[0:POINTS, :], bias=bias_dot[0:POINTS, :]).then_inc(ev, 1)
                else:
                    act.activation(dst[0:POINTS, 0, :], src[0:POINTS, :], ACT.Identity,
                                   bias=bias_p[0:POINTS, 1:2]).then_inc(ev, 1)
                act.activation(dst[0:POINTS, 1, :], src[0:POINTS, :], ACT.Square,
                               bias=bias_p[0:POINTS, side:side + 1]).then_inc(ev, 1)

            def pair_features(i, m, side):
                act.wait_ge((q_mm, k_mm)[side], FEATURES * i + m + 2)
                if m == 0 and isinstance(i, int) and i == 0:
                    act.wait_ge(rows_zero, 4)
                elif m == 0:
                    act.wait_ge(scored, PAIRS * i)
                f, ev = (qf, kf)[side], (q_ev, k_ev)[side]
                for j in range(2):
                    rows = slice(HD * j, HD * (j + 1))
                    act.activation(f[rows, 2 * m + j, :], qk[side][rows, :], ACT.Identity,
                                   bias=bias_s[rows, side * PAIRS + m:side * PAIRS + m + 1]).then_inc(ev, 1)

            def exponent(i, t):
                act.wait_ge(shifted, i * T + t + 1)
                act.activation(prob[:, t % 2, :, :], prob[:, t % 2, :, :], ACT.Exp).then_inc(exped, 1)

            def expert_high(e):
                act.wait_ge(we_in[e], 16)
                at = e * 2 * EW
                act.activation(we[:, at:at + EW], we_raw[:, e, 1, :], ACT.Copy).then_inc(we_high, 1)

            def body(i, nxt, first):
                point_features(i, 0, first)
                point_features(i, 1, first)
                if nxt:
                    frames_high(i + 1, 0, False)
                pair_features(i, 0, 0)
                if nxt:
                    frames_high(i + 1, 1, False)
                pair_features(i, 0, 1)
                if nxt:
                    h_out(i + 1, 0, False)
                for m in range(1, PAIRS):
                    pair_features(i, m, 0)
                    if nxt and m + 1 < T:
                        frames_high(i + 1, m + 1, False)
                    if nxt and m == PAIRS - 1:
                        h_out(i + 1, T - 1, False)
                    pair_features(i, m, 1)
                    if nxt and m < PAIRS - 1:
                        h_out(i + 1, m, False)
                if not nxt:
                    for e in range(EARLY):
                        expert_high(e)
                for t in range(T):
                    act.wait_ge(v_mm, i * T + t + 1)
                    if t == 0:
                        act.wait_ge(points_in, PD * (i + 1))
                        if first:
                            act.wait_ge(fixed_rows, 4 * 16)
                    act.activation(v[:, t, :], ro[t % 2][:, :], ACT.Copy).then_inc(v_ev, 1)
                    if t < T - 1:
                        exponent(i, t)
                for t in range(T):
                    act.wait_ge(pv_mm, i * T + t + 1)
                    if t >= 2 or not first:
                        act.wait_ge(wo_mm, i * T + t - 1)
                    act.activation(ot_h[:, t % 2, :, :], tr[t % 2][:, :], ACT.Copy).then_inc(ot_high, 1)
                    if t == 0:
                        exponent(i, T - 1)
                    for cc in ((), (0, 1), (2,), (3,))[t]:
                        if nxt:
                            z_high(i + 1, cc, False)

            body(0, True, True)
            with act.Fori(1, NBLOCK - 1) as i:
                body(i, True, False)
            body(NBLOCK - 1, False, False)

            for e in range(EARLY, EXPERTS):
                expert_high(e)

            def ffn_high(u, k, first):
                act.wait_ge(z2_t, u + 1)
                if not first:
                    act.wait_ge(ffn_mm, u - 1)
                act.activation(z2t_h[:, k, :, :], tr[k][:, :], ACT.Copy).then_inc(z2t_high, 1)

            def group(w, last, first):
                for k in range(LAST if last else GROUP):
                    ffn_high(GROUP * w + k, k % 2, first and k < 2)

            group(0, False, True)
            with act.Fori(1, GROUPS - 1) as w:
                group(w, False, False)
            group(GROUPS - 1, True, False)

        @block.vector
        def _(dve):
            dve.memset(xs[:, :, :], 0.0).then_inc(xs_zero, 1)
            dve.memset(ones_b[:, :], 1.0).then_inc(consts_made, 1)
            dve.memset(so_far[:, :], 0.0).then_inc(consts_made, 1)
            dve.memset(above[:, :, 0:1], 1.0).then_inc(consts_made, 1)
            dve.memset(above[:, :, EXPERTS:EXPERTS + 1], 0.0).then_inc(consts_made, 1)
            dve.wait_ge(small_in_s, 16)
            dve.tensor_copy(before_b[:, :], const("before")).then_inc(consts_made, 1)
            dve.wait_ge(split_high, 1)
            dve.tensor_tensor(dct_l[:, :, :, :], raw_d[:, :, :, :], dct_h[:, :, :, :], ALU.subtract)\
                .then_inc(split_low, 1)

            def frames_low(a, t):
                dve.wait_ge(xt_high, a * T + t + 1)
                dve.tensor_tensor(xt_l[:, t % 2, :, :], tr[t % 2][:, :].rearrange("p (c r) -> p c r", c=4),
                                  xt_h[:, t % 2, :, :], ALU.subtract).then_inc(xt_low, 1)

            def h_stats(a, t, first):
                dve.wait_ge(h_ready, a * T + t + 1)
                if t == 0 and not first:
                    dve.wait_ge(z_ready, T * a)
                dve.bn_stats(stat[:, t, :], h[:, t, :]).then_inc(stat_d, 1)
                dve.wait_ge(stat_d, a * T + t + 1)
                dve.nop(nofuse=True)
                dve.bn_aggr(mv[:, t, :], stat[:, t, :]).then_inc(aggr_d, 1)

            def z_tiles(a, first):
                dve.wait_ge(scale_p, a + 1)
                if not first:
                    dve.wait_ge(z_t, CC * a)
                for t in range(T):
                    dve.tensor_scalar(z[:, t, :], h[:, t, :], mv[:, t, 0:1], rs[:, t:t + 1],
                                      ALU.subtract, ALU.mult).then_inc(z_ready, 1)

            def z_low(a, cc):
                dve.wait_ge(zt_high, a * CC + cc + 1)
                dve.tensor_tensor(zt_l[:, cc, :], qk[cc % 2][:, :], zt_h[:, cc, :], ALU.subtract)\
                    .then_inc(zt_low, 1)

            dve.wait_ge(gain_in_s, 3 * 16)
            dve.tensor_scalar(gain_q[:, :], gain[:, :], HD ** -0.5, None, ALU.mult).then_inc(gain_made, 1)
            frames_low(0, 0)
            for t in range(T):
                if t + 1 < T:
                    frames_low(0, t + 1)
                h_stats(0, t, True)
                for n, by in ((0, gain_q), (1, gain)):
                    dve.wait_ge(split_high, 1 + 4 * t + 2 * n + 2)
                    dve.scalar_tensor_tensor(out=wqk_l[:, n, t, 0:C], in0=raw_s[:, n, t, :],
                                             scalar=by[:, t:t + 1], in1=wqk_h[:, n, t, 0:C],
                                             op0=ALU.mult, op1=ALU.subtract).then_inc(split_low, 1)
                    low, high = [w[:, n, t, C:QK].rearrange("a (two p h) -> a two p h", two=2, p=POINT)
                                 for w in (wqk_l, wqk_h)]
                    dve.scalar_tensor_tensor(out=low, in0=points_by_parity(raw_p[:, n, t, :]),
                                             scalar=gain[:, t:t + 1], in1=high,
                                             op0=ALU.mult, op1=ALU.subtract).then_inc(split_low, 1)
            z_tiles(0, True)
            for cc in range(CC):
                dve.wait_ge(split_high, 1 + 4 * CC + cc + 1)
                dve.scalar_tensor_tensor(out=wv_l[:, cc, :], in0=raw_v[:, cc, :], scalar=gain[:, cc:cc + 1],
                                         in1=wv_h[:, cc, :], op0=ALU.mult, op1=ALU.subtract)\
                    .then_inc(split_low, 1)
            dve.wait_ge(split_high, SPLITS)
            dve.tensor_tensor(wo_l[:, :, :], raw_o[:, :, :], wo_h[:, :, :], ALU.subtract).then_inc(split_low, 1)

            z_low(0, 0)
            z_low(0, 1)
            dve.wait_ge(bias_in_s, 8 * 16)
            dve.wait_ge(bias_mm, 1)
            dve.tensor_scalar(ps2[0:POINTS, :], bias_out[0:POINTS, 16:17], 2.0, None, ALU.mult)\
                .then_inc(bias_step, 1)
            dve.tensor_tensor(bias_s[:, :], raw_bs[:, :], bias_out[:, 0:2 * PAIRS], ALU.add).then_inc(bias_step, 1)
            dve.tensor_tensor(bias_p[0:POINTS, :], raw_bp[0:POINTS, :], bias_out[0:POINTS, 8:10], ALU.add)\
                .then_inc(bias_step, 1)
            dve.tensor_tensor(v_bias[:, :], raw_bv[:, :], bias_out[:, 12:12 + CC], ALU.add).then_inc(bias_step, 1)
            dve.tensor_scalar(neg_ps[:, :], ps_b[:, :], -1.0, None, ALU.mult).then_inc(bias_step, 1)
            dve.wait_ge(bias_step, 5)
            dve.tensor_copy(v_bias_b[:, :, :], v_bias[:, :].unsqueeze(2).to_broadcast([P, CC, P]))\
                .then_inc(vb_ready, 1)
            dve.tensor_scalar(bias_s[:, 0:PAIRS], bias_s[:, 0:PAIRS], HD ** -0.5, None, ALU.mult)\
                .then_inc(bias_step, 1)
            dve.tensor_tensor(bias_dot[0:POINTS, :], bias_p[0:POINTS, 0:1], ps2[0:POINTS, :], ALU.mult)\
                .then_inc(bias_step, 1)
            for parity, dst in enumerate((v, hb)):
                dve.tensor_copy(dst[FIXED:FIXED + POINT, :, :],
                                neg_ps[FIXED:FIXED + POINT, parity::2].unsqueeze(2).to_broadcast([POINT, T, C]))\
                    .then_inc(fixed_src, 1)
            z_low(0, 2)
            z_low(0, 3)
            dve.wait_ge(ob_mm, 1)
            dve.tensor_tensor(out_bias[:, :], bo_b[:, :], value_out[:, :], ALU.add).then_inc(bias_done, 2)

            def shift(i, t):
                s = sc[t // 2][:, t % 2, :, :]
                k = t % 2
                if t >= 2:
                    dve.wait_ge(probs_t, i * T + t - 1)
                dve.tensor_reduce(mx[:, k, :], s, XA, ALU.max).then_inc(max_d, 1)
                dve.wait_ge(max_d, i * T + t + 1)
                dve.tensor_tensor(prob[:, k, :, :], s, mx[:, k, :].unsqueeze(2).to_broadcast([P, HEADS, FRAMES]),
                                  ALU.subtract).then_inc(shifted, 1)

            def total(i, t):
                k = t % 2
                dve.wait_ge(exped, i * T + t + 1)
                dve.tensor_reduce(sm[:, k, :], prob[:, k, :, :], XA, ALU.add).then_inc(summed, 1)
                dve.wait_ge(summed, i * T + t + 1)
                if t >= 2:
                    dve.wait_ge(normed, i * T + t - 1)
                dve.reciprocal(rc[:, k, :], sm[:, k, :]).then_inc(inverted, 1)

            def spread(i, t, first):
                dve.wait_ge(normed, i * T + t + 1)
                if t >= 2 or not first:
                    dve.wait_ge(pv_mm, i * T + t - 1)
                elif t == 0:
                    dve.wait_ge(prob_t_zero, 1)
                for c in range(CLIPS):
                    q = slice(32 * c, 32 * c + 32)
                    last = dve.transpose(prob_t[q, t % 2, :, 32 * c:32 * c + 32], prob[q, t % 2, :, :])
                last.then_inc(probs_t, 1)

            def attended_low(i, t):
                dve.wait_ge(ot_high, i * T + t + 1)
                dve.tensor_tensor(ot_l[:, t % 2, :, :], tr[t % 2][:, :].rearrange("p (c r) -> p c r", c=CC),
                                  ot_h[:, t % 2, :, :], ALU.subtract).then_inc(ot_low, 1)

            def h1_tile(i, t, first):
                dve.wait_ge(wo_mm, i * T + t + 1)
                if t >= 2:
                    dve.wait_ge(h1_stored[t % 2], 32 * i + 16)
                    dve.wait_ge(y0_d, i * T + t - 1)
                elif not first:
                    dve.wait_ge(h1_stored[t], 32 * i)
                dve.wait_ge(hb_ready, i * T + t + 1)
                dve.tensor_tensor(h1[:, t % 2, 0:C], hb[:, t, :], ro[t % 2][:, :], ALU.add).then_inc(h1_ready, 1)
                dve.wait_ge(h1_ready, i * T + t + 1)
                dve.bn_stats(stat1[:, t, :], h1[:, t % 2, 0:C]).then_inc(stat1_d, 1)
                dve.wait_ge(stat1_d, i * T + t + 1)
                dve.nop(nofuse=True)
                dve.bn_aggr(h1[:, t % 2, C:CW], stat1[:, t, :]).then_inc(aggr1_d, 1)

            def channel0(i, t):
                dve.wait_ge(scale1_p, i * T + t + 1)
                dve.tensor_scalar(y0[:, t:t + 1], h1[:, t % 2, 0:1], h1[:, t % 2, C:C + 1],
                                  h1[:, t % 2, C + 1:CW], ALU.subtract, ALU.mult).then_inc(y0_d, 1)

            def choose(i):
                dve.wait_ge(y0_d, T * (i + 1))
                dve.tensor_tensor(above[:, :, 1:EXPERTS], y0[:, :].unsqueeze(2).to_broadcast([P, T, EXPERTS - 1]),
                                  const("bins").unsqueeze(1).to_broadcast([P, T, EXPERTS - 1]), ALU.is_gt)\
                    .then_inc(above_d, 1)
                dve.wait_ge(above_d, i + 1)
                dve.tensor_tensor(onehot[:, :, :], above[:, :, 0:EXPERTS], above[:, :, 1:EXPERTS + 1],
                                  ALU.subtract).then_inc(onehot_d, 1)

            def slots(i, first):
                dve.wait_ge(rank_mm, i + 1)
                dve.tensor_tensor(slot_b[:, :, :], ro[0][:, 0:T * EXPERTS].rearrange("p (t e) -> p t e", t=T),
                                  const("bucket").unsqueeze(1).to_broadcast([P, T, EXPERTS]), ALU.add)\
                    .then_inc(slot_b_d, 1)
                dve.tensor_reduce(block_sum[:, :], onehot[:, :, :].rearrange("p t e -> p e t"), XA, ALU.add)\
                    .then_inc(block_sum_d, 1)
                dve.wait_ge(slot_b_d, i + 1)
                dve.tensor_tensor(slot_m[:, :, :], slot_b[:, :, :], onehot[:, :, :], ALU.mult)\
                    .then_inc(slot_m_d, 1)
                dve.wait_ge(block_sum_d, i + 1)
                dve.tensor_tensor(so_far[:, :], so_far[:, :], block_sum[:, :], ALU.add).then_inc(so_far_d, 1)
                dve.wait_ge(slot_m_d, i + 1)
                dve.tensor_reduce(slot_f[:, :], slot_m[:, :, :], XA, ALU.add).then_inc(slot_f_d, 1)
                dve.wait_ge(slot_f_d, i + 1)
                if not first:
                    dve.wait_ge(scattered, 16 * T * i)
                dve.tensor_copy(slot[:, :], slot_f[:, :]).then_inc(slot_d, 1)

            def expert_low(e):
                at = e * 2 * EW
                dve.wait_ge(we_high, e + 1)
                dve.tensor_tensor(we[:, at + EW:at + 2 * EW], we_raw[:, e, 1, :], we[:, at:at + EW],
                                  ALU.subtract).then_inc(we_low, 1)

            def body(i, nxt, first, second):
                if not first:
                    slots(i - 1, second)
                if nxt:
                    frames_low(i + 1, 0)
                    frames_low(i + 1, 1)
                    for t in range(2, T):
                        h_stats(i + 1, t - 2, False)
                        frames_low(i + 1, t)
                    h_stats(i + 1, T - 2, False)
                    h_stats(i + 1, T - 1, False)
                    z_tiles(i + 1, False)
                else:
                    for e in range(EARLY):
                        expert_low(e)
                dve.wait_ge(scored, PAIRS * (i + 1))
                shift(i, 0)
                shift(i, 1)
                for t in range(2):
                    total(i, t)
                    spread(i, t, first)
                    shift(i, t + 2)
                total(i, 2)
                attended_low(i, 0)
                total(i, 3)
                attended_low(i, 1)
                spread(i, 2, first)
                spread(i, 3, first)
                if nxt:
                    z_low(i + 1, 0)
                    z_low(i + 1, 1)
                attended_low(i, 2)
                h1_tile(i, 0, first)
                h1_tile(i, 1, first)
                channel0(i, 0)
                if nxt:
                    z_low(i + 1, 2)
                attended_low(i, 3)
                h1_tile(i, 2, first)
                channel0(i, 1)
                if nxt:
                    z_low(i + 1, 3)
                h1_tile(i, 3, first)
                channel0(i, 2)
                channel0(i, 3)
                choose(i)

            body(0, True, True, False)
            body(1, True, False, True)
            with dve.Fori(2, NBLOCK - 1) as i:
                body(i, True, False, False)
            body(NBLOCK - 1, False, False, False)
            slots(NBLOCK - 1, False)

            dve.wait_ge(count_mm, 1)
            dve.tensor_copy(counts[:, :], ro[1][:, 0:EXPERTS]).then_inc(plan_d, 1)
            dve.wait_ge(plan_d, 1)
            dve.tensor_tensor(exceeds, counts[:, :].unsqueeze(2).to_broadcast([P, EXPERTS, NTILE]),
                              const("tile128").unsqueeze(1).to_broadcast([P, EXPERTS, NTILE]), ALU.is_gt)\
                .then_inc(plan_d, 1)
            dve.wait_ge(plan_d, 2)
            dve.tensor_reduce(tiles_of[:, :], exceeds, XA, ALU.add).then_inc(plan_d, 1)
            dve.wait_ge(plan_d, 3)
            dve.tensor_tensor(lower_m[:, :, :], tiles_of[:, :].unsqueeze(1).to_broadcast([P, EXPERTS, EXPERTS]),
                              const("lower").rearrange("p (a b) -> p a b", a=EXPERTS), ALU.mult)\
                .then_inc(plan_d, 1)
            dve.wait_ge(plan_d, 4)
            dve.tensor_reduce(first_of[:, :], lower_m[:, :, :], XA, ALU.add).then_inc(plan_d, 1)
            dve.wait_ge(plan_d, 5)
            dve.tensor_scalar(started[:, :], first_of[:, :], const("partition"), None, ALU.is_le)\
                .then_inc(plan_d, 1)
            dve.wait_ge(plan_d, 6)
            dve.tensor_reduce(expert_of[:, :], started[:, 1:EXPERTS], XA, ALU.add).then_inc(plan_d, 1)
            dve.tensor_tensor(skipped[:, :], started[:, 1:EXPERTS], tiles_of[:, 0:EXPERTS - 1], ALU.mult)\
                .then_inc(plan_s, 1)
            dve.wait_ge(plan_s, 1)
            dve.tensor_reduce(start_of[:, :], skipped[:, :], XA, ALU.add).then_inc(plan_s, 1)
            dve.wait_ge(plan_s, 2)
            dve.tensor_tensor(in_bucket[:, :], const("partition"), start_of[:, :], ALU.subtract)\
                .then_inc(plan_s, 1)
            dve.wait_ge(plan_s, 3)
            dve.wait_ge(plan_d, 7)
            dve.scalar_tensor_tensor(out=table_f[:, :], in0=expert_of[:, :], scalar=float(BUCKET // P),
                                     in1=in_bucket[:, :], op0=ALU.mult, op1=ALU.add).then_inc(plan_s, 1)
            dve.wait_ge(plan_s, 4)
            dve.tensor_copy(table_r[:, :], table_f[:, :]).then_inc(plan_d, 1)
            for e in (2, 3):
                expert_low(e)
            dve.wait_ge(scattered, 16 * T * NBLOCK)
            for k in range(2):
                dve.wait_ge(h1_stored[k], 16 * NTILE // 2)
            dve.wait_ge(plan_t, 1)
            dve.tensor_copy(expert_row[0:1, :], ro[0][0:1, 0:FTILE]).then_inc(index_d, 1)
            dve.wait_ge(picked_t, 1)
            dve.tensor_copy(index[:, :], tr[0][:, 0:FTILE]).then_inc(index_d, 1)
            dve.tensor_copy(index_now[:, :], tr[0][:, 0:GROUP]).then_inc(index_now_d, 1)
            expert_low(4)

            def ffn_norm(u, w, k, first):
                dve.wait_ge(g_in[k], 16 * (w + 1))
                if not first:
                    dve.wait_ge(z2_t, u - 1)
                dve.tensor_scalar(z2[:, k % 2, :], g[:, k, 0:C], g[:, k, C:C + 1], g[:, k, C + 1:CW],
                                  ALU.subtract, ALU.mult).then_inc(z2_ready, 1)

            def ffn_low(u, k):
                dve.wait_ge(z2t_high, u + 1)
                dve.tensor_tensor(z2t_l[:, k % 2, :, :], tr[k % 2][:, :].rearrange("p (c r) -> p c r", c=CC),
                                  z2t_h[:, k % 2, :, :], ALU.subtract).then_inc(z2t_low, 1)

            def ffn_out(u, w, k):
                dve.wait_ge(ffn_mm, u + 1)
                n = GROUP // 4 * w + k // 4
                if not (isinstance(n, int) and n == 0):
                    dve.wait_ge(res_out[k % 4], 16 * n)
                dve.tensor_tensor(res[:, k % 4, :], g[:, k, 0:C], ro[k % 2][:, :], ALU.add).then_inc(res_ready, 1)

            ffn_norm(0, 0, 0, True)
            ffn_norm(1, 0, 1, True)
            ffn_low(0, 0)
            ffn_low(1, 1)
            ffn_norm(2, 0, 2, False)
            ffn_norm(3, 0, 3, False)
            for e in range(5, EXPERTS):
                expert_low(e)

            def next_index(u, k):
                dve.wait_ge(index_d, 2)
                dve.tensor_copy(index_now[:, k:k + 1], index[:, bass.ds(u, 1)]).then_inc(index_now_d, 1)

            def group(w, last):
                for k in range(LAST if last else GROUP):
                    u = GROUP * w + k
                    ffn_out(u, w, k)
                    if (k + 4 < LAST or not last) and not (isinstance(u, int) and u + 4 < GROUP):
                        next_index(u + 4, (k + 4) % GROUP)
                    if k + 2 < LAST or not last:
                        ffn_low(u + 2, k)
                    if (k + 3 < LAST or not last) and not (isinstance(u, int) and u == 0):
                        ffn_norm(u + 3, w if k + 3 < GROUP else w + 1, (k + 3) % GROUP, False)

            group(0, False)
            with dve.Fori(1, GROUPS - 1) as w:
                group(w, False)
            group(GROUPS - 1, True)

        @block.tensor
        def _(pe):
            def product(out_ap, pairs):
                n = 0
                for (wh, wl), (mh, ml) in pairs:
                    for w, m in ((wh, mh), (wh, ml), (wl, mh)):
                        n += 1
                        last = pe.matmul(out_ap, w, m, start=n == 1, stop=n == 3 * len(pairs))
                return last

            def transpose_frames(a, t):
                pe.wait_ge(folded, 2 * (a * T + t + 1))
                for c in range(4):
                    last = pe.transpose(tr[t % 2][:, c * P:(c + 1) * P],
                                        fold[:, t % 2, c // 2, (c % 2) * P:(c % 2 + 1) * P], ident)
                last.then_inc(frames_t, 1)

            def dct(a, t):
                pe.wait_ge(xt_low, a * T + t + 1)
                for eo in range(2):
                    last = product(ro[t % 2][:, eo * HALF:(eo + 1) * HALF],
                                   [((xt_h[:, t % 2, 2 * eo + c, :], xt_l[:, t % 2, 2 * eo + c, :]),
                                     (dct_h[:, eo, c, :], dct_l[:, eo, c, :])) for c in range(2)])
                last.then_inc(dct_mm, 1)

            def transpose_z(a, cc):
                pe.wait_ge(z_ready, T * (a + 1))
                if cc >= 2:
                    pe.wait_ge(zt_low, a * CC + cc - 1)
                for t in range(T):
                    last = pe.transpose(qk[cc % 2][:, t * P:(t + 1) * P], z[:, t, cc * P:(cc + 1) * P], ident)
                last.then_inc(z_t, 1)

            def shift_row(n):
                if n == 0:
                    pe.wait_ge(w_in_s, 4 * 16)
                    pe.wait_ge(gain_in_s, 3 * 16)
                w = (raw_s[:, 0], raw_s[:, 1], raw_v)[n]
                for cc in range(CC):
                    last = pe.matmul(bias_rows[n], shift_c[:, cc:cc + 1], w[:, cc, :],
                                     start=cc == 0, stop=cc == CC - 1)
                last.then_inc(rows_mm, 1)

            pe.wait_ge(small_in_s, 16)
            transpose_frames(0, 0)
            transpose_frames(0, 1)
            pe.wait_ge(split_low, 1)
            for t in range(T):
                if t >= 2:
                    pe.wait_ge(h_ready, t - 1)
                dct(0, t)
                if t + 2 < T:
                    transpose_frames(0, t + 2)
                if t == 1:
                    shift_row(0)

            shift_row(1)
            pe.wait_ge(wvo_in_s, 2 * 16)
            pe.wait_ge(xt_low, T)
            shift_row(2)
            for n in range(2):
                for cc in range(CC):
                    last = pe.matmul(bias_rows[3][:, n * POINTS:(n + 1) * POINTS], shift_c[:, cc:cc + 1],
                                     points_by_parity(raw_p[:, n, cc, :]), start=cc == 0, stop=cc == CC - 1)
            last.then_inc(rows_mm, 1)
            transpose_z(0, 0)
            transpose_z(0, 1)
            pe.wait_ge(rows_ev, 4)
            pe.wait_ge(h_ready, T)
            one = ident[0:1, 0:1]
            for n, at in ((0, 0), (1, PAIRS), (2, 12)):
                for m in range(CC):
                    pe.matmul(bias_out[:, at + m:at + m + 1], v[0:1, n, m * P:(m + 1) * P], one,
                              start=True, stop=True)
            for n in range(2):
                pe.matmul(bias_out[0:POINTS, 8 + n:9 + n], v[0:1, 3, n * POINTS:(n + 1) * POINTS], one,
                          start=True, stop=True)
            pe.matmul(bias_out[0:POINTS, 16:17], const("head_of")[0:HEADS, :], ps_c[:, :],
                      start=True, stop=True).then_inc(bias_mm, 1)
            transpose_z(0, 2)
            transpose_z(0, 3)
            pe.wait_ge(vb_ready, 1)
            for cc in range(CC):
                last = pe.matmul(value_out[:, :], v_bias_b[:, cc, :], raw_o[:, cc, :],
                                 start=cc == 0, stop=cc == CC - 1)
            last.then_inc(ob_mm, 1)

            def features(i, s, side):
                if s == 0 and side == 0:
                    pe.wait_ge(zt_low, CC * (i + 1))
                elif s:
                    pe.wait_ge((q_ev, k_ev)[side], 2 * (FEATURES * i + s))
                cols = slice(C, QK) if s == 0 else slice((s - 1) * P, s * P)
                rows = POINTS if s == 0 else P
                product(qk[side][0:rows, :],
                        [((wqk_h[:, side, cc, cols], wqk_l[:, side, cc, cols]),
                          (zt_h[:, cc, :], zt_l[:, cc, :])) for cc in range(CC)])\
                    .then_inc((q_mm, k_mm)[side], 1)

            def scores(i, m, first):
                pe.wait_ge(q_ev, 2 * (FEATURES * i + m + 2))
                pe.wait_ge(k_ev, 2 * (FEATURES * i + m + 2))
                pe.wait_ge(points_in, PD * (i + 1))
                if m == 0:
                    if first:
                        pe.wait_ge(fixed_rows, 4 * 16)
                    else:
                        pe.wait_ge(shifted, T * i)
                for hd in (2 * m, 2 * m + 1):
                    for t in range(T):
                        for c in range(CLIPS):
                            cols = slice(t * P + 32 * c, t * P + 32 * c + 32)
                            last = pe.matmul(sc[t // 2][32 * c:32 * c + 32, t % 2, hd, :], qf[:, hd, cols],
                                             kf[:, hd, cols], start=True, stop=True)
                last.then_inc(scored, 1)

            def values(i, t):
                if t >= 2:
                    pe.wait_ge(v_ev, i * T + t - 1)
                product(ro[t % 2][:, :],
                        [((zt_h[:, cc, t * P:(t + 1) * P], zt_l[:, cc, t * P:(t + 1) * P]),
                          (wv_h[:, cc, :], wv_l[:, cc, :])) for cc in range(CC)]).then_inc(v_mm, 1)

            def attend(i, t):
                pe.wait_ge(probs_t, i * T + t + 1)
                pe.wait_ge(v_ev, i * T + t + 1)
                if t >= 2:
                    pe.wait_ge(ot_low, i * T + t - 1)
                for hd in range(HEADS):
                    half = 64 * (hd % 2)
                    last = pe.matmul(tr[t % 2][half:half + HD, (hd // 2) * P:(hd // 2 + 1) * P],
                                     v[:, t, hd * HD:(hd + 1) * HD], prob_t[:, t % 2, hd, :],
                                     start=True, stop=True)
                last.then_inc(pv_mm, 1)

            def project(i, t):
                pe.wait_ge(ot_low, i * T + t + 1)
                if t >= 2:
                    pe.wait_ge(h1_ready, i * T + t - 1)
                else:
                    pe.wait_ge(v_ev, i * T + t + 3)
                product(ro[t % 2][:, :],
                        [((ot_h[:, t % 2, cc, :], ot_l[:, t % 2, cc, :]), (wo_h[:, cc, :], wo_l[:, cc, :]))
                         for cc in range(CC)]).then_inc(wo_mm, 1)

            def rank(i, first):
                pe.wait_ge(onehot_d, i + 1)
                pe.wait_ge(h1_ready, T * (i + 1))
                if not first:
                    pe.wait_ge(so_far_d, i)
                r = ro[0][:, 0:T * EXPERTS].rearrange("p (t e) -> p t e", t=T)
                pe.matmul(r, before_b[:, :], onehot[:, :, :], start=True, stop=False)
                for t in range(1, T):
                    pe.matmul(r[:, t:T, :], ones_b[:, :], onehot[:, 0:T - t, :], start=False, stop=False)
                pe.matmul(r, ones_b[:, :], so_far[:, :].unsqueeze(1).to_broadcast([P, T, EXPERTS]),
                          start=False, stop=True).then_inc(rank_mm, 1)

            def body(i, nxt, first, second):
                n = 0
                for s in range(FEATURES):
                    for side in range(2):
                        features(i, s, side)
                        if n == 1:
                            if not first:
                                rank(i - 1, second)
                            if nxt:
                                if first:
                                    pe.wait_ge(xt_low, T)
                                else:
                                    pe.wait_ge(ot_low, T * i)
                                transpose_frames(i + 1, 0)
                        if nxt and n == 2:
                            transpose_frames(i + 1, 1)
                        if n == 3:
                            if nxt and not first:
                                pe.wait_ge(slot_b_d, i)
                            if nxt and first:
                                pe.wait_ge(h_ready, T)
                            if nxt:
                                dct(i + 1, 0)
                        if nxt and n == 4:
                            transpose_frames(i + 1, 2)
                        if nxt and n == 5:
                            if not first:
                                pe.wait_ge(h1_ready, T * i)
                            dct(i + 1, 1)
                        if nxt and n == 6:
                            transpose_frames(i + 1, 3)
                        if nxt and n in (7, 8):
                            pe.wait_ge(h_ready, (i + 1) * T + n - 6)
                            dct(i + 1, n - 5)
                        if n in (5, 7, 9):
                            scores(i, (n - 5) // 2, first)
                        n += 1
                if nxt:
                    pe.wait_ge(h_ready, (i + 2) * T)
                else:
                    pe.wait_ge(slot_b_d, i)
                values(i, 0)
                scores(i, PAIRS - 1, first)
                values(i, 1)
                values(i, 2)
                values(i, 3)
                attend(i, 0)
                attend(i, 1)
                if nxt:
                    transpose_z(i + 1, 0)
                    transpose_z(i + 1, 1)
                project(i, 0)
                attend(i, 2)
                project(i, 1)
                if nxt:
                    transpose_z(i + 1, 2)
                attend(i, 3)
                project(i, 2)
                if nxt:
                    transpose_z(i + 1, 3)
                project(i, 3)

            body(0, True, True, False)
            body(1, True, False, True)
            with pe.Fori(2, NBLOCK - 1) as i:
                body(i, True, False, False)
            body(NBLOCK - 1, False, False, False)
            rank(NBLOCK - 1, False)
            pe.wait_ge(so_far_d, NBLOCK)
            pe.matmul(ro[1][:, 0:EXPERTS], ones_b[:, :], so_far[:, :], start=True, stop=True).then_inc(count_mm, 1)

            pe.wait_ge(plan_d, 8)
            pe.matmul(ro[0][0:1, 0:FTILE], expert_of[0:FTILE, :], ident[0:FTILE, 0:FTILE],
                      start=True, stop=True).then_inc(plan_t, 1)
            pe.wait_ge(table_in, 16)
            pe.transpose(tr[0][:, 0:FTILE], picked[0:FTILE, :], ident[0:FTILE, 0:FTILE]).then_inc(picked_t, 1)
            pe.wait_ge(index_d, 2)

            def transpose_rows(u, k, first):
                pe.wait_ge(z2_ready, u + 1)
                if not first:
                    pe.wait_ge(z2t_low, u - 1)
                for cc in range(CC):
                    last = pe.transpose(tr[k][:, cc * P:(cc + 1) * P], z2[:, k, cc * P:(cc + 1) * P], ident)
                last.then_inc(z2_t, 1)

            def expert_product(u, k, first):
                e = pe.value_load(expert_row[0:1, bass.ds(u, 1)], min_val=0, max_val=EXPERTS - 1)
                pe.wait_ge(we_low, e + 1)
                pe.wait_ge(z2t_low, u + 1)
                if not first:
                    pe.wait_ge(res_ready, u - 1)
                at = e * (2 * EW)
                product(ro[k][:, :],
                        [((z2t_h[:, k, cc, :], z2t_l[:, k, cc, :]),
                          (we[:, bass.ds(at + cc * C, C)], we[:, bass.ds(at + EW + cc * C, C)]))
                         for cc in range(CC)]).then_inc(ffn_mm, 1)

            transpose_rows(0, 0, True)
            transpose_rows(1, 1, True)

            def group(w, last, first):
                for k in range(LAST if last else GROUP):
                    expert_product(GROUP * w + k, k % 2, first and k < 2)
                    if k + 2 < LAST or not last:
                        transpose_rows(GROUP * w + k + 2, k % 2, False)

            group(0, False, True)
            with pe.Fori(1, GROUPS - 1) as w:
                group(w, False, False)
            group(GROUPS - 1, True, False)


_INS = ["x", "L0_attn_ln_g", "L0_attn_ln_b", "L0_attn_wq", "L0_attn_bq", "L0_attn_wk", "L0_attn_bk",
        "L0_attn_wv", "L0_attn_bv", "L0_attn_wqp", "L0_attn_bqp", "L0_attn_wkp", "L0_attn_bkp",
        "L0_attn_wo", "L0_attn_bo", "L0_attn_pscale", "L0_ffn_W"]


def kernel(**inputs):
    import concourse.bacc as bacc
    from concourse.bass_utils import run_bass_kernel_spmd

    nc = bacc.Bacc("TRN2", target_bir_lowering=False, num_devices=1)
    dct, small, place = constants()
    arrays = {f"in_{n}": np.ascontiguousarray(inputs[n]) for n in _INS}
    arrays["const_dct"], arrays["const_small"] = dct, small
    aps = [nc.dram_tensor(n, a.shape, mybir.dt.from_np(a.dtype), kind="ExternalInput").ap()
           for n, a in arrays.items()]
    out = nc.dram_tensor("out", (BATCH, FRAMES, C), mybir.dt.float32, kind="ExternalOutput").ap()
    audio_tower(nc, *aps, place, out)
    r = run_bass_kernel_spmd(nc, [arrays], core_ids=[0])
    return r.results[0]["out"]
```
